# Optimizing a Trainium2 kernel written in Bass

```python
import numpy as np
import jax
import jax.numpy as jnp

def _softmax(x, axis=-1):
    return jax.nn.softmax(x, axis=axis)

def _gelu(x):
    return jax.nn.gelu(x, approximate=True)

def _silu(x):
    return jax.nn.silu(x)

def _sigmoid(x):
    return jax.nn.sigmoid(x)

def _layernorm(x, axis=-1, eps=1e-05):
    m = jnp.mean(x, axis=axis, keepdims=True)
    v = jnp.var(x, axis=axis, keepdims=True)
    return (x - m) / jnp.sqrt(v + eps)

def _scatter_add(tgt, idx, src, axis=0):
    return tgt.at[idx].add(src)

def _segment_sum(src, seg, n):
    return jax.ops.segment_sum(src, seg, n)
kernel_name = 'mk_decoder_postln_d1_seqx_r4_53dab3'

def setup_inputs(seed: int=0):
    np.random.seed(seed)
    _w = jnp.asarray

    def _rec_inputs():
        import jax
        import jax.numpy as jnp
        _rk = jax.random.key(seed)
        x = 7.22e-05 + 1 * jax.random.normal(jax.random.fold_in(_rk, 1), (4, 512, 512), jnp.float32)
        _lenS = 512 - jax.random.randint(jax.random.fold_in(_rk, 7), (4,), 0, max(1, 512 // 4) + 1, jnp.int32)
        _lenS2 = 1024 - jax.random.randint(jax.random.fold_in(_rk, 8), (4,), 0, max(1, 1024 // 4) + 1, jnp.int32)
        _ctx_1024P = jax.random.normal(jax.random.fold_in(_rk, 11), (4, 16, 256), jnp.float32)
        _ctx_1024c = jax.random.dirichlet(jax.random.fold_in(_rk, 511), 0.3 * jnp.ones((16,), jnp.float32), (4, 1024))
        _ctx_1024t = jnp.einsum('bsk,bkd->bsd', _ctx_1024c, _ctx_1024P)
        _ctx_1024t = _ctx_1024t * jax.lax.rsqrt(jnp.mean(jnp.square(_ctx_1024t)) + 1e-12) * 0.953939
        ctx_1024 = -0.000673644 + 1.00013 * (_ctx_1024t + 0.3 * jax.random.normal(jax.random.fold_in(_rk, 611), (4, 1024, 256), jnp.float32))
        return (x, ctx_1024)
    x, ctx_1024 = _rec_inputs()

    def _L0_attn_setup():
        import math
        import jax, jax.numpy as jnp
        import numpy as np
        HID = 512
        H = 16
        HKV = 8
        D = HID // H
        F = D
        SEQ = 512
        BATCH = 2
        THETA = 10000.0

        def _rotate_half(x):
            x1, x2 = (x[..., :x.shape[-1] // 2], x[..., x.shape[-1] // 2:])
            return jnp.concatenate((-x2, x1), axis=-1)

        def _softmax_kernel(x, R):
            n = jnp.sqrt(jnp.sum(x * x, axis=-1, keepdims=True))
            x = x / jnp.maximum(n, 1e-06)
            p = jnp.einsum('...d,ed->...e', x, R)
            feats = jnp.concatenate([jnp.sin(p), jnp.cos(p)], axis=-1)
            return feats / math.sqrt(F)
        key = jax.random.key(seed)
        ks = jax.random.split(key, 10)
        s = lambda k, shape, scale=0.02: jax.random.normal(k, shape, dtype=jnp.float32) * scale
        return {'hidden_states': jax.random.normal(ks[0], (BATCH, SEQ, HID), dtype=jnp.float32), 'Wq': s(ks[1], (HID, HID)), 'bq': s(ks[2], (HID,)), 'Wk': s(ks[3], (HKV * D, HID)), 'bk': s(ks[4], (HKV * D,)), 'Wv': s(ks[5], (HKV * D, HID)), 'bv': s(ks[6], (HKV * D,)), 'Wo': s(ks[7], (HID, HID)), 'bo': s(ks[8], (HID,)), 'rand_matrix': jax.random.normal(ks[9], (F // 2, D), dtype=jnp.float32)}
    _L0_attn_all = _L0_attn_setup()
    _L0_attn_in = {k: v for k, v in _L0_attn_all.items() if k in ('Wq', 'bq', 'Wk', 'bk', 'Wv', 'bv', 'Wo', 'bo', 'rand_matrix')}
    del _L0_attn_all

    def _L0_xattn_setup():
        import jax, jax.numpy as jnp
        import numpy as np
        B, S1, S2, DCA = (2, 512, 256, 16)
        QDIM, KDIM, H = (512, 256, 16)
        HD = QDIM // H
        SCALE = HD ** (-0.5)
        EPS = 1e-06
        DCA_WEIGHT = 1.0

        def _ln(t, w, b):
            m = jnp.mean(t, axis=-1, keepdims=True)
            v = jnp.var(t, axis=-1, keepdims=True)
            return (t - m) * jax.lax.rsqrt(v + EPS) * w + b

        def _attn(q, k, v):
            s = jnp.einsum('bhqd,bhkd->bhqk', q, k) * SCALE
            p = jax.nn.softmax(s, axis=-1)
            return jnp.einsum('bhqk,bhkd->bhqd', p, v)
        key = jax.random.key(seed)
        ks = jax.random.split(key, 8)
        w = lambda k, shape: jax.random.normal(k, shape, jnp.float32) * 0.02
        return {'x': jax.random.normal(ks[0], (B, S1, QDIM), jnp.float32), 'y': jax.random.normal(ks[1], (B, S2 + DCA, KDIM), jnp.float32), 'Wq': w(ks[2], (QDIM, QDIM)), 'bq': jnp.zeros((QDIM,), jnp.float32), 'Wk': w(ks[3], (KDIM, QDIM)), 'bk': jnp.zeros((QDIM,), jnp.float32), 'Wv': w(ks[4], (KDIM, QDIM)), 'bv': jnp.zeros((QDIM,), jnp.float32), 'Wkv_dca': w(ks[5], (KDIM, 2 * QDIM)), 'bkv_dca': jnp.zeros((2 * QDIM,), jnp.float32), 'qn_w': jnp.ones((HD,), jnp.float32), 'qn_b': jnp.zeros((HD,), jnp.float32), 'kn_w': jnp.ones((HD,), jnp.float32), 'kn_b': jnp.zeros((HD,), jnp.float32), 'kn_dca_w': jnp.ones((HD,), jnp.float32), 'kn_dca_b': jnp.zeros((HD,), jnp.float32), 'Wo': w(ks[6], (QDIM, QDIM)), 'bo': jnp.zeros((QDIM,), jnp.float32)}
    _L0_xattn_all = _L0_xattn_setup()
    _L0_xattn_in = {k: v for k, v in _L0_xattn_all.items() if k in ('Wq', 'bq', 'Wk', 'bk', 'Wv', 'bv', 'Wkv_dca', 'bkv_dca', 'qn_w', 'qn_b', 'kn_w', 'kn_b', 'kn_dca_w', 'kn_dca_b', 'Wo', 'bo')}
    del _L0_xattn_all

    def _L0_ffn_setup():
        import jax, jax.numpy as jnp
        import numpy as np
        TARGET_SPARSITY = 0.9
        LN_EPS = 1e-05

        def ternary_quant(W):
            scale = jnp.mean(jnp.abs(W))
            q = jnp.clip(jnp.round(W / (scale + 1e-08)), -1.0, 1.0) * scale
            return W + jax.lax.stop_gradient(q - W)

        def layernorm(x, gamma, beta):
            mu = jnp.mean(x, axis=-1, keepdims=True)
            var = jnp.var(x, axis=-1, keepdims=True)
            return (x - mu) * jax.lax.rsqrt(var + LN_EPS) * gamma + beta
        key = jax.random.key(seed)
        ks = jax.random.split(key, 3)
        B, S, D, N = (4, 512, 512, 2048)
        x = jax.random.normal(ks[0], (B, S, D), dtype=jnp.float32)
        W_syn = jax.random.normal(ks[1], (N, D), dtype=jnp.float32) * (1.0 / np.sqrt(D))
        b_syn = jnp.zeros((N,), dtype=jnp.float32)
        W_out = jax.random.normal(ks[2], (D, N), dtype=jnp.float32) * (1.0 / np.sqrt(N))
        b_out = jnp.zeros((D,), dtype=jnp.float32)
        gamma = jnp.ones((D,), dtype=jnp.float32)
        beta = jnp.zeros((D,), dtype=jnp.float32)
        return {'x': x, 'W_syn': W_syn, 'b_syn': b_syn, 'W_out': W_out, 'b_out': b_out, 'gamma': gamma, 'beta': beta}
    _L0_ffn_all = _L0_ffn_setup()
    _L0_ffn_in = {k: v for k, v in _L0_ffn_all.items() if k in ('W_syn', 'b_syn', 'W_out', 'b_out', 'gamma', 'beta')}
    del _L0_ffn_all
    return {'x': x, 'ctx_1024': ctx_1024, 'L0_attn_Wq': _L0_attn_in['Wq'], 'L0_attn_bq': _L0_attn_in['bq'], 'L0_attn_Wk': _L0_attn_in['Wk'], 'L0_attn_bk': _L0_attn_in['bk'], 'L0_attn_Wv': _L0_attn_in['Wv'], 'L0_attn_bv': _L0_attn_in['bv'], 'L0_attn_Wo': _L0_attn_in['Wo'], 'L0_attn_bo': _L0_attn_in['bo'], 'L0_attn_rand_matrix': _L0_attn_in['rand_matrix'], 'L0_xattn_Wq': _L0_xattn_in['Wq'], 'L0_xattn_bq': _L0_xattn_in['bq'], 'L0_xattn_Wk': _L0_xattn_in['Wk'], 'L0_xattn_bk': _L0_xattn_in['bk'], 'L0_xattn_Wv': _L0_xattn_in['Wv'], 'L0_xattn_bv': _L0_xattn_in['bv'], 'L0_xattn_Wkv_dca': _L0_xattn_in['Wkv_dca'], 'L0_xattn_bkv_dca': _L0_xattn_in['bkv_dca'], 'L0_xattn_qn_w': _L0_xattn_in['qn_w'], 'L0_xattn_qn_b': _L0_xattn_in['qn_b'], 'L0_xattn_kn_w': _L0_xattn_in['kn_w'], 'L0_xattn_kn_b': _L0_xattn_in['kn_b'], 'L0_xattn_kn_dca_w': _L0_xattn_in['kn_dca_w'], 'L0_xattn_kn_dca_b': _L0_xattn_in['kn_dca_b'], 'L0_xattn_Wo': _L0_xattn_in['Wo'], 'L0_xattn_bo': _L0_xattn_in['bo'], 'L0_ffn_W_syn': _L0_ffn_in['W_syn'], 'L0_ffn_b_syn': _L0_ffn_in['b_syn'], 'L0_ffn_W_out': _L0_ffn_in['W_out'], 'L0_ffn_b_out': _L0_ffn_in['b_out'], 'L0_ffn_gamma': _L0_ffn_in['gamma'], 'L0_ffn_beta': _L0_ffn_in['beta']}

def reference(x, ctx_1024, L0_attn_Wq, L0_attn_bq, L0_attn_Wk, L0_attn_bk, L0_attn_Wv, L0_attn_bv, L0_attn_Wo, L0_attn_bo, L0_attn_rand_matrix, L0_xattn_Wq, L0_xattn_bq, L0_xattn_Wk, L0_xattn_bk, L0_xattn_Wv, L0_xattn_bv, L0_xattn_Wkv_dca, L0_xattn_bkv_dca, L0_xattn_qn_w, L0_xattn_qn_b, L0_xattn_kn_w, L0_xattn_kn_b, L0_xattn_kn_dca_w, L0_xattn_kn_dca_b, L0_xattn_Wo, L0_xattn_bo, L0_ffn_W_syn, L0_ffn_b_syn, L0_ffn_W_out, L0_ffn_b_out, L0_ffn_gamma, L0_ffn_beta):
    import jax
    import jax.numpy as jnp

    def _L0_attn_ref(hidden_states, Wq, bq, Wk, bk, Wv, bv, Wo, bo, rand_matrix):
        import math
        import jax, jax.numpy as jnp
        import numpy as np
        HID = 512
        H = 16
        HKV = 8
        D = HID // H
        F = D
        SEQ = 512
        BATCH = 2
        THETA = 10000.0

        def _rotate_half(x):
            x1, x2 = (x[..., :x.shape[-1] // 2], x[..., x.shape[-1] // 2:])
            return jnp.concatenate((-x2, x1), axis=-1)

        def _softmax_kernel(x, R):
            n = jnp.sqrt(jnp.sum(x * x, axis=-1, keepdims=True))
            x = x / jnp.maximum(n, 1e-06)
            p = jnp.einsum('...d,ed->...e', x, R)
            feats = jnp.concatenate([jnp.sin(p), jnp.cos(p)], axis=-1)
            return feats / math.sqrt(F)
        b, s, _ = hidden_states.shape
        q = (hidden_states @ Wq.T + bq).reshape(b, s, H, D).transpose(0, 2, 1, 3)
        k = (hidden_states @ Wk.T + bk).reshape(b, s, HKV, D).transpose(0, 2, 1, 3)
        v = (hidden_states @ Wv.T + bv).reshape(b, s, HKV, D).transpose(0, 2, 1, 3)
        inv_freq = 1.0 / THETA ** (jnp.arange(0, D, 2, dtype=jnp.float32) / D)
        freqs = jnp.arange(s, dtype=jnp.float32)[:, None] * inv_freq[None, :]
        emb = jnp.concatenate((freqs, freqs), axis=-1)
        cos = jnp.cos(emb)[None, None, :, :]
        sin = jnp.sin(emb)[None, None, :, :]
        q = q * cos + _rotate_half(q) * sin
        k = k * cos + _rotate_half(k) * sin
        rep = H // HKV
        k = jnp.repeat(k, rep, axis=1)
        v = jnp.repeat(v, rep, axis=1)
        qp = _softmax_kernel(q, rand_matrix)
        kp = _softmax_kernel(k, rand_matrix)
        kv = jnp.einsum('bhsf,bhsd->bsfd', kp, v)
        out = jnp.einsum('bhsf,bsfd->bhsd', qp, kv)
        out = out.reshape(b, s, HID)
        return out @ Wo.T + bo

    def _L0_xattn_ref(x, y, Wq, bq, Wk, bk, Wv, bv, Wkv_dca, bkv_dca, qn_w, qn_b, kn_w, kn_b, kn_dca_w, kn_dca_b, Wo, bo):
        import jax, jax.numpy as jnp
        import numpy as np
        B, S1, S2, DCA = (2, 512, 256, 16)
        QDIM, KDIM, H = (512, 256, 16)
        HD = QDIM // H
        SCALE = HD ** (-0.5)
        EPS = 1e-06
        DCA_WEIGHT = 1.0

        def _ln(t, w, b):
            m = jnp.mean(t, axis=-1, keepdims=True)
            v = jnp.var(t, axis=-1, keepdims=True)
            return (t - m) * jax.lax.rsqrt(v + EPS) * w + b

        def _attn(q, k, v):
            s = jnp.einsum('bhqd,bhkd->bhqk', q, k) * SCALE
            p = jax.nn.softmax(s, axis=-1)
            return jnp.einsum('bhqk,bhkd->bhqd', p, v)
        b, s1, _ = x.shape
        y_dca = y[:, -DCA:, :]
        y_main = y[:, :-DCA, :]
        kv_dca = (y_dca @ Wkv_dca + bkv_dca).reshape(b, DCA, 2, H, HD)
        k_dca = _ln(kv_dca[:, :, 0], kn_dca_w, kn_dca_b)
        v_dca = kv_dca[:, :, 1]
        s2 = y_main.shape[1]
        q = _ln((x @ Wq + bq).reshape(b, s1, H, HD), qn_w, qn_b)
        kv = jnp.concatenate([y_main @ Wk + bk, y_main @ Wv + bv], axis=-1)
        kv = kv.reshape(b, s2, H, 2 * HD)
        k = _ln(kv[..., :HD], kn_w, kn_b)
        v = kv[..., HD:]
        qT = q.transpose(0, 2, 1, 3)
        ctx = _attn(qT, k.transpose(0, 2, 1, 3), v.transpose(0, 2, 1, 3))
        ctx = ctx.transpose(0, 2, 1, 3).reshape(b, s1, QDIM)
        ctx_dca = _attn(qT, k_dca.transpose(0, 2, 1, 3), v_dca.transpose(0, 2, 1, 3))
        ctx_dca = ctx_dca.transpose(0, 2, 1, 3).reshape(b, s1, QDIM)
        ctx = ctx + DCA_WEIGHT * ctx_dca
        return ctx @ Wo + bo

    def _L0_ffn_ref(x, W_syn, b_syn, W_out, b_out, gamma, beta):
        import jax, jax.numpy as jnp
        import numpy as np
        TARGET_SPARSITY = 0.9
        LN_EPS = 1e-05

        def ternary_quant(W):
            scale = jnp.mean(jnp.abs(W))
            q = jnp.clip(jnp.round(W / (scale + 1e-08)), -1.0, 1.0) * scale
            return W + jax.lax.stop_gradient(q - W)

        def layernorm(x, gamma, beta):
            mu = jnp.mean(x, axis=-1, keepdims=True)
            var = jnp.var(x, axis=-1, keepdims=True)
            return (x - mu) * jax.lax.rsqrt(var + LN_EPS) * gamma + beta
        B, S, D = x.shape
        N = W_syn.shape[0]
        x_flat = x.reshape(-1, D)
        z = x_flat @ ternary_quant(W_syn).T + b_syn
        k = max(1, int(N * (1.0 - TARGET_SPARSITY)))
        topv, _ = jax.lax.top_k(z, k)
        thresh = topv[:, -1:]
        hidden = jnp.where(z >= thresh, jax.nn.relu(z), 0.0)
        out = hidden @ ternary_quant(W_out).T + b_out
        out = out.reshape(B, S, D)
        return layernorm(x + out, gamma, beta)
    x = _layernorm(x + _L0_attn_ref(x, L0_attn_Wq, L0_attn_bq, L0_attn_Wk, L0_attn_bk, L0_attn_Wv, L0_attn_bv, L0_attn_Wo, L0_attn_bo, L0_attn_rand_matrix), axis=-1)
    x = _layernorm(x + _L0_xattn_ref(x, ctx_1024, L0_xattn_Wq, L0_xattn_bq, L0_xattn_Wk, L0_xattn_bk, L0_xattn_Wv, L0_xattn_bv, L0_xattn_Wkv_dca, L0_xattn_bkv_dca, L0_xattn_qn_w, L0_xattn_qn_b, L0_xattn_kn_w, L0_xattn_kn_b, L0_xattn_kn_dca_w, L0_xattn_kn_dca_b, L0_xattn_Wo, L0_xattn_bo), axis=-1)
    x = _layernorm(x + _L0_ffn_ref(x, L0_ffn_W_syn, L0_ffn_b_syn, L0_ffn_W_out, L0_ffn_b_out, L0_ffn_gamma, L0_ffn_beta), axis=-1)
    return x

_drawn_inputs = setup_inputs


def setup_inputs(seed=0):
    import zlib

    import numpy as np

    out = dict(_drawn_inputs(seed))
    spreads = {'L0_xattn_bq': (0.0, 0.508),
     'L0_xattn_bk': (0.0, 0.1),
     'L0_xattn_bv': (0.0, 0.1),
     'L0_xattn_bkv_dca': (0.0, 0.1),
     'L0_xattn_qn_w': (1.0, 0.6),
     'L0_xattn_qn_b': (0.0, 0.8),
     'L0_xattn_kn_w': (1.0, 0.6),
     'L0_xattn_kn_b': (0.0, 0.8),
     'L0_xattn_kn_dca_w': (1.0, 0.6),
     'L0_xattn_kn_dca_b': (0.0, 0.8),
     'L0_xattn_bo': (0.0, 0.1),
     'L0_ffn_b_syn': (0.0, 0.1),
     'L0_ffn_b_out': (0.0, 0.1),
     'L0_ffn_gamma': (1.0, 0.2),
     'L0_ffn_beta': (0.0, 0.1)}
    factors = {'L0_attn_bq': 7.478, 'L0_attn_bk': 7.563, 'L0_attn_bv': 4.198}
    for name, (base, spread) in spreads.items():
        noise = np.random.default_rng([zlib.crc32(name.encode()), seed]).standard_normal(out[name].shape)
        drawn = base * np.exp(spread * noise) if base else spread * noise
        out[name] = jnp.asarray(drawn.astype(out[name].dtype))
    for name, factor in factors.items():
        out[name] = (out[name] * factor).astype(out[name].dtype)
    return out
```

```python
import concourse.bass as bass
from concourse import mybir
from contextlib import ExitStack

F32 = mybir.dt.float32
F32R = mybir.dt.float32r
U32 = mybir.dt.uint32
ALU = mybir.AluOpType
ACT = mybir.ActivationFunctionType
AX = mybir.AxisListType

P = 128
BATCH, SEQ, DM = 4, 512, 512
TT = SEQ // P
DC = DM // P
HEADS, KV_HEADS, HD = 16, 8, 32
TWO_PI_HI = 6.28125
TWO_PI_MID = 0.0019350051879882812
TWO_PI_LO = 3.0199159819567e-07
PI = 3.1415925
START = 1
ROUND_MAGIC = 12582912.0


class Chain:

    def __init__(self, eng, sem):
        self.eng, self.sem, self.n = eng, sem, 0

    def __call__(self, ins):
        self.n += 1
        return ins.then_inc(self.sem, 1)

    def wait(self):
        self.eng.wait_ge(self.sem, self.n)


def bank_plan(groups, slots):
    assert len(groups) % slots == 0
    return {g: (i % slots, i // slots + 1) for i, g in enumerate(groups)}


def start_counters(nc, counters):
    with nc.Block() as block:
        @block.sync
        def _(sp):
            for s in counters:
                sp.sem_inc(s, START)


def self_attention(nc, io, x1_dram):
    QKV = DM + 2 * KV_HEADS * HD
    QK_HEADS = HEADS + KV_HEADS
    FE = HD // 2
    SLOTS = 8
    groups = [(n, t) for t in range(TT) for n in ("q", "kv")]
    groups += [(n, t) for t in range(TT) for n in ("rot0", "rot1", "proj")]
    groups += [("wo", t) for t in range(TT)]
    bank = bank_plan(groups, SLOTS)
    USES = len(groups) // SLOTS
    POOL_H = 5

    with ExitStack() as ctx:
        def sb(name, shape, dt=F32):
            return ctx.enter_context(nc.sbuf_tensor("sa_" + name, shape, dt))

        def sem(name):
            return ctx.enter_context(nc.semaphore("a_" + name))

        counters = []

        def counter(name):
            counters.append(sem(name))
            return counters[-1]

        ps = [ctx.enter_context(nc.psum_tensor(f"a_ps{i}", [P, 512], F32)) for i in range(SLOTS)]
        full = [counter(f"bank{i}_full") for i in range(SLOTS)]
        free = [counter(f"bank{i}_free") for i in range(SLOTS)]

        w1h, w1l = sb("w1h", [P, DC, QKV], F32R), sb("w1l", [P, DC, QKV], F32R)
        woh, wol = sb("woh", [P, DC, DM], F32R), sb("wol", [P, DC, DM], F32R)
        b1 = sb("b1", [P, QKV])
        bo = sb("bo", [P, DM])
        cosb, sinb = sb("cosb", [P, TT, HD]), sb("sinb", [P, TT, HD])
        ident = sb("ident", [P, P])
        rmat = sb("rmat", [P, 4 * FE])
        xt = sb("xt", [P, DC, SEQ])
        xth, xtl = sb("xth", [P, DC, SEQ], F32R), sb("xtl", [P, DC, SEQ], F32R)
        xres = sb("xres", [P, TT, DM])
        qkv = sb("qkv", [P, 2, QKV])
        vs = sb("vs", [P, TT, KV_HEADS * HD])
        turn = sb("turn", [P, 2, QK_HEADS * HD])
        qkr = sb("qkr", [P, TT, QK_HEADS * HD])
        sq = sb("sq", [P, QK_HEADS * HD])
        ssum = sb("ssum", [P, TT * QK_HEADS])
        rn = sb("rn", [P, TT * QK_HEADS])
        qkT = sb("qkT", [P, 6, P])
        feat = sb("feat", [P, 2, QK_HEADS * HD])
        fk = sb("fk", [P, QK_HEADS * HD])
        sc = sb("sc", [P, 2, QK_HEADS * HD])
        prod = sb("prod", [P, HEADS, KV_HEADS, HD])
        w1 = prod[:].rearrange("p h g d -> p (h g d)").rearrange("p (c n) -> p c n", c=DC)
        wo = xt[:]
        amat = sb("amat", [P, HEADS, KV_HEADS])
        o = sb("o", [P, DM])
        oT = sb("oT", [P, TT, DM])
        oth, otl = sb("oth", [P, TT, DM], F32R), sb("otl", [P, TT, DM], F32R)
        s = sb("s", [P, 2, DM])
        st6 = sb("st6", [P, 6])
        mv = sb("mv", [P, 2, 2])
        ve = sb("ve", [P, 2])
        rstd = sb("rstd", [P, 2])
        half = sb("half", [P, 1])
        x1 = sb("x1", [P, 2, DM])

        w_in, const_in, xt_in, xres_in = sem("w_in"), sem("const_in"), counter("xt_in"), counter("xres_in")
        rzero = sem("rzero")
        wh_ready, w_ready = sem("wh_ready"), sem("w_ready")
        xh_ready, xl_ready = counter("xh_ready"), counter("xl_ready")
        qkv_ready, v_ready, turn_ready = counter("qkv_ready"), counter("v_ready"), counter("turn_ready")
        qkr_ready, sq_ready, sqsum_ready, norm_ready = counter("qkr_ready"), counter("sq_ready"), counter("sqsum_ready"), counter("norm_ready")
        qkT_ready, proj_done = counter("qkT_ready"), counter("proj_done")
        arg_ready, sc_ready = counter("arg_ready"), counter("sc_ready")
        prodp_ready, prod_used, a_ready = counter("prodp_ready"), counter("prod_used"), counter("a_ready")
        oT_ready, oh_ready, ol_ready = counter("oT_ready"), counter("oh_ready"), counter("ol_ready")
        x_biased, ve_ready, rstd_ready = counter("x_biased"), counter("ve_ready"), counter("rstd_ready")
        x1_ready, x1_out = counter("x1_ready"), [counter(f"x1_out{i}") for i in range(2)]
        dchain = sem("dchain")

        start_counters(nc, counters)
        with nc.Block() as block:

            @block.sync
            def _(sp):
                sp.dma_start(w1, io["w1T"].rearrange("(c p) n -> p c n", p=P)).then_inc(w_in, 16)
                sp.dma_start(wo, io["woT"].rearrange("(c p) n -> p c n", p=P)).then_inc(w_in, 16)
                sp.dma_start(b1[:], io["b1"].partition_broadcast(P)).then_inc(const_in, 16)
                sp.dma_start(bo[:], io["a_bo"].partition_broadcast(P)).then_inc(const_in, 16)
                sp.dma_start(cosb[:], io["cos"].rearrange("(t p) d -> p t d", p=P)).then_inc(const_in, 16)
                sp.dma_start(sinb[:], io["sin"].rearrange("(t p) d -> p t d", p=P)).then_inc(const_in, 16)
                sp.dma_start(ident[:], io["ident"]).then_inc(const_in, 16)
                sp.wait_ge(rzero, 1)
                for j in range(4):
                    sp.dma_start(rmat[HD * j:HD * (j + 1), FE * j:FE * (j + 1)], io["randT"]).then_inc(const_in, 16)
                sp.wait_ge(w_ready, 1)
                with sp.Fori(0, BATCH) as b:
                    sp.wait_ge(xh_ready, START + b)
                    sp.wait_ge(xl_ready, START + b)
                    sp.dma_start(xt[:], io["xT"][bass.ds(b, 1)].rearrange("o (c p) n -> p (o c) n", p=P)).then_inc(xt_in, 16)
                    sp.wait_ge(x1_ready, START + b * TT)
                    sp.dma_start(xres[:], io["x"][bass.ds(b, 1)].rearrange("o (t p) n -> p (o t) n", p=P)).then_inc(xres_in, 16)
                    for t in range(TT):
                        sp.wait_ge(x1_ready, START + b * TT + t + 1)
                        sp.dma_start(x1_dram[bass.ds(b * TT + t, 1)].rearrange("o p n -> p (o n)"), x1[:, t % 2]).then_inc(x1_out[t % 2], 16)
                for i in range(2):
                    sp.wait_ge(x1_out[i], START + 16 * BATCH * TT // 2)

            @block.scalar
            def _(act):
                act.wait_ge(w_in, 32)
                nc.scalar.copy(w1h[:], w1)
                nc.scalar.copy(woh[:], wo).then_inc(wh_ready, 1)
                with act.Fori(0, BATCH) as b:
                    act.wait_ge(xt_in, START + b * 16 + 16)
                    act.wait_ge(v_ready, START + b * TT)
                    nc.scalar.copy(xth[:], xt[:]).then_inc(xh_ready, 1)
                    for t in range(TT):
                        act.wait_ge(qkr_ready, START + b * TT + t + 1)
                        if t:
                            act.wait_ge(sqsum_ready, START + b * TT + t)
                        else:
                            act.wait_ge(sqsum_ready, START + b * TT)
                        nc.scalar.activation(sq[:], qkr[:, t], ACT.Square).then_inc(sq_ready, 1)
                    act.wait_ge(sqsum_ready, START + b * TT + TT)
                    nc.scalar.activation(rn[:], ssum[:], ACT.Sqrt).then_inc(norm_ready, 1)
                    for t in range(TT):
                        for i in range(2):
                            slot, use = bank[f"rot{i}", t]
                            act.wait_ge(full[slot], START + b * USES + use)
                            if i == 0:
                                act.wait_ge(proj_done, START + b * TT + t)
                            nc.scalar.copy(qkT[:, 3 * i:3 * i + 3], ps[slot][:, 0:3 * P].rearrange("p (c n) -> p c n", n=P)).then_inc(free[slot], 1)
                        act.wait_ge(free[slot], START + b * USES + use)
                        act.sem_inc(qkT_ready, 1)
                    for t in range(TT + 2):
                        act.wait_ge(oT_ready, START + b * TT + max(t - 1, 0))
                        if t < TT:
                            act.wait_ge(arg_ready, START + b * TT + t + 1)
                            nc.scalar.activation(sc[:, t % 2], feat[:, t % 2], ACT.Sin).then_inc(sc_ready, 1)
                        if t == 2:
                            act.wait_ge(x1_ready, START + b * TT)
                        if t >= 2:
                            nc.scalar.copy(oth[:, t - 2], oT[:, t - 2]).then_inc(oh_ready, 1)

            @block.gpsimd
            def _(pool):
                pool.memset(rmat[:], 0.0).then_inc(rzero, 1)
                pool.memset(half[:], -0.5)
                pool.wait_ge(const_in, 16 * 9)
                pool.wait_ge(w_ready, 1)
                with pool.Fori(0, BATCH) as b:
                    def lower_part(t):
                        pool.wait_ge(oh_ready, START + b * TT + t + 1)
                        nc.gpsimd.tensor_tensor(otl[:, t], oT[:, t], oth[:, t].bitcast(F32), ALU.subtract).then_inc(ol_ready, 1)

                    pool.wait_ge(xres_in, START + b * 16 + 16)
                    nc.gpsimd.tensor_tensor(xres[:], xres[:], bo[:].unsqueeze(1).broadcast_to([P, TT, DM]), ALU.add).then_inc(x_biased, 1)
                    for t in range(TT):
                        pool.wait_ge(qkv_ready, START + b * TT + t + 1)
                        pool.wait_ge(qkr_ready, START + b * TT + max(t - 1, 0))
                        x3 = qkv[:, t % 2, 0:QK_HEADS * HD].rearrange("p (h d) -> p h d", d=HD)
                        o3 = turn[:, t % 2].rearrange("p (h d) -> p h d", d=HD)
                        sn = sinb[:, t].unsqueeze(1).broadcast_to([P, QK_HEADS, HD])
                        nc.gpsimd.tensor_tensor(o3[:, :, 0:FE], x3[:, :, FE:HD], sn[:, :, 0:FE], ALU.mult)
                        nc.gpsimd.tensor_tensor(o3[:, :, FE:HD], x3[:, :, 0:FE], sn[:, :, FE:HD], ALU.mult).then_inc(turn_ready, 1)
                    for t in range(TT):
                        f = sc[:, t % 2].rearrange("p (h d) -> p h d", d=HD)
                        pool.wait_ge(sc_ready, START + b * TT + t + 1)
                        pool.wait_ge(prod_used, START + b * 2 * TT + 2 * t)
                        nc.gpsimd.tensor_tensor(
                            prod[:, 0:POOL_H],
                            f[:, 0:POOL_H].unsqueeze(2).broadcast_to([P, POOL_H, KV_HEADS, HD]),
                            f[:, HEADS:].unsqueeze(1).broadcast_to([P, POOL_H, KV_HEADS, HD]), ALU.mult).then_inc(prodp_ready, 1)
                        pool.wait_ge(a_ready, START + b * TT + t + 1)
                        pool.wait_ge(prod_used, START + b * 2 * TT + 2 * t + 1)
                        v3 = vs[:, t].rearrange("p (g d) -> p d g", d=HD)
                        p4 = prod[:].rearrange("p h g d -> p (h g d)").rearrange("p (h d g) -> p h d g", h=HEADS, g=KV_HEADS)
                        nc.gpsimd.tensor_tensor(
                            p4[:, 0:POOL_H],
                            amat[:, 0:POOL_H].unsqueeze(2).broadcast_to([P, POOL_H, HD, KV_HEADS]),
                            v3.unsqueeze(1).broadcast_to([P, POOL_H, HD, KV_HEADS]), ALU.mult).then_inc(prodp_ready, 1)
                        if t >= 2:
                            lower_part(t - 2)
                    lower_part(TT - 2)
                    lower_part(TT - 1)
                    for t in range(TT):
                        pool.wait_ge(ve_ready, START + b * TT + t + 1)
                        nc.gpsimd.tensor_tensor(rstd[:, t % 2:t % 2 + 1], ve[:, t % 2:t % 2 + 1], half[:], ALU.pow).then_inc(rstd_ready, 1)

            def self_attend(dve, c, b, t):
                f = sc[:, t % 2].rearrange("p (h d) -> p h d", d=HD)
                NH = HEADS - POOL_H
                dve.wait_ge(sc_ready, START + b * TT + t + 1)
                c.wait()
                c(nc.vector.tensor_tensor(
                    prod[:, POOL_H:],
                    f[:, POOL_H:HEADS].unsqueeze(2).broadcast_to([P, NH, KV_HEADS, HD]),
                    f[:, HEADS:].unsqueeze(1).broadcast_to([P, NH, KV_HEADS, HD]), ALU.mult))
                c.wait()
                dve.wait_ge(prodp_ready, START + b * 2 * TT + 2 * t + 1)
                nc.vector.tensor_reduce(amat[:], prod[:], AX.X, ALU.add).then_inc(prod_used, 1)
                dve.wait_ge(prod_used, START + b * 2 * TT + 2 * t + 1)
                dve.sem_inc(a_ready, 1)
                v3 = vs[:, t].rearrange("p (g d) -> p d g", d=HD)
                p4 = prod[:].rearrange("p h g d -> p (h g d)").rearrange("p (h d g) -> p h d g", h=HEADS, g=KV_HEADS)
                c(nc.vector.tensor_tensor(
                    p4[:, POOL_H:],
                    amat[:, POOL_H:].unsqueeze(2).broadcast_to([P, NH, HD, KV_HEADS]),
                    v3.unsqueeze(1).broadcast_to([P, NH, HD, KV_HEADS]), ALU.mult))
                c.wait()
                dve.wait_ge(prodp_ready, START + b * 2 * TT + 2 * t + 2)
                nc.vector.tensor_reduce(o[:].rearrange("p (h d) -> p h d", d=HD), p4, AX.X, ALU.add).then_inc(prod_used, 1)
                dve.wait_ge(prod_used, START + b * 2 * TT + 2 * t + 2)
                nc.vector.transpose(oT[:, t], o[:]).then_inc(oT_ready, 1)

            @block.vector
            def _(dve):
                dve.wait_ge(w_in, 32)
                dve.wait_ge(wh_ready, 1)
                nc.vector.tensor_tensor(w1l[:], w1, w1h[:].bitcast(F32), ALU.subtract)
                nc.vector.tensor_tensor(wol[:], wo, woh[:].bitcast(F32), ALU.subtract).then_inc(w_ready, 1)
                dve.wait_ge(const_in, 16 * 9)
                with dve.Fori(0, BATCH) as b:
                    dve.sem_clear(dchain)
                    c = Chain(dve, dchain)
                    dve.wait_ge(xh_ready, START + b + 1)
                    c(nc.vector.tensor_tensor(xtl[:], xt[:], xth[:].bitcast(F32), ALU.subtract))
                    c.wait()
                    dve.sem_inc(xl_ready, 1)
                    for t in range(TT):
                        for n, lo in (("q", 0), ("kv", 512)):
                            slot, use = bank[n, t]
                            dve.wait_ge(full[slot], START + b * USES + use)
                            c(nc.vector.tensor_tensor(qkv[:, t % 2, lo:lo + 512], ps[slot][:], b1[:, lo:lo + 512], ALU.add))
                            c.wait()
                            dve.sem_inc(free[slot], 1)
                        dve.sem_inc(qkv_ready, 1)
                        c(nc.vector.tensor_scalar(vs[:, t], qkv[:, t % 2, QK_HEADS * HD:], 1.0 / 16, None, ALU.mult))
                        c(nc.vector.tensor_tensor(qkr[:, t].rearrange("p (h d) -> p h d", d=HD),
                                                  qkv[:, t % 2, 0:QK_HEADS * HD].rearrange("p (h d) -> p h d", d=HD),
                                                  cosb[:, t].unsqueeze(1).broadcast_to([P, QK_HEADS, HD]), ALU.mult))
                        c.wait()
                        dve.sem_inc(v_ready, 1)
                        dve.wait_ge(turn_ready, START + b * TT + t + 1)
                        nc.vector.tensor_tensor(qkr[:, t], qkr[:, t], turn[:, t % 2], ALU.add).then_inc(qkr_ready, 1)
                        dve.wait_ge(sq_ready, START + b * TT + t + 1)
                        nc.vector.tensor_reduce(ssum[:, t * QK_HEADS:(t + 1) * QK_HEADS], sq[:].rearrange("p (h d) -> p h d", d=HD),
                                                AX.X, ALU.add).then_inc(sqsum_ready, 1)
                    dve.wait_ge(norm_ready, START + b + 1)
                    c(nc.vector.tensor_scalar(rn[:], rn[:], 1e-6, None, ALU.max))
                    c.wait()
                    c(nc.vector.reciprocal(rn[:], rn[:]))
                    for t in range(TT):
                        slot, use = bank["proj", t]
                        f = feat[:, t % 2].rearrange("p (h d) -> p h d", d=HD)
                        dve.wait_ge(full[slot], START + b * USES + use)
                        if t >= 2:
                            dve.wait_ge(sc_ready, START + b * TT + t - 1)
                        c.wait()
                        c(nc.vector.tensor_tensor(f[:, :, 0:FE], ps[slot][:, 0:QK_HEADS * FE].rearrange("p (h d) -> p h d", d=FE),
                                                  rn[:, t * QK_HEADS:(t + 1) * QK_HEADS].unsqueeze(2).broadcast_to([P, QK_HEADS, FE]), ALU.mult))
                        c.wait()
                        dve.sem_inc(free[slot], 1)
                        c(nc.vector.tensor_scalar(f[:, :, FE:HD], f[:, :, 0:FE], 1.5707963267948966, None, ALU.add))
                        c.wait()
                        c(nc.vector.tensor_scalar(fk[:], feat[:, t % 2], 0.15915494309189535, ROUND_MAGIC, ALU.mult, ALU.add))
                        c.wait()
                        c(nc.vector.tensor_scalar(fk[:], fk[:], ROUND_MAGIC, None, ALU.subtract))
                        c.wait()
                        for part in (TWO_PI_HI, TWO_PI_MID, TWO_PI_LO):
                            c(nc.vector.scalar_tensor_tensor(feat[:, t % 2], fk[:], -part, feat[:, t % 2], ALU.mult, ALU.add))
                            c.wait()
                        nc.vector.tensor_scalar(feat[:, t % 2], feat[:, t % 2], -PI, PI, ALU.max, ALU.min).then_inc(arg_ready, 1)
                        if t >= 1:
                            self_attend(dve, c, b, t - 1)
                    self_attend(dve, c, b, TT - 1)
                    for t in range(TT):
                        slot, use = bank["wo", t]
                        if t == 0:
                            dve.wait_ge(x_biased, START + b + 1)
                        dve.wait_ge(full[slot], START + b * USES + use)
                        c(nc.vector.tensor_tensor(s[:, t % 2], ps[slot][:], xres[:, t], ALU.add))
                        c.wait()
                        dve.sem_inc(free[slot], 1)
                        c(nc.vector.bn_stats(st6[:], s[:, t % 2]))
                        c.wait()
                        c(nc.vector.bn_aggr(mv[:, t % 2], st6[:]))
                        c.wait()
                        nc.vector.tensor_scalar(ve[:, t % 2:t % 2 + 1], mv[:, t % 2, 1:2], 1e-5, None, ALU.add).then_inc(ve_ready, 1)
                        dve.wait_ge(rstd_ready, START + b * TT + t + 1)
                        dve.wait_ge(x1_out[t % 2], START + (b * (TT // 2) + t // 2) * 16)
                        nc.vector.tensor_scalar(x1[:, t % 2], s[:, t % 2], mv[:, t % 2, 0:1], rstd[:, t % 2:t % 2 + 1],
                                                ALU.subtract, ALU.mult).then_inc(x1_ready, 1)
                    c.wait()

            @block.tensor
            def _(pe):
                def product(slot, pairs):
                    for i, (l, r) in enumerate(pairs):
                        last = nc.tensor.matmul(ps[slot][:], l, r, start=(i == 0), stop=(i == len(pairs) - 1))
                    return last

                pe.wait_ge(const_in, 16 * 9)
                pe.wait_ge(w_ready, 1)
                with pe.Fori(0, BATCH) as b:
                    pe.wait_ge(xh_ready, START + b + 1)
                    pe.wait_ge(xl_ready, START + b + 1)
                    for t in range(TT):
                        tok = slice(P * t, P * (t + 1))
                        for n, lo in (("q", 0), ("kv", 512)):
                            slot, use = bank[n, t]
                            pe.wait_ge(free[slot], START + b * USES + use - 1)
                            product(slot, [(x[:, k, tok], w[:, k, lo:lo + 512]) for k in range(DC)
                                           for x, w in ((xth, w1h), (xtl, w1h), (xth, w1l))]).then_inc(full[slot], 1)
                    for t in range(TT):
                        pe.wait_ge(qkr_ready, START + b * TT + t + 1)
                        for i in range(2):
                            slot, use = bank[f"rot{i}", t]
                            pe.wait_ge(free[slot], START + b * USES + use - 1)
                            for k in range(3):
                                last = nc.tensor.transpose(ps[slot][:, P * k:P * (k + 1)], qkr[:, t, P * (3 * i + k):P * (3 * i + k + 1)], ident[:])
                            last.then_inc(full[slot], 1)
                        slot, use = bank["proj", t]
                        pe.wait_ge(free[slot], START + b * USES + use - 1)
                        pe.wait_ge(qkT_ready, START + b * TT + t + 1)
                        for k in range(6):
                            last = nc.tensor.matmul(ps[slot][:, 4 * FE * k:4 * FE * (k + 1)], qkT[:, k], rmat[:], start=True, stop=True)
                        last.then_inc(full[slot], 1)
                        pe.wait_ge(full[slot], START + b * USES + use)
                        pe.sem_inc(proj_done, 1)
                    for t in range(TT):
                        slot, use = bank["wo", t]
                        pe.wait_ge(free[slot], START + b * USES + use - 1)
                        pe.wait_ge(ol_ready, START + b * TT + TT)
                        product(slot, [(x[:, k, P * t:P * (t + 1)], w[:, k]) for k in range(DC)
                                       for x, w in ((oth, woh), (otl, woh), (oth, wol))]).then_inc(full[slot], 1)


CTX, CDM, DCA = 1024, 256, 16
KT_N = CTX // P
CC = CDM // P
MAIN = CTX - DCA
LAST = P - DCA
GROUP = 4
GROUPS = HEADS // GROUP
ROWS = 3 * HD


def cross_attention(nc, io, x1_dram, x2_dram, wq_dram, wd_dram):
    HT = HEADS * HD
    TILES = TT + KT_N
    PAIRS = KT_N // 2
    groups = []
    for t in range(TT + 1):
        groups += [("x1T", t)] * (t < TT) + [("head", t - 1)] * (t > 0)
    groups += [("head", n) for n in range(TT, TILES)]
    for g in range(GROUPS):
        groups += [("kT", g), ("qT", g)]
        groups += [("max", g, i, t) for i in range(GROUP) for t in range(TT)]
        groups += [("shift", g, j) for j in range(2)]
        groups += [("score", g, kk, i) for kk in range(PAIRS) for i in range(GROUP)]
    groups += [("wo", t) for t in range(TT)]
    bank = bank_plan(groups, 2)
    USES = len(groups) // 2
    EXPS = GROUPS * PAIRS * GROUP

    with ExitStack() as ctx:
        def sem(name):
            return ctx.enter_context(nc.semaphore("c_" + name))

        counters = []

        def counter(name):
            counters.append(sem(name))
            return counters[-1]

        def sb_in(stack):
            return lambda name, shape, dt=F32: stack.enter_context(nc.sbuf_tensor("sc_" + name, shape, dt))

        sb = sb_in(ctx)
        wide = [ctx.enter_context(nc.psum_tensor(f"c_wide{i}", [P, 2, 512], F32)) for i in range(2)]
        acc = {n: ctx.enter_context(nc.psum_tensor("c_" + n, [P, 512], F32)) for n in ("ctx_main", "sum_main", "ctx_dca", "sum_dca")}
        full = [counter(f"wide{i}_full") for i in range(2)]

        qk = sb("qk", [P, TILES, HT])
        packh, packl = sb("packh", [P, CTX + SEQ], F32R), sb("packl", [P, CTX + SEQ], F32R)
        v = sb("v", [P, KT_N, HT])
        vd = sb("vd", [P, HT])
        kT = sb("kT", [ROWS + 2, GROUP, CTX], F32R)
        qT = sb("qT", [ROWS + 2, GROUP, SEQ], F32R)
        wkvh, wkvl = sb("wkvh", [P, CC, 2 * HT], F32R), sb("wkvl", [P, CC, 2 * HT], F32R)
        woh, wol = sb("woh", [P, DC, DM], F32R), sb("wol", [P, DC, DM], F32R)
        x1 = sb("x1", [P, TT, DM])
        ct = sb("ct", [P, 2, SEQ])
        rec = sb("rec", [P, 2, SEQ])
        bq, bkv, bkv7, bo = sb("bq", [P, HT]), sb("bkv", [P, 2 * HT]), sb("bkv7", [P, 2 * HT]), sb("bo", [P, DM])
        nw, nb = sb("nw", [P, 3, HD]), sb("nb", [P, 3, HD])
        ident = sb("ident", [P, P])
        dca_row = sb("dca_row", [P, 1])
        ones, ones_dca = sb("ones", [P, HD]), sb("ones_dca", [P, HD])
        yd = sb("yd", [P, CC, P])
        eps6, half = sb("eps6", [P, 1]), sb("half", [P, 1])
        ss, sd = sb("ss", [P, 2, HEADS]), sb("sd", [P, 2, HEADS])
        mx = sb("mx", [P, ROWS + HEADS * TT * 2])
        st6, mv, ve, rstd = sb("st6", [P, 6]), sb("mv", [P, 2, 2]), sb("ve", [P, 2]), sb("rstd", [P, 2])
        with ExitStack() as region:
            r = sb_in(region)
            x1h, x1l = r("x1h", [P, DC, SEQ], F32R), r("x1l", [P, DC, SEQ], F32R)
            wqh, wql = r("wqh", [P, DC, HT], F32R), r("wql", [P, DC, HT], F32R)
        with ExitStack() as region:
            r = sb_in(region)
            yh, yl = r("yh", [P, CC, CTX], F32R), r("yl", [P, CC, CTX], F32R)
            yt, wd = r("yt", [P, CC, CTX]), r("wd", [P, CC, 2 * HT])
        p = sb("p", [P, 2, GROUP, 2, SEQ])
        with ExitStack() as region:
            r = sb_in(region)
            raw, sq, kn = r("raw", [P, 4, HT]), r("sq", [P, 2, HT]), r("kn", [P, 2, HT])
        cth, ctl = sb("cth", [P, GROUPS, SEQ], F32R), sb("ctl", [P, GROUPS, SEQ], F32R)
        x2 = rec

        const_in, w_ready = sem("const_in"), sem("w_ready")
        x1_in, wq_in, y_in, wd_in = counter("x1_in"), counter("wq_in"), counter("y_in"), counter("wd_in")
        x1h_ready, x1l_ready, yh_ready, yl_ready, yd_ready = counter("x1h_ready"), counter("x1l_ready"), counter("yh_ready"), counter("yl_ready"), counter("yd_ready")
        raw_ready, sq_ready, ss_ready, sd_ready, unit_ready, kn_ready = (counter(n) for n in ("raw_ready", "sq_ready", "ss_ready", "sd_ready", "unit_ready", "kn_ready"))
        vd_ready = counter("vd_ready")
        packh_ready, packl_ready = counter("packh_ready"), counter("packl_ready")
        heads_in = [counter(f"head{i}_in") for i in range(GROUP)]
        v_ready, wo_taken = counter("v_ready"), counter("wo_taken")
        mx_ready, shift_ready, exp_ready, pv_done = counter("mx_ready"), counter("shift_ready"), counter("exp_ready"), counter("pv_done")
        ct_ready, ch_ready, cl_ready = counter("ct_ready"), counter("ch_ready"), counter("cl_ready")
        x1_biased, ve_ready, rstd_ready, x2_ready = counter("x1_biased"), counter("ve_ready"), counter("rstd_ready"), counter("x2_ready")
        x2_out = [counter(f"x2_out{i}") for i in range(2)]
        HEAD_DMAS = 16 * 6
        dchain, pchain = sem("dchain"), sem("pchain")
        spill, split = sem("spill"), sem("split")
        stage = qk[:].rearrange("p a n -> p (a n)")
        W = {"wkv": (CC, 2 * HT), "wo": (DC, DM), "wq": (DC, HT), "wd": (CC, 2 * HT)}
        staged = {n: stage[:, 2048 * i:2048 * (i + 1)].rearrange("p (c n) -> p c n", c=W[n][0]) for i, n in enumerate(("wkv", "wo", "wq"))}
        staged["wd"] = v[:, 0:4].rearrange("p a n -> p (a n)").rearrange("p (c n) -> p c n", c=CC)

        with nc.Block() as block:
            @block.sync
            def _(sp):
                for s in counters:
                    sp.sem_inc(s, START)
                for n in W:
                    sp.dma_start(staged[n], io["c_" + n].rearrange("(c p) n -> p c n", p=P)).then_inc(const_in, 16)
                sp.dma_start(bq[:], io["c_bq"].partition_broadcast(P)).then_inc(const_in, 16)
                sp.dma_start(bkv[:], io["c_bkv"].partition_broadcast(P)).then_inc(const_in, 16)
                sp.dma_start(bkv7[0:LAST], io["c_bkv"].partition_broadcast(LAST)).then_inc(const_in, 16)
                sp.dma_start(bkv7[LAST:P], io["c_bd"].partition_broadcast(DCA)).then_inc(const_in, 16)
                sp.dma_start(bo[:], io["c_bo"].partition_broadcast(P)).then_inc(const_in, 16)
                for t_, src in ((nw, "nw"), (nb, "nb")):
                    for k in range(2):
                        sp.dma_start(t_[:, k], io[src][k].partition_broadcast(P)).then_inc(const_in, 16)
                    sp.dma_start(t_[0:LAST, 2], io[src][1].partition_broadcast(LAST)).then_inc(const_in, 16)
                    sp.dma_start(t_[LAST:P, 2], io[src][2].partition_broadcast(DCA)).then_inc(const_in, 16)
                sp.dma_start(ident[:], io["ident"]).then_inc(const_in, 16)
                sp.dma_start(dca_row[:], io["dca_row"]).then_inc(const_in, 16)
                sp.dma_start(rec[ROWS:ROWS + 2].rearrange("p a n -> p (a n)"), io["key_rows"]).then_inc(const_in, 16)
                sp.wait_ge(w_ready, 1)
                sp.dma_start(wd_dram, staged["wd"]).then_inc(spill, 16)
                sp.wait_ge(split, 2)
                sp.dma_start(wq_dram[0], wqh[:].bitcast(F32)).then_inc(spill, 16)
                sp.dma_start(wq_dram[1], wql[:].bitcast(F32)).then_inc(spill, 16)
                sp.wait_ge(spill, 48)

            @block.scalar
            def _(act):
                act.wait_ge(const_in, 16 * 20)
                for i in range(GROUP):
                    nc.scalar.copy(kT[ROWS:ROWS + 2, i], rec[ROWS:ROWS + 2].rearrange("p a n -> p (a n)"))
                act.wait_ge(w_ready, 1)
                nc.scalar.copy(wqh[:], staged["wq"])
                nc.scalar.copy(wkvh[:], staged["wkv"])
                nc.scalar.copy(woh[:], staged["wo"]).then_inc(split, 1)

            @block.gpsimd
            def _(pool):
                pool.memset(ones[:], 1.0)
                pool.memset(eps6[:], 1e-6)
                pool.memset(half[:], -0.5)
                pool.memset(mx[:], 0.0)
                pool.memset(yd[:], 0.0)

            @block.vector
            def _(dve):
                dve.wait_ge(const_in, 16 * 20)
                c = Chain(dve, dchain)
                c(nc.vector.tensor_scalar(ones_dca[:], ident[:, 0:HD], 0.0, dca_row[:, 0:1], ALU.mult, ALU.add))
                for part, mean in ((staged["wq"], ss[:].rearrange("p a h -> p (a h)")), (staged["wkv"][:, :, 0:HT], ss[:].rearrange("p a h -> p (a h)")),
                                   (staged["wd"][:, :, 0:HT], ss[:].rearrange("p a h -> p (a h)")), (bq[:].unsqueeze(1), ss[:, 0]),
                                   (bkv[:, 0:HT].unsqueeze(1), ss[:, 0]), (bkv7[:, 0:HT].unsqueeze(1), ss[:, 0])):
                    n = part.shape[1]
                    step = min(n, 2)
                    for k in range(0, n, step):
                        w = part[:, k:k + step].rearrange("p c (h d) -> p c h d", d=HD)
                        m = mean.rearrange("p (c h) -> p c h", h=HEADS)
                        c.wait()
                        c(nc.vector.tensor_reduce(m, w, AX.X, ALU.add))
                        c.wait()
                        c(nc.vector.tensor_scalar(m, m, -1.0 / HD, None, ALU.mult))
                        c.wait()
                        c(nc.vector.tensor_tensor(w, w, m.unsqueeze(3).broadcast_to([P, step, HEADS, HD]), ALU.add))
                c.wait()
                dve.sem_inc(w_ready, 1)
                dve.wait_ge(split, 1)
                nc.vector.tensor_tensor(wql[:], staged["wq"], wqh[:].bitcast(F32), ALU.subtract)
                nc.vector.tensor_tensor(wkvl[:], staged["wkv"], wkvh[:].bitcast(F32), ALU.subtract)
                nc.vector.tensor_tensor(wol[:], staged["wo"], woh[:].bitcast(F32), ALU.subtract).then_inc(split, 1)
                dve.wait_ge(split, 2)
                dve.sem_clear(dchain)

        with nc.Block() as block:
            @block.sync
            def _(sp):
                with sp.Fori(0, BATCH) as b:
                    first = sp.snap(b * TT)
                    sp.wait_ge(x2_ready, START + b * TT)
                    sp.dma_start(x1[:], x1_dram[bass.ds(first, TT)].rearrange("t p n -> p t n")).then_inc(x1_in, 16)
                    sp.wait_ge(pv_done, START + b * GROUPS * PAIRS)
                    sp.dma_start(wqh[:].bitcast(F32), wq_dram[0]).then_inc(wq_in, 16)
                    sp.dma_start(wql[:].bitcast(F32), wq_dram[1]).then_inc(wq_in, 16)
                    sp.wait_ge(raw_ready, START + b * TILES + TT)
                    sp.dma_start(wd[:], wd_dram).then_inc(wd_in, 16)
                    sp.dma_start(yt[:], io["yT"][bass.ds(b, 1)].rearrange("o (c p) n -> p (o c) n", p=P)).then_inc(y_in, 16)
                    for g in range(GROUPS):
                        sp.wait_ge(packl_ready, START + b * 2 * GROUPS + 2 * g + 2)
                        for i in range(GROUP):
                            of = slice(HD * i, HD * (i + 1))
                            for r, kp, qp in ((0, packh, packh), (1, packl, packh), (2, packh, packl)):
                                to = slice(HD * r, HD * (r + 1))
                                sp.dma_start(kT[to, i].bitcast(F32), kp[of, 0:CTX].bitcast(F32)).then_inc(heads_in[i], 16)
                                sp.dma_start(qT[to, i].bitcast(F32), qp[of, CTX:].bitcast(F32)).then_inc(heads_in[i], 16)
                    for t in range(TT):
                        sp.wait_ge(x2_ready, START + b * TT + t + 1)
                        sp.dma_start(x2_dram[bass.ds(b * TT + t, 1)].rearrange("o p n -> p (o n)"), x2[:, t % 2]).then_inc(x2_out[t % 2], 16)
                for i in range(2):
                    sp.wait_ge(x2_out[i], START + 16 * BATCH * TT // 2)

            @block.scalar
            def _(act):
                with act.Fori(0, BATCH) as b:
                    def square(n):
                        act.wait_ge(raw_ready, START + b * TILES + n + 1)
                        act.wait_ge(ss_ready, START + b * TILES + max(n - 1, 0))
                        nc.scalar.activation(sq[:, n % 2], raw[:, n % 4], ACT.Square).then_inc(sq_ready, 1)

                    def deviation(n):
                        act.wait_ge(ss_ready, START + b * TILES + n + 1)
                        act.wait_ge(unit_ready, START + b * TILES + max(n - 1, 0))
                        nc.scalar.activation(sd[:, n % 2], ss[:, n % 2], ACT.Sqrt, bias=eps6[:, 0:1], scale=1.0 / HD).then_inc(sd_ready, 1)

                    def heads(n):
                        if n < TILES:
                            square(n)
                        if 0 <= n - 1 < TILES:
                            deviation(n - 1)

                    act.wait_ge(x1_in, START + b * 16 + 16)
                    for t in range(TT + 1):
                        if t < TT:
                            slot, use = bank["x1T", t]
                            act.wait_ge(full[slot], START + b * USES + use)
                            nc.scalar.copy(x1h[:, :, P * t:P * (t + 1)], wide[slot][:, 0].rearrange("p (c n) -> p c n", n=P)).then_inc(x1h_ready, 1)
                        if t > 0:
                            heads(t - 1)
                    act.wait_ge(y_in, START + b * 16 + 16)
                    nc.scalar.copy(yh[:], yt[:]).then_inc(yh_ready, 1)
                    nc.scalar.copy(yd[:, :, LAST:P], yt[:, :, MAIN:CTX]).then_inc(yd_ready, 1)
                    for n in range(TT, TILES + 1):
                        heads(n)
                    for g in range(GROUPS):
                        for i in range(GROUP):
                            act.wait_ge(heads_in[i], START + (b * GROUPS + g) * HEAD_DMAS)
                        for kind, lo, n in (("kT", 0, CTX), ("qT", CTX, SEQ)):
                            slot, use = bank[kind, g]
                            act.wait_ge(full[slot], START + b * USES + use)
                            nc.scalar.copy(packh[:, lo:lo + n], wide[slot][:].rearrange("p a n -> p (a n)")[:, 0:n]).then_inc(packh_ready, 1)
                        for j in range(2):
                            slot, use = bank["shift", g, j]
                            act.wait_ge(full[slot], START + b * USES + use)
                            nc.scalar.copy(qT[ROWS:ROWS + 2, 2 * j:2 * j + 2], wide[slot][ROWS:ROWS + 2]).then_inc(shift_ready, 1)
                        for kk in range(PAIRS):
                            act.wait_ge(pv_done, START + (b * GROUPS * PAIRS + g * PAIRS + kk - 1 if g * PAIRS + kk else b * GROUPS * PAIRS))
                            for i in range(GROUP):
                                slot, use = bank["score", g, kk, i]
                                act.wait_ge(full[slot], START + b * USES + use)
                                nc.scalar.activation(p[:, kk % 2, i], wide[slot][:], ACT.Exp, scale=float(HD) ** -0.5).then_inc(exp_ready, 1)
                        if g == 0:
                            act.wait_ge(x2_ready, START + b * TT)
                        act.wait_ge(ct_ready, START + b * GROUPS + g + 1)
                        nc.scalar.copy(cth[:, g], ct[:, g % 2]).then_inc(ch_ready, 1)

            @block.gpsimd
            def _(pool):
                with pool.Fori(0, BATCH) as b:
                    pool.sem_clear(pchain)
                    c = Chain(pool, pchain)

                    def weigh(n):
                        k = 0 if n < TT else 2 if n == TILES - 1 else 1
                        rw, kw, to = (x.rearrange("p (h d) -> p h d", d=HD) for x in (raw[:, n % 4], kn[:, n % 2], qk[:, n]))
                        pool.wait_ge(unit_ready, START + b * TILES + n + 1)
                        c(nc.gpsimd.tensor_tensor(kw, rw, nw[:, k].unsqueeze(1).broadcast_to([P, HEADS, HD]), ALU.mult))
                        c.wait()
                        nc.gpsimd.tensor_tensor(to, kw, nb[:, k].unsqueeze(1).broadcast_to([P, HEADS, HD]), ALU.add).then_inc(kn_ready, 1)

                    pool.wait_ge(packl_ready, START + b * 2 * GROUPS)
                    for n in range(TILES):
                        weigh(n)
                    pool.wait_ge(x1l_ready, START + b * TT + TT)
                    nc.gpsimd.tensor_tensor(x1[:], x1[:], bo[:].unsqueeze(1).broadcast_to([P, TT, DM]), ALU.add).then_inc(x1_biased, 1)
                    for g in range(GROUPS):
                        pool.wait_ge(ch_ready, START + b * GROUPS + g + 1)
                        nc.gpsimd.tensor_tensor(ctl[:, g], ct[:, g % 2], cth[:, g].bitcast(F32), ALU.subtract).then_inc(cl_ready, 1)
                    for t in range(TT):
                        pool.wait_ge(ve_ready, START + b * TT + t + 1)
                        nc.gpsimd.tensor_tensor(rstd[:, t % 2:t % 2 + 1], ve[:, t % 2:t % 2 + 1], half[:], ALU.pow).then_inc(rstd_ready, 1)
                    c.wait()

            @block.vector
            def _(dve):
                with dve.Fori(0, BATCH) as b:
                    dve.sem_clear(dchain)
                    c = Chain(dve, dchain)

                    def take(n):
                        slot, use = bank["head", n]
                        dve.wait_ge(full[slot], START + b * USES + use)
                        if n < TT:
                            dve.wait_ge(kn_ready, START + b * TILES + max(n - 3, 0))
                            nc.vector.tensor_tensor(raw[:, n % 4], wide[slot][:, 0], bq[:], ALU.add).then_inc(raw_ready, 1)
                            return
                        k = n - TT
                        bias = bkv7 if k == KT_N - 1 else bkv
                        dve.wait_ge(kn_ready, START + b * TILES + n - 3)
                        nc.vector.tensor_tensor(raw[:, n % 4], wide[slot][:, 0], bias[:, 0:HT], ALU.add).then_inc(raw_ready, 1)
                        nc.vector.tensor_tensor(v[:, k], wide[slot][:, 1], bias[:, HT:2 * HT], ALU.add).then_inc(v_ready, 1)
                        if k == KT_N - 1:
                            dve.wait_ge(v_ready, START + b * KT_N + KT_N)
                            nc.vector.tensor_scalar(vd[:], v[:, k], dca_row[:, 0:1], None, ALU.mult).then_inc(vd_ready, 1)

                    def square_sum(n):
                        dve.wait_ge(sq_ready, START + b * TILES + n + 1)
                        dve.wait_ge(sd_ready, START + b * TILES + max(n - 1, 0))
                        nc.vector.tensor_reduce(ss[:, n % 2], sq[:, n % 2].rearrange("p (h d) -> p h d", d=HD), AX.X, ALU.add).then_inc(ss_ready, 1)

                    def unit(n):
                        dve.wait_ge(sd_ready, START + b * TILES + n + 1)
                        c(nc.vector.reciprocal(sd[:, n % 2], sd[:, n % 2]))
                        c.wait()
                        rw = raw[:, n % 4].rearrange("p (h d) -> p h d", d=HD)
                        nc.vector.tensor_tensor(rw, rw, sd[:, n % 2].unsqueeze(2).broadcast_to([P, HEADS, HD]), ALU.mult).then_inc(unit_ready, 1)

                    def heads(n):
                        if n < TILES:
                            take(n)
                        if 0 <= n - 1 < TILES:
                            square_sum(n - 1)
                        if 0 <= n - 2 < TILES:
                            unit(n - 2)

                    for t in range(TT + 1):
                        if t < TT:
                            slot, use = bank["x1T", t]
                            dve.wait_ge(x1h_ready, START + b * TT + t + 1)
                            nc.vector.tensor_tensor(x1l[:, :, P * t:P * (t + 1)], wide[slot][:, 0].rearrange("p (c n) -> p c n", n=P),
                                                    x1h[:, :, P * t:P * (t + 1)].bitcast(F32), ALU.subtract).then_inc(x1l_ready, 1)
                        if t > 0:
                            heads(t - 1)
                    dve.wait_ge(yh_ready, START + b + 1)
                    nc.vector.tensor_tensor(yl[:], yt[:], yh[:].bitcast(F32), ALU.subtract).then_inc(yl_ready, 1)
                    for n in range(TT, TILES + 2):
                        heads(n)
                    for g in range(GROUPS):
                        for a, (kind, lo, n) in enumerate((("kT", 0, CTX), ("qT", CTX, SEQ))):
                            slot, use = bank[kind, g]
                            dve.wait_ge(packh_ready, START + b * 2 * GROUPS + 2 * g + a + 1)
                            nc.vector.tensor_tensor(packl[:, lo:lo + n], wide[slot][:].rearrange("p a n -> p (a n)")[:, 0:n],
                                                    packh[:, lo:lo + n].bitcast(F32), ALU.subtract).then_inc(packl_ready, 1)
                        for i in range(GROUP):
                            for t in range(TT):
                                slot, use = bank["max", g, i, t]
                                at = ROWS + 2 * ((GROUP * g + i) * TT + t)
                                dve.wait_ge(full[slot], START + b * USES + use)
                                flat = wide[slot][:].rearrange("p a n -> p (a n)")
                                c(nc.vector.tensor_reduce(mx[:, at + 1:at + 2], flat[:, MAIN:CTX], AX.X, ALU.max, negate=True))
                                nc.vector.tensor_reduce(mx[:, at:at + 1], flat[:, 0:MAIN], AX.X, ALU.max, negate=True).then_inc(mx_ready, 1)
                        dve.wait_ge(pv_done, START + b * GROUPS * PAIRS + PAIRS * (g + 1))
                        dve.wait_ge(cl_ready, START + b * GROUPS + max(g - 1, 0))
                        if g == 0:
                            for x in x2_out:
                                dve.wait_ge(x, START + b * 16 * TT // 2)
                        for k, kind in enumerate(("main", "dca")):
                            c(nc.vector.reciprocal(rec[:, k], acc["sum_" + kind][:]))
                            c.wait()
                            c(nc.vector.tensor_tensor(rec[:, k], acc["ctx_" + kind][:], rec[:, k], ALU.mult))
                            c.wait()
                        nc.vector.tensor_tensor(ct[:, g % 2], rec[:, 0], rec[:, 1], ALU.add).then_inc(ct_ready, 1)
                    dve.wait_ge(ct_ready, START + b * GROUPS + GROUPS)
                    for t in range(TT):
                        slot, use = bank["wo", t]
                        if t == 0:
                            dve.wait_ge(x1_biased, START + b + 1)
                        dve.wait_ge(full[slot], START + b * USES + use)
                        s = ct[:, t % 2]
                        nc.vector.tensor_tensor(s, wide[slot][:, 0], x1[:, t], ALU.add).then_inc(wo_taken, 1)
                        dve.wait_ge(wo_taken, START + b * TT + t + 1)
                        c(nc.vector.bn_stats(st6[:], s))
                        c.wait()
                        c(nc.vector.bn_aggr(mv[:, t % 2], st6[:]))
                        c.wait()
                        nc.vector.tensor_scalar(ve[:, t % 2:t % 2 + 1], mv[:, t % 2, 1:2], 1e-5, None, ALU.add).then_inc(ve_ready, 1)
                        dve.wait_ge(rstd_ready, START + b * TT + t + 1)
                        dve.wait_ge(x2_out[t % 2], START + (b * (TT // 2) + t // 2) * 16)
                        nc.vector.tensor_scalar(x2[:, t % 2], s, mv[:, t % 2, 0:1], rstd[:, t % 2:t % 2 + 1],
                                                ALU.subtract, ALU.mult).then_inc(x2_ready, 1)
                    c.wait()

            @block.tensor
            def _(pe):
                def product(out, pairs, first=True):
                    for i, (l, r) in enumerate(pairs):
                        last = nc.tensor.matmul(out, l, r, start=(first and i == 0), stop=(i == len(pairs) - 1))
                    return last

                def taken(kind, *at):
                    if kind == "x1T":
                        return x1l_ready, at[0] + 1, TT
                    if kind == "head":
                        return (raw_ready, at[0] + 1, TILES) if at[0] < TT else (v_ready, at[0] - TT + 1, KT_N)
                    if kind in ("kT", "qT"):
                        return packl_ready, 2 * at[0] + 1 + (kind == "qT"), 2 * GROUPS
                    if kind == "max":
                        return mx_ready, (GROUP * at[0] + at[1]) * TT + at[2] + 1, HEADS * TT
                    if kind == "shift":
                        return shift_ready, 2 * at[0] + at[1] + 1, 2 * GROUPS
                    if kind == "score":
                        return exp_ready, (at[0] * PAIRS + at[1]) * GROUP + at[2] + 1, EXPS
                    return wo_taken, at[0] + 1, TT

                with pe.Fori(0, BATCH) as b:
                    def claim(*group):
                        at = groups.index(group)
                        what, value, per_batch = taken(*groups[at - 2])
                        pe.wait_ge(what, START + (b * per_batch + (value if at >= 2 else 0)))
                        return bank[group][0]

                    def x1_turned(t):
                        slot = claim("x1T", t)
                        for k in range(DC):
                            last = nc.tensor.transpose(wide[slot][:, 0, P * k:P * (k + 1)], x1[:, t, P * k:P * (k + 1)], ident[:])
                        last.then_inc(full[slot], 1)

                    def queries(t):
                        slot = claim("head", t)
                        pe.wait_ge(x1l_ready, START + b * TT + t + 1)
                        tok = slice(P * t, P * (t + 1))
                        product(wide[slot][:, 0], [(x[:, k, tok], w[:, k]) for k in range(DC)
                                                   for x, w in ((x1h, wqh), (x1l, wqh), (x1h, wql))]).then_inc(full[slot], 1)

                    pe.wait_ge(x1_in, START + b * 16 + 16)
                    for t in range(TT + 1):
                        if t < TT:
                            x1_turned(t)
                        if t == 1:
                            pe.wait_ge(wq_in, START + b * 32 + 32)
                        if t > 0:
                            queries(t - 1)
                    pe.wait_ge(yh_ready, START + b + 1)
                    pe.wait_ge(yl_ready, START + b + 1)
                    for k in range(KT_N):
                        slot = claim("head", TT + k)
                        keys = LAST if k == KT_N - 1 else P
                        tok = slice(P * k, P * k + keys)
                        if k == KT_N - 1:
                            pe.wait_ge(yd_ready, START + b + 1)
                            pe.wait_ge(wd_in, START + b * 16 + 16)
                        for half_ in range(2):
                            cols = slice(HT * half_, HT * (half_ + 1))
                            if k == KT_N - 1:
                                for cc in range(CC):
                                    nc.tensor.matmul(wide[slot][:, half_], yd[:, cc], wd[:, cc, cols], start=(cc == 0), stop=False)
                            last = product(wide[slot][0:keys, half_], [(x[:, cc, tok], w[:, cc, cols]) for cc in range(CC)
                                                                       for x, w in ((yh, wkvh), (yl, wkvh), (yh, wkvl))], k < KT_N - 1)
                        last.then_inc(full[slot], 1)

                    for g in range(GROUPS):
                        if g == 0:
                            pe.wait_ge(kn_ready, START + b * TILES + TILES)
                        for kind, first, n in (("kT", TT, KT_N), ("qT", 0, TT)):
                            slot = claim(kind, g)
                            for k in range(n):
                                last = nc.tensor.transpose(wide[slot][:, k // 4, P * (k % 4):P * (k % 4 + 1)],
                                                           qk[:, first + k, P * g:P * (g + 1)], ident[:])
                            last.then_inc(full[slot], 1)
                        for i in range(GROUP):
                            pe.wait_ge(heads_in[i], START + (b * GROUPS + g + 1) * HEAD_DMAS)
                            for t in range(TT):
                                slot = claim("max", g, i, t)
                                for a in range(2):
                                    last = nc.tensor.matmul(wide[slot][:, a], qT[0:ROWS, i, P * t:P * (t + 1)], kT[0:ROWS, i, 512 * a:512 * (a + 1)],
                                                            start=True, stop=True)
                                last.then_inc(full[slot], 1)
                        for j in range(2):
                            slot = claim("shift", g, j)
                            pe.wait_ge(mx_ready, START + b * HEADS * TT + (GROUP * g + 2 * j + 2) * TT)
                            for i in range(2):
                                for t in range(TT):
                                    at = 2 * ((GROUP * g + 2 * j + i) * TT + t)
                                    last = nc.tensor.transpose(wide[slot][0:ROWS + 2, i, P * t:P * (t + 1)], mx[:, at:at + ROWS + 2], ident[:])
                            last.then_inc(full[slot], 1)

                        def scores(kk):
                            for i in range(GROUP):
                                slot = claim("score", g, kk, i)
                                if kk == 0:
                                    pe.wait_ge(shift_ready, START + b * 2 * GROUPS + 2 * g + i // 2 + 1)
                                for a in range(2):
                                    k = 2 * kk + a
                                    last = nc.tensor.matmul(wide[slot][:, a], kT[:, i, P * k:P * (k + 1)], qT[:, i], start=True, stop=True)
                                last.then_inc(full[slot], 1)

                        def values(kk):
                            pe.wait_ge(exp_ready, START + b * EXPS + (g * PAIRS + kk + 1) * GROUP)
                            if kk == 0:
                                pe.wait_ge(ct_ready, START + b * GROUPS + g)
                            for a in range(2):
                                k = 2 * kk + a
                                rows = LAST if k == KT_N - 1 else P
                                work = [("ctx_main", rows, lambda i: v[0:rows, k, HD * (GROUP * g + i):HD * (GROUP * g + i + 1)], k == 0, k == KT_N - 1),
                                        ("sum_main", rows, lambda i: ones[0:rows], k == 0, k == KT_N - 1)]
                                if k == KT_N - 1:
                                    work += [("ctx_dca", P, lambda i: vd[:, HD * (GROUP * g + i):HD * (GROUP * g + i + 1)], True, True),
                                             ("sum_dca", P, lambda i: ones_dca[:], True, True)]
                                for name, m, left, start, stop in work:
                                    for i in range(GROUP):
                                        last = nc.tensor.matmul(acc[name][HD * i:HD * (i + 1)], left(i), p[0:m, kk % 2, i, a], start=start, stop=stop,
                                                                tile_position=(0, HD * i))
                            last.then_inc(pv_done, 1)

                        if g == 0:
                            pe.wait_ge(vd_ready, START + b + 1)
                        for kk in range(PAIRS):
                            scores(kk)
                            if kk:
                                values(kk - 1)
                        values(PAIRS - 1)
                    for t in range(TT):
                        slot = claim("wo", t)
                        pe.wait_ge(cl_ready, START + b * GROUPS + GROUPS)
                        product(wide[slot][:, 0], [(x[:, k, P * t:P * (t + 1)], w[:, k]) for k in range(GROUPS)
                                                   for x, w in ((cth, woh), (ctl, woh), (cth, wol))]).then_inc(full[slot], 1)


FF = 2048
KEEP = 204
FC = FF // P
KEY_BITS = 31
AIM = 200
START_SIGMAS = 1.2831
DENSITY = 358.7
STEP_GAINS = (0.96, 0.78, 0.7, 0.52, 0.35)
COUNTS = len(STEP_GAINS) + 1


def sparse_ffn(nc, io, x2_dram, out):
    HALF = FF // 2
    with ExitStack() as ctx:
        def sb(name, shape, dt=F32):
            return ctx.enter_context(nc.sbuf_tensor("sf_" + name, shape, dt))

        def sem(name):
            return ctx.enter_context(nc.semaphore("f_" + name))

        counters = []

        def counter(name):
            counters.append(sem(name))
            return counters[-1]

        wide = [ctx.enter_context(nc.psum_tensor(f"f_wide{i}", [P, 2, 512], F32)) for i in range(4)]

        w_in_t = sb("w_in_t", [P, DC, FF], F32R)
        w_out_t = sb("w_out_t", [P, FC, DM], F32R)
        b_syn, b_out, gamma, beta = sb("b_syn", [P, FF]), sb("b_out", [P, DM]), sb("gamma", [P, DM]), sb("beta", [P, DM])
        ident, ones = sb("ident", [P, P]), sb("ones", [P, P])
        bits = sb("bits", [P, KEY_BITS], U32)
        places = sb("places", [P, 9])
        parts, total = sb("parts", [P, 2, 64]), sb("total", [P, 2])
        scale, limit, low_limit = sb("scale", [P, 2]), sb("limit", [P, 2]), sb("low_limit", [P, 2])
        square_sums = sb("square_sums", [P, 5])
        spread, bias_spread = sb("spread", [P, 1]), sb("bias_spread", [P, 1])
        first_guess = sb("first_guess", [P, 1])
        gains = sb("gains", [P, COUNTS - 1])
        half, aim = sb("half", [P, 2]), sb("aim", [P, 1])
        xin, xres, x2b = sb("xin", [P, TT, DM]), sb("xres", [P, TT, DM]), sb("x2b", [P, 2, DM])
        z = sb("z", [P, TT, FF])
        guess = sb("guess", [P, 2, 1])
        above = sb("above", [P, 2, 1])
        miss, far, step = sb("miss", [P, 1]), sb("far", [P, 1]), sb("step", [P, 1])
        top = sb("top", [P, 2, 9])
        place, chosen = sb("place", [P, 2, 1]), sb("chosen", [P, 2, 9])
        cut = sb("cut", [P, 2, 1])
        kept, wrong = sb("kept", [P, 2]), sb("wrong", [P, 2])
        any_wrong = sb("any_wrong", [P, 1], U32)
        key, trial = sb("key", [P, 1], U32), sb("trial", [P, 1], U32)
        count = sb("count", [P, 1])
        enough = sb("enough", [P, 1], U32)
        st6, mv, ve, rstd = sb("st6", [P, 2, 6]), sb("mv", [P, 2, 2]), sb("ve", [P, 2]), sb("rstd", [P, 2])
        with ExitStack() as region:
            w_raw = region.enter_context(nc.sbuf_tensor("sf_w_raw", [P, 4 * FF], F32))
            sign = region.enter_context(nc.sbuf_tensor("sf_sign", [P, 2, FF], F32))
        x2h, x2l = sb("x2h", [P, 2, DC, P], F32R), sb("x2l", [P, 2, DC, P], F32R)
        hid = sb("hid", [P, 2, FF])
        hTh, hTl = sb("hTh", [P, FC, P], F32R), sb("hTl", [P, FC, P], F32R)
        s, u, y = sb("s", [P, 2, DM]), sb("u", [P, 2, DM]), sb("y", [P, 2, DM])
        unused = sb("unused", [P, 2, FF], mybir.dt.bfloat16)

        const_in, w_in = sem("const_in"), [sem(f"w{i}_in") for i in range(2)]
        ones_ready, part_ready, total_ready, signs_ready = sem("ones_ready"), sem("part_ready"), sem("total_ready"), sem("signs_ready")
        squares_ready, sums_ready, spread_ready, root_ready = sem("squares_ready"), sem("sums_ready"), sem("spread_ready"), sem("root_ready")
        xin_in = [counter(f"xin{h}_in") for h in range(2)]
        xres_in = [counter(f"xres{h}_in") for h in range(2)]
        y_out = [counter(f"y{h}_out") for h in range(2)]
        (xT_full, x2h_ready, x2l_ready, z_full, z_ready, counted, stepped, tried, kept_ready, wrong_ready, wrong_sum,
         hid_ready, hT_full, hh_ready, hl_ready, out_full, s_ready, x2_biased, ve_ready, rstd_ready, residual_used,
         y_ready) = (counter(n) for n in (
             "xT_full", "x2h_ready", "x2l_ready", "z_full", "z_ready", "counted", "stepped", "tried", "kept_ready", "wrong_ready",
             "wrong_sum", "hid_ready", "hT_full", "hh_ready", "hl_ready", "out_full", "s_ready", "x2_biased", "ve_ready",
             "rstd_ready", "residual_used", "y_ready"))
        dchain, pchain = sem("dchain"), sem("pchain")

        with nc.Block() as block:
            @block.sync
            def _(sp):
                for c in counters:
                    sp.sem_inc(c, START)
                sp.dma_start(w_raw[:].rearrange("p (c n) -> p c n", c=DC), io["w_synT"].rearrange("(c p) n -> p c n", p=P)).then_inc(w_in[0], 16)
                for t_, n in ((b_syn, "b_syn"), (b_out, "b_out"), (gamma, "gamma"), (beta, "beta"), (places, "places"), (bits, "bits")):
                    sp.dma_start(t_[:], io[n].partition_broadcast(P)).then_inc(const_in, 16)
                sp.dma_start(ident[:], io["ident"]).then_inc(const_in, 16)
                sp.wait_ge(signs_ready, 4)
                sp.dma_start(w_raw[:].rearrange("p (c n) -> p c n", c=FC), io["w_outT"].rearrange("(c p) n -> p c n", p=P)).then_inc(w_in[1], 16)
                sp.wait_ge(const_in, 16 * 7)

            @block.gpsimd
            def _(pool):
                pool.memset(half[:], -0.5)
                pool.memset(aim[:], float(FF - 2 * AIM))
                pool.memset(ones[:], 1.0).then_inc(ones_ready, 1)

            @block.scalar
            def _(act):
                for a in range(4):
                    act.wait_ge(signs_ready, a + 1)
                    nc.scalar.activation(z[:, a], w_in_t[:, a].bitcast(F32), ACT.Square, accum_out=square_sums[:, a:a + 1]).then_inc(squares_ready, 1)
                act.wait_ge(const_in, 16 * 7)
                act.wait_ge(squares_ready, 4)
                nc.scalar.activation(z[:, 0], b_syn[:], ACT.Square, accum_out=square_sums[:, 4:5]).then_inc(squares_ready, 1)
                act.wait_ge(spread_ready, 1)
                nc.scalar.activation(spread[:], spread[:], ACT.Sqrt).then_inc(root_ready, 1)

            @block.tensor
            def _(pe):
                pe.wait_ge(ones_ready, 1)
                for k in range(2):
                    pe.wait_ge(part_ready, k + 1)
                    nc.tensor.matmul(wide[k][:, 0, 0:1], ones[:], total[:, k:k + 1], start=True, stop=True).then_inc(total_ready, 1)
                pe.wait_ge(squares_ready, 4)
                nc.tensor.matmul(wide[2][:, 0, 0:4], ones[:], square_sums[:, 0:4], start=True, stop=True).then_inc(sums_ready, 1)

            @block.vector
            def _(dve):
                c = Chain(dve, dchain)
                for k, dst in enumerate((w_in_t[:].rearrange("p c n -> p (c n)"), w_out_t[:].rearrange("p c n -> p (c n)"))):
                    dve.wait_ge(w_in[k], 16)
                    c(nc.vector.tensor_reduce(parts[:, k], w_raw[:].rearrange("p (a n) -> p a n", a=64), AX.X, ALU.add, apply_absolute_value=True))
                    c.wait()
                    nc.vector.tensor_reduce(total[:, k:k + 1], parts[:, k], AX.X, ALU.add).then_inc(part_ready, 1)
                    dve.wait_ge(total_ready, k + 1)
                    c(nc.vector.tensor_scalar(scale[:, k:k + 1], wide[k][:, 0, 0:1], 1.0 / (FF * DM), None, ALU.mult))
                    c.wait()
                    c(nc.vector.tensor_scalar(limit[:, k:k + 1], scale[:, k:k + 1], 1e-8, 0.5, ALU.add, ALU.mult))
                    c.wait()
                    c(nc.vector.tensor_scalar(low_limit[:, k:k + 1], limit[:, k:k + 1], -1.0, None, ALU.mult))
                    c(nc.vector.tensor_scalar(scale[:, k:k + 1], scale[:, k:k + 1], -1.0, None, ALU.mult))
                    for a in range(4):
                        part = slice(FF * a, FF * (a + 1))
                        c.wait()
                        if a >= 2:
                            dve.wait_ge(signs_ready, 4 * k + a - 1)
                        c(nc.vector.tensor_scalar(sign[:, a % 2], w_raw[:, part], limit[:, k:k + 1], None, ALU.is_gt))
                        c.wait()
                        nc.vector.scalar_tensor_tensor(dst[:, part], w_raw[:, part], low_limit[:, k:k + 1], sign[:, a % 2], ALU.is_lt, ALU.subtract).then_inc(signs_ready, 1)
                dve.wait_ge(sums_ready, 1)
                c(nc.vector.tensor_reduce(spread[:], wide[2][:, 0, 0:4], AX.X, ALU.add))
                c.wait()
                dve.wait_ge(squares_ready, 5)
                for factor in (scale[:, 0:1], scale[:, 0:1]):
                    c(nc.vector.tensor_scalar(spread[:], spread[:], factor, None, ALU.mult))
                    c.wait()
                c(nc.vector.tensor_tensor(spread[:], spread[:], square_sums[:, 4:5], ALU.add))
                c.wait()
                nc.vector.tensor_scalar(spread[:], spread[:], 1.0 / FF, None, ALU.mult).then_inc(spread_ready, 1)
                dve.wait_ge(root_ready, 1)
                c(nc.vector.tensor_scalar(first_guess[:], spread[:], -START_SIGMAS, None, ALU.mult))
                for i, gain in enumerate(STEP_GAINS):
                    c(nc.vector.tensor_scalar(gains[:, i:i + 1], spread[:], -gain / (2 * DENSITY), None, ALU.mult))
                c.wait()
                dve.wait_ge(signs_ready, 8)
                dve.sem_clear(dchain)

        def after(b, t, per_tile):
            return START + b * (TT * per_tile) + t * per_tile

        def over_pairs(eng, first, pair, chain=None):
            first()
            with eng.Fori(0, BATCH - 1) as b:
                pair(b, 0, True)
                pair(b, 2, True)
            pair(BATCH - 1, 0, True)
            pair(BATCH - 1, 2, False)

        with nc.Block() as block:
            @block.sync
            def _(sp):
                def load(to, first, t, done):
                    sp.dma_start(to[:, t:t + 2], x2_dram[bass.ds(first, 2)].rearrange("t p n -> p t n")).then_inc(done[t // 2], 16)

                def pair(b, t, more):
                    first = b * TT + t if isinstance(b, int) else sp.snap(b * TT + t)
                    ahead = b * TT + t + 2 if isinstance(b, int) else sp.snap(b * TT + t + 2)
                    if more:
                        sp.wait_ge(xT_full, START + b * 2 + t // 2)
                        load(xin, ahead, (t + 2) % TT, xin_in)
                    sp.wait_ge(residual_used, START + b * 2 + t // 2)
                    load(xres, first, t, xres_in)
                    sp.wait_ge(y_ready, START + b * 2 + t // 2 + 1)
                    sp.dma_start(out[bass.ds(b, 1), t * P:(t + 2) * P].rearrange("o (t p) n -> p (o t) n", p=P), y[:]).then_inc(y_out[t // 2], 16)

                over_pairs(sp, lambda: load(xin, 0, 0, xin_in), pair)
                for i in range(2):
                    sp.wait_ge(y_out[i], START + 16 * BATCH)

            @block.scalar
            def _(act):
                def split(b, t):
                    act.wait_ge(xT_full, START + b * 2 + t // 2 + 1)
                    act.wait_ge(z_full, after(b, t, 2))
                    nc.scalar.copy(x2h[:], wide[0][:].rearrange("p t (c n) -> p t c n", n=P)).then_inc(x2h_ready, 1)

                def rounds(b, t, some):
                    for r in some:
                        for i in range(2):
                            if r == 0:
                                act.wait_ge(z_ready, after(b, t + i + 1, 2))
                                act.wait_ge(kept_ready, after(b, t, 1))
                                bias = first_guess[:]
                            else:
                                act.wait_ge(stepped, START + b * 20 + t * 5 + 2 * (r - 1) + i + 1)
                                bias = guess[:, i]
                            nc.scalar.activation(unused[:, i], z[:, t % 4 + i], ACT.Sign, bias=bias, accum_out=above[:, i]).then_inc(counted, 1)

                def turned(b, n):
                    act.wait_ge(out_full, after(b, n, 1))
                    for a in range(2):
                        act.wait_ge(hT_full, START + b * 8 + 2 * n + a + 1)
                        nc.scalar.copy(hTh[:, 8 * a:8 * a + 8], wide[3 - 3 * a][:].rearrange("p a (c n) -> p (a c) n", n=P)).then_inc(hh_ready, 1)

                def first():
                    split(0, 0)
                    rounds(0, 0, range(COUNTS))

                def pair(b, t, more):
                    if more:
                        split(b, t + 2)
                    for i in range(2):
                        act.wait_ge(tried, after(b, t + i + 1, 1))
                        nc.scalar.activation(unused[:, i], hid[:, i], ACT.Sign, accum_out=kept[:, i:i + 1]).then_inc(kept_ready, 1)
                    if more:
                        rounds(b, t + 2, [0])
                    turned(b, t)
                    if more:
                        rounds(b, t + 2, [1, 2])
                    turned(b, t + 1)
                    if more:
                        rounds(b, t + 2, range(3, COUNTS))

                over_pairs(act, first, pair)

            @block.gpsimd
            def _(pool):
                def steps(c, b, t, some):
                    for r in some:
                        for i in range(2):
                            pool.wait_ge(counted, START + b * 24 + t * 6 + 2 * r + i + 1)
                            c(nc.gpsimd.tensor_tensor(miss[:], above[:, i], aim[:], ALU.add))
                            c.wait()
                            c(nc.gpsimd.tensor_tensor(far[:], miss[:], miss[:], ALU.mult))
                            c.wait()
                            c(nc.gpsimd.tensor_scalar(far[:], far[:], 64.5, None, ALU.is_gt))
                            c.wait()
                            c(nc.gpsimd.tensor_tensor(step[:], far[:], miss[:], ALU.mult))
                            c.wait()
                            c(nc.gpsimd.tensor_tensor(step[:], step[:], gains[:, r:r + 1], ALU.mult))
                            c.wait()
                            c(nc.gpsimd.tensor_tensor(guess[:, i], step[:], first_guess[:] if r == 0 else guess[:, i], ALU.add))
                            c.wait()
                            pool.sem_inc(stepped, 1)

                def pair(b, t, more):
                    c = Chain(pool, pchain)
                    if more:
                        steps(c, b, t + 2, range(3))
                    pool.wait_ge(s_ready, after(b, t, 1))
                    pool.wait_ge(xres_in[t // 2], START + b * 16 + 16)
                    nc.gpsimd.tensor_tensor(x2b[:], xres[:, t:t + 2], b_out[:].unsqueeze(1).broadcast_to([P, 2, DM]), ALU.add).then_inc(x2_biased, 1)
                    if more:
                        steps(c, b, t + 2, range(3, COUNTS - 1))
                    for n in range(2):
                        pool.wait_ge(ve_ready, START + b * 4 + t + n + 1)
                        nc.gpsimd.tensor_tensor(rstd[:], ve[:], half[:], ALU.pow).then_inc(rstd_ready, 1)
                    pool.sem_clear(pchain)

                def first():
                    steps(Chain(pool, pchain), 0, 0, range(COUNTS - 1))
                    pool.sem_clear(pchain)

                over_pairs(pool, first, pair)

            @block.vector
            def _(dve):
                def into_hidden(b, t, i):
                    if i == 0:
                        dve.wait_ge(x2h_ready, START + b * 2 + t // 2 + 1)
                        nc.vector.tensor_tensor(x2l[:], wide[0][:].rearrange("p t (c n) -> p t c n", n=P), x2h[:].bitcast(F32), ALU.subtract).then_inc(x2l_ready, 1)
                    for a in range(2):
                        cols = slice(HALF * a, HALF * (a + 1))
                        dve.wait_ge(z_full, START + b * 8 + 2 * (t + i) + a + 1)
                        nc.vector.scalar_tensor_tensor(z[:, t % 4 + i, cols], wide[1 + a][:].rearrange("p a n -> p (a n)"), scale[:, 0:1],
                                                       b_syn[:, cols], ALU.mult, ALU.add).then_inc(z_ready, 1)

                def search_bits(t):
                    for i in range(2):
                        nc.vector.memset(key[:], 0).then_inc(dchain, 1)
                        dve.wait_ge(dchain, 1)
                        dve.sem_clear(dchain)
                        with dve.Fori(0, KEY_BITS) as k:
                            nc.vector.tensor_tensor(trial[:], key[:], bits[:, bass.ds(k, 1)], ALU.bitwise_or).then_inc(dchain, 1)
                            dve.wait_ge(dchain, 1)
                            nc.vector.tensor_scalar(hid[:, i], z[:, t % 4 + i], trial[:].bitcast(F32), None, ALU.is_ge, ALU.add, accum_out=count[:]).then_inc(dchain, 1)
                            dve.wait_ge(dchain, 2)
                            nc.vector.tensor_scalar(enough[:], count[:], KEEP - 0.5, None, ALU.is_ge).then_inc(dchain, 1)
                            dve.wait_ge(dchain, 3)
                            nc.vector.copy_predicated(key[:], enough[:], trial[:]).then_inc(dchain, 1)
                            dve.wait_ge(dchain, 4)
                            dve.sem_clear(dchain)
                        zt = z[:, t % 4 + i]
                        nc.vector.scalar_tensor_tensor(hid[:, i], zt, key[:].bitcast(F32), zt, ALU.is_ge, ALU.mult).then_inc(dchain, 1)
                        dve.wait_ge(dchain, 1)
                        dve.sem_clear(dchain)

                def keep_largest(c, b, t, i):
                    zt = z[:, t % 4 + i]
                    dve.wait_ge(counted, START + b * 24 + t * 6 + 10 + i + 1)
                    c(nc.vector.tensor_scalar(top[:, i, 8:9], guess[:, i], -1.0, None, ALU.mult))
                    c(nc.vector.tensor_scalar(place[:, i], above[:, i], -0.5, KEEP - 1 - FF / 2, ALU.mult, ALU.add))
                    c.wait()
                    c(nc.vector.scalar_tensor_tensor(hid[:, i], zt, top[:, i, 8:9], zt, ALU.is_lt, ALU.mult))
                    c.wait()
                    c(nc.vector.max(top[:, i, 0:8], hid[:, i]))
                    c.wait()
                    c(nc.vector.scalar_tensor_tensor(chosen[:, i], places[:], place[:, i], top[:, i], ALU.is_equal, ALU.mult))
                    c.wait()
                    c(nc.vector.tensor_reduce(cut[:, i], chosen[:, i], AX.X, ALU.add))
                    c.wait()
                    c(nc.vector.scalar_tensor_tensor(hid[:, i], zt, cut[:, i], zt, ALU.is_ge, ALU.mult))
                    c.wait()
                    dve.sem_inc(tried, 1)

                def check_kept(c, b, t):
                    dve.wait_ge(kept_ready, after(b, t + 2, 1))
                    c(nc.vector.tensor_scalar(wrong[:], kept[:], float(KEEP), None, ALU.not_equal))
                    c.wait()
                    dve.sem_inc(wrong_ready, 1)
                    dve.wait_ge(wrong_sum, START + b * 2 + t // 2 + 1)
                    c(nc.vector.tensor_copy(any_wrong[:], wide[1][:, 1, 0:1]))
                    c.wait()
                    dve.sem_clear(dchain)
                    c.n = 0
                    rows = dve.value_load(any_wrong[0:1, 0:1])
                    with dve.If(rows > 0):
                        search_bits(t)
                    dve.sem_inc(hid_ready, 1)

                def layernorm(c, nth, src, to):
                    for i in range(2):
                        c(nc.vector.bn_stats(st6[:, i], src[:, i]))
                    c.wait()
                    for i in range(2):
                        c(nc.vector.bn_aggr(mv[:, i], st6[:, i]))
                    c.wait()
                    nc.vector.tensor_scalar(ve[:], mv[:, :, 1], 1e-5, None, ALU.add).then_inc(ve_ready, 1)
                    dve.wait_ge(rstd_ready, nth)
                    for i in range(2):
                        c(nc.vector.tensor_scalar(to[:, i], src[:, i], mv[:, i, 0:1], rstd[:, i:i + 1], ALU.subtract, ALU.mult))
                    c.wait()

                def first():
                    for i in range(2):
                        into_hidden(0, 0, i)

                def finish(c, b, t):
                    for i in range(2):
                        for a in range(2):
                            dve.wait_ge(hh_ready, START + b * 8 + 2 * (t + i) + a + 1)
                            nc.vector.tensor_tensor(hTl[:, 8 * a:8 * a + 8], wide[3 - 3 * a][:].rearrange("p a (c n) -> p (a c) n", n=P),
                                                    hTh[:, 8 * a:8 * a + 8].bitcast(F32), ALU.subtract).then_inc(hl_ready, 1)
                    dve.wait_ge(x2_biased, START + b * 2 + t // 2 + 1)
                    for i in range(2):
                        dve.wait_ge(out_full, after(b, t + i + 1, 1))
                        nc.vector.scalar_tensor_tensor(s[:, i], wide[1 + i][:, 0], scale[:, 1:2], x2b[:, i], ALU.mult, ALU.add).then_inc(s_ready, 1)
                    dve.wait_ge(s_ready, after(b, t + 2, 1))
                    layernorm(c, START + b * 4 + t + 1, s, u)
                    c(nc.vector.tensor_tensor(u[:], u[:], gamma[:].unsqueeze(1).broadcast_to([P, 2, DM]), ALU.mult))
                    c.wait()
                    c(nc.vector.tensor_tensor(u[:], u[:], beta[:].unsqueeze(1).broadcast_to([P, 2, DM]), ALU.add))
                    c.wait()
                    nc.vector.tensor_tensor(u[:], u[:], xres[:, t:t + 2], ALU.add).then_inc(residual_used, 1)
                    dve.wait_ge(residual_used, START + b * 2 + t // 2 + 1)
                    dve.wait_ge(y_out[1 - t // 2], START + b * 16 + (16 if t else 0))
                    layernorm(c, START + b * 4 + t + 2, u, y)
                    dve.sem_inc(y_ready, 1)

                def pair(b, t, more):
                    c = Chain(dve, dchain)
                    for i in range(2):
                        keep_largest(c, b, t, i)
                        if more:
                            into_hidden(b, t + 2, i)
                    check_kept(c, b, t)
                    finish(c, b, t)
                    dve.sem_clear(dchain)

                over_pairs(dve, first, pair)

            @block.tensor
            def _(pe):
                def into_hidden(b, t, first=False):
                    pe.wait_ge(xin_in[t // 2 % 2], (START + b * 16 + 16) if t < 4 else (START + b * 16 + 32))
                    if not first:
                        pe.wait_ge(hl_ready, START + b * 8 + 2 * (t - 2))
                    for i in range(2):
                        for k in range(DC):
                            last = nc.tensor.transpose(wide[0][:, i, P * k:P * (k + 1)], xin[:, t % 4 + i, P * k:P * (k + 1)], ident[:])
                    last.then_inc(xT_full, 1)
                    pe.wait_ge(x2l_ready, START + b * 2 + t // 2 + 1)
                    for i in range(2):
                        for a in range(2):
                            if i:
                                pe.wait_ge(z_ready, START + b * 8 + 2 * t + a + 1)
                            elif not first:
                                pe.wait_ge(z_ready, after(b, t, 2))
                                pe.wait_ge(s_ready, after(b, t - 2, 1))
                            for h in range(2):
                                cols = slice(HALF * a + 512 * h, HALF * a + 512 * (h + 1))
                                for k in range(DC):
                                    for x in (x2h, x2l):
                                        last = nc.tensor.matmul(wide[1 + a][:, h], x[:, i, k], w_in_t[:, k, cols],
                                                                start=(k == 0 and x is x2h), stop=(k == DC - 1 and x is x2l))
                            last.then_inc(z_full, 1)

                def pair(b, t, more):
                    if more:
                        into_hidden(b, t + 2)
                    pe.wait_ge(z_ready, after(b, t + (4 if more else 2), 2))
                    pe.wait_ge(wrong_ready, START + b * 2 + t // 2 + 1)
                    nc.tensor.matmul(wide[1][:, 1, 0:1], ones[:], wrong[:, 0:1], start=True, stop=False)
                    nc.tensor.matmul(wide[1][:, 1, 0:1], ones[:], wrong[:, 1:2], start=False, stop=True).then_inc(wrong_sum, 1)
                    for i in range(2):
                        for a in range(2):
                            pe.wait_ge(hid_ready, START + b * 2 + t // 2 + 1)
                            pe.wait_ge(hl_ready, after(b, t + i, 2))
                            for k in range(8):
                                last = nc.tensor.transpose(wide[3 - 3 * a][:, k // 4, P * (k % 4):P * (k % 4 + 1)], hid[:, i, P * (8 * a + k):P * (8 * a + k + 1)], ident[:])
                            last.then_inc(hT_full, 1)
                        pe.wait_ge(hl_ready, after(b, t + i + 1, 2))
                        for k in range(FC):
                            for x in (hTh, hTl):
                                last = nc.tensor.matmul(wide[1 + i][:, 0], x[:, k], w_out_t[:, k], start=(k == 0 and x is hTh), stop=(k == FC - 1 and x is hTl))
                        last.then_inc(out_full, 1)

                over_pairs(pe, lambda: into_hidden(0, 0, first=True), pair)


def decoder_layer(nc, io, out):
    def scratch(name, shape):
        return nc.dram_tensor(name, shape, F32, kind="Internal").ap()

    tiles = BATCH * TT
    x1_dram, x2_dram = scratch("x1_scratch", [tiles, P, DM]), scratch("x2_scratch", [tiles, P, DM])
    wq_dram, wd_dram = scratch("wq_scratch", [2, P, DC, HEADS * HD]), scratch("wd_scratch", [P, CC, 2 * HEADS * HD])
    self_attention(nc, io, x1_dram)
    cross_attention(nc, io, x1_dram, x2_dram, wq_dram, wd_dram)
    sparse_ffn(nc, io, x2_dram, out)


def rotary_tables(np):
    f32 = np.float32
    inv_freq = (f32(1.0) / f32(10000.0) ** (np.arange(0, HD, 2, dtype=f32) / f32(HD))).astype(f32)
    angle = np.arange(SEQ, dtype=f32)[:, None] * inv_freq[None, :]
    angle = np.concatenate([angle, angle], axis=-1).astype(np.float64)
    sign = np.where(np.arange(HD) < HD // 2, -1.0, 1.0)
    return [by_sixteenths(np, t.astype(f32), 0) for t in (np.cos(angle), np.sin(angle) * sign)]


def by_sixteenths(np, a, axis):
    shape = a.shape
    a = a.reshape(shape[:axis] + (SEQ // 16, 4, 4) + shape[axis + 1:])
    a = np.moveaxis(a, axis, axis + 2)
    return np.ascontiguousarray(a.reshape(shape))


def kernel(**inputs):
    import numpy as np
    import concourse.bacc as bacc
    from concourse.bass_utils import run_bass_kernel_spmd

    given = {k: np.asarray(v) for k, v in inputs.items()}
    attn, cross, ffn = ({k[len(p):]: v for k, v in given.items() if k.startswith(p)} for p in ("L0_attn_", "L0_xattn_", "L0_ffn_"))
    x, ctx = given["x"], given["ctx_1024"]
    HT = HEADS * HD
    cos, sin = rotary_tables(np)
    wkv = np.concatenate([cross["Wk"], cross["Wv"]], axis=1).reshape(CDM, HEADS, 2, HD)
    bkv = np.concatenate([cross["bk"], cross["bv"]]).reshape(HEADS, 2, HD)
    is_dca = np.arange(CTX) >= MAIN
    arrays = {
        "x": x,
        "xT": by_sixteenths(np, x.transpose(0, 2, 1), 2),
        "w1T": np.concatenate([attn["Wq"], attn["Wk"], attn["Wv"]], axis=0).T,
        "b1": np.concatenate([attn["bq"], attn["bk"], attn["bv"]]),
        "woT": attn["Wo"].T,
        "a_bo": attn["bo"],
        "randT": attn["rand_matrix"].T,
        "cos": cos,
        "sin": sin,
        "ident": np.eye(P, dtype=np.float32),
        "yT": ctx.transpose(0, 2, 1),
        "c_wkv": np.concatenate([wkv[:, :, 0].reshape(CDM, HT), wkv[:, :, 1].reshape(CDM, HT)], axis=1),
        "c_bkv": np.concatenate([bkv[:, 0].reshape(HT), bkv[:, 1].reshape(HT)]),
        "c_wq": cross["Wq"],
        "c_bq": cross["bq"],
        "c_wd": cross["Wkv_dca"],
        "c_bd": cross["bkv_dca"],
        "c_wo": cross["Wo"],
        "c_bo": cross["bo"],
        "nw": np.stack([cross["qn_w"], cross["kn_w"], cross["kn_dca_w"]]),
        "nb": np.stack([cross["qn_b"], cross["kn_b"], cross["kn_dca_b"]]),
        "key_rows": np.stack([~is_dca, is_dca]).astype(np.float32),
        "dca_row": is_dca[-P:].astype(np.float32)[:, None],
        "w_synT": ffn["W_syn"].T,
        "w_outT": ffn["W_out"].T,
        "b_syn": ffn["b_syn"],
        "b_out": ffn["b_out"],
        "gamma": ffn["gamma"],
        "beta": ffn["beta"],
        "places": np.append(np.arange(8), -1).astype(np.float32),
        "bits": np.uint32(1) << np.arange(KEY_BITS - 1, -1, -1, dtype=np.uint32),
    }
    nc = bacc.Bacc("TRN2", target_bir_lowering=False, num_devices=1)
    arrays = {"in_" + k: np.ascontiguousarray(a) for k, a in arrays.items()}
    io = {k[3:]: nc.dram_tensor(k, a.shape, mybir.dt.from_np(a.dtype), kind="ExternalInput").ap() for k, a in arrays.items()}
    out = nc.dram_tensor("out", [BATCH, SEQ, DM], F32, kind="ExternalOutput").ap()
    decoder_layer(nc, io, out)
    result = run_bass_kernel_spmd(nc, [arrays], core_ids=[0])
    return result.results[0]["out"]
```

```python
import concourse.bass as bass
from concourse import mybir
from contextlib import ExitStack

F32 = mybir.dt.float32
F32R = mybir.dt.float32r
U32 = mybir.dt.uint32
ALU = mybir.AluOpType
ACT = mybir.ActivationFunctionType
AX = mybir.AxisListType

P = 128
BATCH, SEQ, DM = 4, 512, 512
TT = SEQ // P
DC = DM // P
HEADS, KV_HEADS, HD = 16, 8, 32
TURN = 6.283185
START = 1
ROUND_MAGIC = 12582912.0


class Chain:

    def __init__(self, eng, sem):
        self.eng, self.sem, self.n = eng, sem, 0

    def __call__(self, ins):
        self.n += 1
        return ins.then_inc(self.sem, 1)

    def wait(self):
        self.eng.wait_ge(self.sem, self.n)


def bank_plan(groups, slots):
    assert len(groups) % slots == 0
    return {g: (i % slots, i // slots + 1) for i, g in enumerate(groups)}


def start_counters(nc, counters):
    with nc.Block() as block:
        @block.sync
        def _(sp):
            for s in counters:
                sp.sem_inc(s, START)


def self_attention(nc, io, x1_dram):
    QKV = DM + 2 * KV_HEADS * HD
    QK_HEADS = HEADS + KV_HEADS
    FE = HD // 2
    SLOTS, USES, AHEAD = 8, 3, 2
    bank = {g: (i, 1) for i, g in enumerate((n, t) for t in range(AHEAD) for n in ("q", "kv"))}
    groups = [(n, t) for t in range(AHEAD, TT) for n in ("q", "kv")]
    groups += [(n, t) for t in range(TT) for n in ("rot0", "rot1", "proj")]
    groups += [("next", i) for i in range(2 * AHEAD)] + [("wo", t) for t in range(TT)]
    assert len(groups) == SLOTS * USES
    bank.update({g: (i % SLOTS, i // SLOTS + (2 if i % SLOTS < 2 * AHEAD else 1)) for i, g in enumerate(groups)})
    POOL_H = 7

    with ExitStack() as ctx:
        def sb(name, shape, dt=F32):
            return ctx.enter_context(nc.sbuf_tensor("sa_" + name, shape, dt))

        def sem(name):
            return ctx.enter_context(nc.semaphore("a_" + name))

        counters = []

        def counter(name):
            counters.append(sem(name))
            return counters[-1]

        ps = [ctx.enter_context(nc.psum_tensor(f"a_ps{i}", [P, 512], F32)) for i in range(SLOTS)]
        full = [counter(f"bank{i}_full") for i in range(SLOTS)]
        free = [counter(f"bank{i}_free") for i in range(SLOTS)]

        w1h, w1l = sb("w1h", [P, DC, QKV], F32R), sb("w1l", [P, DC, QKV], F32R)
        woh, wol = sb("woh", [P, DC, DM], F32R), sb("wol", [P, DC, DM], F32R)
        b1 = sb("b1", [P, QKV])
        bo = sb("bo", [P, DM])
        cosb, sinb = sb("cosb", [P, TT, HD]), sb("sinb", [P, TT, HD])
        ident = sb("ident", [P, P])
        rmat = sb("rmat", [P, 4 * FE])
        xt = sb("xt", [P, DC, SEQ])
        xth, xtl = sb("xth", [P, DC, SEQ], F32R), sb("xtl", [P, DC, SEQ], F32R)
        xres = sb("xres", [P, TT, DM])
        qkv = sb("qkv", [P, 2, QKV])
        vs = sb("vs", [P, TT, KV_HEADS * HD])
        turn = sb("turn", [P, 2, QK_HEADS * HD])
        qkr = sb("qkr", [P, TT, QK_HEADS * HD])
        sq = sb("sq", [P, QK_HEADS * HD])
        ssum = sb("ssum", [P, TT * QK_HEADS])
        rn = sb("rn", [P, TT * QK_HEADS])
        qkT = sb("qkT", [P, 6, P])
        feat = sb("feat", [P, 2, QK_HEADS * HD])
        whole = sb("whole", [P, QK_HEADS * HD])
        sc = sb("sc", [P, 2, QK_HEADS * HD])
        prod = sb("prod", [P, HEADS, KV_HEADS, HD])
        prod_v = sb("prod_v", [P, HEADS, HD, KV_HEADS])
        w1 = prod[:].rearrange("p h g d -> p (h g d)").rearrange("p (c n) -> p c n", c=DC)
        wo = xt[:]
        amat = sb("amat", [P, HEADS, KV_HEADS])
        o = sb("o", [P, DM])
        oT = sb("oT", [P, TT, DM])
        oth, otl = sb("oth", [P, TT, DM], F32R), sb("otl", [P, TT, DM], F32R)
        s = sb("s", [P, 2, DM])
        st6 = sb("st6", [P, 6])
        mv = sb("mv", [P, 2, 2])
        ve = sb("ve", [P, 2])
        rstd = sb("rstd", [P, 2])
        half = sb("half", [P, 1])
        x1 = sb("x1", [P, 2, DM])

        w_in, const_in, xt_in, xres_in = sem("w_in"), sem("const_in"), counter("xt_in"), counter("xres_in")
        rzero = sem("rzero")
        wh_ready, w_ready = sem("wh_ready"), sem("w_ready")
        xh_ready, xl_ready = counter("xh_ready"), counter("xl_ready")
        qkv_ready, v_ready, turn_ready = counter("qkv_ready"), counter("v_ready"), counter("turn_ready")
        qkr_ready, sq_ready, sqsum_ready, norm_ready = counter("qkr_ready"), counter("sq_ready"), counter("sqsum_ready"), counter("norm_ready")
        qkT_ready, proj_done = counter("qkT_ready"), counter("proj_done")
        arg_ready, sc_ready = counter("arg_ready"), counter("sc_ready")
        prod_ready, prod_v_ready, a_ready, o_ready = counter("prod_ready"), counter("prod_v_ready"), counter("a_ready"), counter("o_ready")
        oT_ready, oh_ready, ol_ready = counter("oT_ready"), counter("oh_ready"), counter("ol_ready")
        x_biased, ve_ready, rstd_ready = counter("x_biased"), counter("ve_ready"), counter("rstd_ready")
        x1_ready, x1_out = counter("x1_ready"), [counter(f"x1_out{i}") for i in range(2)]
        dchain = sem("dchain")

        def over_batches(eng, batch):
            with eng.Fori(0, BATCH - 1) as b:
                batch(b, False)
            batch(BATCH - 1, True)

        start_counters(nc, counters)
        with nc.Block() as block:

            @block.sync
            def _(sp):
                sp.dma_start(w1, io["w1T"].rearrange("(c p) n -> p c n", p=P)).then_inc(w_in, 16)
                sp.dma_start(wo, io["woT"].rearrange("(c p) n -> p c n", p=P)).then_inc(w_in, 16)
                sp.dma_start(b1[:], io["b1"].partition_broadcast(P)).then_inc(const_in, 16)
                sp.dma_start(bo[:], io["a_bo"].partition_broadcast(P)).then_inc(const_in, 16)
                sp.dma_start(cosb[:], io["cos"].rearrange("(t p) d -> p t d", p=P)).then_inc(const_in, 16)
                sp.dma_start(sinb[:], io["sin"].rearrange("(t p) d -> p t d", p=P)).then_inc(const_in, 16)
                sp.dma_start(ident[:], io["ident"]).then_inc(const_in, 16)
                sp.wait_ge(rzero, 1)
                for j in range(4):
                    sp.dma_start(rmat[HD * j:HD * (j + 1), FE * j:FE * (j + 1)], io["randT"]).then_inc(const_in, 16)
                sp.wait_ge(w_ready, 1)
                sp.dma_start(xt[:], io["xT"][0:1].rearrange("o (c p) n -> p (o c) n", p=P)).then_inc(xt_in, 16)

                def batch(b, final):
                    if not final:
                        following = sp.snap(b + 1)
                        sp.wait_ge(xh_ready, START + b + 1)
                        sp.wait_ge(xl_ready, START + b + 1)
                        sp.dma_start(xt[:], io["xT"][bass.ds(following, 1)].rearrange("o (c p) n -> p (o c) n", p=P)).then_inc(xt_in, 16)
                    sp.wait_ge(x1_ready, START + b * TT)
                    sp.dma_start(xres[:], io["x"][bass.ds(b, 1)].rearrange("o (t p) n -> p (o t) n", p=P)).then_inc(xres_in, 16)
                    for t in range(TT):
                        sp.wait_ge(x1_ready, START + b * TT + t + 1)
                        sp.dma_start(x1_dram[bass.ds(b * TT + t, 1)].rearrange("o p n -> p (o n)"), x1[:, t % 2]).then_inc(x1_out[t % 2], 16)
                over_batches(sp, batch)
                for i in range(2):
                    sp.wait_ge(x1_out[i], START + 16 * BATCH * TT // 2)

            @block.scalar
            def _(act):
                act.wait_ge(w_in, 32)
                nc.scalar.copy(w1h[:], w1)
                nc.scalar.copy(woh[:], wo).then_inc(wh_ready, 1)
                act.wait_ge(xt_in, START + 16)
                nc.scalar.copy(xth[:], xt[:]).then_inc(xh_ready, 1)

                def batch(b, final):
                    for t in range(TT):
                        act.wait_ge(qkr_ready, START + b * TT + t + 1)
                        if t:
                            act.wait_ge(sqsum_ready, START + b * TT + t)
                        else:
                            act.wait_ge(sqsum_ready, START + b * TT)
                        nc.scalar.activation(sq[:], qkr[:, t], ACT.Square).then_inc(sq_ready, 1)
                    act.wait_ge(sqsum_ready, START + b * TT + TT)
                    nc.scalar.activation(rn[:], ssum[:], ACT.Sqrt).then_inc(norm_ready, 1)

                    def turned(t):
                        for i in range(2):
                            slot, use = bank[f"rot{i}", t]
                            act.wait_ge(full[slot], START + b * USES + use)
                            if i == 0:
                                act.wait_ge(proj_done, START + b * TT + t)
                            nc.scalar.copy(qkT[:, 3 * i:3 * i + 3], ps[slot][:, 0:3 * P].rearrange("p (c n) -> p c n", n=P)).then_inc(free[slot], 1)
                        act.wait_ge(free[slot], START + b * USES + use)
                        act.sem_inc(qkT_ready, 1)

                    def features(t):
                        act.wait_ge(a_ready, START + b * TT + max(t - 1, 0))
                        act.wait_ge(arg_ready, START + b * TT + t + 1)
                        nc.scalar.activation(sc[:, t % 2], feat[:, t % 2], ACT.Sin, scale=TURN).then_inc(sc_ready, 1)

                    turned(0)
                    turned(1)
                    features(0)
                    turned(2)
                    features(1)
                    turned(3)
                    if not final:
                        act.wait_ge(xt_in, START + b * 16 + 32)
                        act.wait_ge(v_ready, START + b * TT + TT)
                        nc.scalar.copy(xth[:], xt[:]).then_inc(xh_ready, 1)
                    for t in range(TT):
                        if t + 2 < TT:
                            features(t + 2)
                        if t == 0:
                            act.wait_ge(x1_ready, START + b * TT)
                        act.wait_ge(oT_ready, START + b * TT + t + 1)
                        nc.scalar.copy(oth[:, t], oT[:, t]).then_inc(oh_ready, 1)

                over_batches(act, batch)

            @block.gpsimd
            def _(pool):
                pool.memset(rmat[:], 0.0).then_inc(rzero, 1)
                pool.memset(half[:], -0.5)
                pool.wait_ge(const_in, 16 * 9)
                pool.wait_ge(w_ready, 1)
                def batch(b, final):
                    def lower_part(t):
                        pool.wait_ge(oh_ready, START + b * TT + t + 1)
                        nc.gpsimd.tensor_tensor(otl[:, t], oT[:, t], oth[:, t].bitcast(F32), ALU.subtract).then_inc(ol_ready, 1)

                    for t in range(TT):
                        pool.wait_ge(qkv_ready, START + b * TT + t + 1)
                        pool.wait_ge(qkr_ready, START + b * TT + max(t - 1, 0))
                        x3 = qkv[:, t % 2, 0:QK_HEADS * HD].rearrange("p (h d) -> p h d", d=HD)
                        o3 = turn[:, t % 2].rearrange("p (h d) -> p h d", d=HD)
                        sn = sinb[:, t].unsqueeze(1).broadcast_to([P, QK_HEADS, HD])
                        nc.gpsimd.tensor_tensor(o3[:, :, 0:FE], x3[:, :, FE:HD], sn[:, :, 0:FE], ALU.mult)
                        nc.gpsimd.tensor_tensor(o3[:, :, FE:HD], x3[:, :, 0:FE], sn[:, :, FE:HD], ALU.mult).then_inc(turn_ready, 1)

                    def feature_products(t):
                        f = sc[:, t % 2].rearrange("p (h d) -> p h d", d=HD)
                        pool.wait_ge(sc_ready, START + b * TT + t + 1)
                        pool.wait_ge(a_ready, START + b * TT + t)
                        nc.gpsimd.tensor_tensor(
                            prod[:, 0:POOL_H],
                            f[:, 0:POOL_H].unsqueeze(2).broadcast_to([P, POOL_H, KV_HEADS, HD]),
                            f[:, HEADS:].unsqueeze(1).broadcast_to([P, POOL_H, KV_HEADS, HD]), ALU.mult).then_inc(prod_ready, 1)

                    def value_products(t):
                        pool.wait_ge(a_ready, START + b * TT + t + 1)
                        pool.wait_ge(o_ready, START + b * TT + t)
                        nc.gpsimd.tensor_tensor(
                            prod_v[:, 0:POOL_H],
                            amat[:, 0:POOL_H].unsqueeze(2).broadcast_to([P, POOL_H, HD, KV_HEADS]),
                            vs[:, t].rearrange("p (g d) -> p d g", d=HD).unsqueeze(1).broadcast_to([P, POOL_H, HD, KV_HEADS]),
                            ALU.mult).then_inc(prod_v_ready, 1)

                    pool.wait_ge(xres_in, START + b * 16 + 16)
                    nc.gpsimd.tensor_tensor(xres[:], xres[:], bo[:].unsqueeze(1).broadcast_to([P, TT, DM]), ALU.add).then_inc(x_biased, 1)
                    feature_products(0)
                    for t in range(TT):
                        value_products(t)
                        if t + 1 < TT:
                            feature_products(t + 1)
                        if t >= 2:
                            lower_part(t - 2)
                    lower_part(TT - 2)
                    lower_part(TT - 1)
                    for t in range(TT):
                        pool.wait_ge(ve_ready, START + b * TT + t + 1)
                        nc.gpsimd.tensor_tensor(rstd[:, t % 2:t % 2 + 1], ve[:, t % 2:t % 2 + 1], half[:], ALU.pow).then_inc(rstd_ready, 1)

                over_batches(pool, batch)

            NH = HEADS - POOL_H

            def feature_products(dve, c, b, t):
                f = sc[:, t % 2].rearrange("p (h d) -> p h d", d=HD)
                dve.wait_ge(sc_ready, START + b * TT + t + 1)
                c.wait()
                c(nc.vector.tensor_tensor(
                    prod[:, POOL_H:],
                    f[:, POOL_H:HEADS].unsqueeze(2).broadcast_to([P, NH, KV_HEADS, HD]),
                    f[:, HEADS:].unsqueeze(1).broadcast_to([P, NH, KV_HEADS, HD]), ALU.mult))

            def feature_sums(dve, c, b, t):
                c.wait()
                dve.wait_ge(prod_ready, START + b * TT + t + 1)
                c(nc.vector.tensor_reduce(amat[:], prod[:], AX.X, ALU.add))
                c.wait()
                dve.sem_inc(a_ready, 1)

            def value_products(dve, c, b, t):
                c(nc.vector.tensor_tensor(
                    prod_v[:, POOL_H:],
                    amat[:, POOL_H:].unsqueeze(2).broadcast_to([P, NH, HD, KV_HEADS]),
                    vs[:, t].rearrange("p (g d) -> p d g", d=HD).unsqueeze(1).broadcast_to([P, NH, HD, KV_HEADS]), ALU.mult))

            def value_sums(dve, c, b, t):
                c.wait()
                dve.wait_ge(prod_v_ready, START + b * TT + t + 1)
                nc.vector.tensor_reduce(o[:].rearrange("p (h d) -> p h d", d=HD), prod_v[:], AX.X, ALU.add).then_inc(o_ready, 1)
                dve.wait_ge(o_ready, START + b * TT + t + 1)
                nc.vector.transpose(oT[:, t], o[:]).then_inc(oT_ready, 1)

            @block.vector
            def _(dve):
                dve.wait_ge(w_in, 32)
                dve.wait_ge(wh_ready, 1)
                nc.vector.tensor_tensor(w1l[:], w1, w1h[:].bitcast(F32), ALU.subtract)
                nc.vector.tensor_tensor(wol[:], wo, woh[:].bitcast(F32), ALU.subtract).then_inc(w_ready, 1)
                dve.wait_ge(const_in, 16 * 9)
                dve.wait_ge(xh_ready, START + 1)
                nc.vector.tensor_tensor(xtl[:], xt[:], xth[:].bitcast(F32), ALU.subtract).then_inc(xl_ready, 1)

                def batch(b, final):
                    dve.sem_clear(dchain)
                    c = Chain(dve, dchain)
                    for t in range(TT):
                        for n, lo in (("q", 0), ("kv", 512)):
                            slot, use = bank[n, t]
                            dve.wait_ge(full[slot], START + b * USES + use)
                            c(nc.vector.tensor_tensor(qkv[:, t % 2, lo:lo + 512], ps[slot][:], b1[:, lo:lo + 512], ALU.add))
                            c.wait()
                            dve.sem_inc(free[slot], 1)
                        dve.sem_inc(qkv_ready, 1)
                        c(nc.vector.tensor_scalar(vs[:, t], qkv[:, t % 2, QK_HEADS * HD:], 1.0 / 16, None, ALU.mult))
                        c(nc.vector.tensor_tensor(qkr[:, t].rearrange("p (h d) -> p h d", d=HD),
                                                  qkv[:, t % 2, 0:QK_HEADS * HD].rearrange("p (h d) -> p h d", d=HD),
                                                  cosb[:, t].unsqueeze(1).broadcast_to([P, QK_HEADS, HD]), ALU.mult))
                        c.wait()
                        dve.sem_inc(v_ready, 1)
                        dve.wait_ge(turn_ready, START + b * TT + t + 1)
                        nc.vector.tensor_tensor(qkr[:, t], qkr[:, t], turn[:, t % 2], ALU.add).then_inc(qkr_ready, 1)
                        dve.wait_ge(sq_ready, START + b * TT + t + 1)
                        nc.vector.tensor_reduce(ssum[:, t * QK_HEADS:(t + 1) * QK_HEADS], sq[:].rearrange("p (h d) -> p h d", d=HD),
                                                AX.X, ALU.add).then_inc(sqsum_ready, 1)
                    dve.wait_ge(norm_ready, START + b + 1)
                    c(nc.vector.tensor_scalar(rn[:], rn[:], 1e-6, None, ALU.max))
                    c.wait()
                    c(nc.vector.reciprocal(rn[:], rn[:]))
                    c.wait()
                    c(nc.vector.tensor_scalar(rn[:], rn[:], 0.15915494309189535, None, ALU.mult))

                    def feature_arguments(t):
                        slot, use = bank["proj", t]
                        f = feat[:, t % 2].rearrange("p (h d) -> p h d", d=HD)
                        dve.wait_ge(full[slot], START + b * USES + use)
                        if t >= 2:
                            dve.wait_ge(sc_ready, START + b * TT + t - 1)
                        c.wait()
                        c(nc.vector.tensor_tensor(f[:, :, 0:FE], ps[slot][:, 0:QK_HEADS * FE].rearrange("p (h d) -> p h d", d=FE),
                                                  rn[:, t * QK_HEADS:(t + 1) * QK_HEADS].unsqueeze(2).broadcast_to([P, QK_HEADS, FE]), ALU.mult))
                        c.wait()
                        dve.sem_inc(free[slot], 1)
                        c(nc.vector.tensor_scalar(f[:, :, FE:HD], f[:, :, 0:FE], 0.25, None, ALU.add))
                        c.wait()
                        c(nc.vector.tensor_scalar(whole[:], feat[:, t % 2], ROUND_MAGIC, ROUND_MAGIC, ALU.add, ALU.subtract))
                        c.wait()
                        nc.vector.tensor_tensor(feat[:, t % 2], feat[:, t % 2], whole[:], ALU.subtract).then_inc(arg_ready, 1)

                    feature_arguments(0)
                    feature_products(dve, c, b, 0)
                    feature_arguments(1)
                    for t in range(TT):
                        feature_sums(dve, c, b, t)
                        value_products(dve, c, b, t)
                        if t + 1 < TT:
                            feature_products(dve, c, b, t + 1)
                        if t == 0 and not final:
                            dve.wait_ge(xh_ready, START + b + 2)
                            nc.vector.tensor_tensor(xtl[:], xt[:], xth[:].bitcast(F32), ALU.subtract).then_inc(xl_ready, 1)
                        value_sums(dve, c, b, t)
                        if t + 2 < TT:
                            feature_arguments(t + 2)
                    for t in range(TT):
                        slot, use = bank["wo", t]
                        if t == 0:
                            dve.wait_ge(x_biased, START + b + 1)
                        dve.wait_ge(full[slot], START + b * USES + use)
                        c(nc.vector.tensor_tensor(s[:, t % 2], ps[slot][:], xres[:, t], ALU.add))
                        c.wait()
                        dve.sem_inc(free[slot], 1)
                        c(nc.vector.bn_stats(st6[:], s[:, t % 2]))
                        c.wait()
                        c(nc.vector.bn_aggr(mv[:, t % 2], st6[:]))
                        c.wait()
                        nc.vector.tensor_scalar(ve[:, t % 2:t % 2 + 1], mv[:, t % 2, 1:2], 1e-5, None, ALU.add).then_inc(ve_ready, 1)
                        dve.wait_ge(rstd_ready, START + b * TT + t + 1)
                        dve.wait_ge(x1_out[t % 2], START + (b * (TT // 2) + t // 2) * 16)
                        nc.vector.tensor_scalar(x1[:, t % 2], s[:, t % 2], mv[:, t % 2, 0:1], rstd[:, t % 2:t % 2 + 1],
                                                ALU.subtract, ALU.mult).then_inc(x1_ready, 1)
                    c.wait()

                over_batches(dve, batch)

            @block.tensor
            def _(pe):
                def product(slot, pairs):
                    for i, (l, r) in enumerate(pairs):
                        last = nc.tensor.matmul(ps[slot][:], l, r, start=(i == 0), stop=(i == len(pairs) - 1))
                    return last

                pe.wait_ge(const_in, 16 * 9)
                pe.wait_ge(w_ready, 1)
                def projections(b, tiles):
                    for t in tiles:
                        tok = slice(P * t, P * (t + 1))
                        for n, lo in (("q", 0), ("kv", 512)):
                            slot, use = bank[n, t]
                            pe.wait_ge(free[slot], START + b * USES + use - 1)
                            product(slot, [(x[:, k, tok], w[:, k, lo:lo + 512]) for k in range(DC)
                                           for x, w in ((xth, w1h), (xtl, w1h), (xth, w1l))]).then_inc(full[slot], 1)

                pe.wait_ge(xh_ready, START + 1)
                pe.wait_ge(xl_ready, START + 1)
                projections(0, range(AHEAD))

                def batch(b, final):
                    projections(b, range(AHEAD, TT))
                    for t in range(TT):
                        pe.wait_ge(qkr_ready, START + b * TT + t + 1)
                        for i in range(2):
                            slot, use = bank[f"rot{i}", t]
                            pe.wait_ge(free[slot], START + b * USES + use - 1)
                            for k in range(3):
                                last = nc.tensor.transpose(ps[slot][:, P * k:P * (k + 1)], qkr[:, t, P * (3 * i + k):P * (3 * i + k + 1)], ident[:])
                            last.then_inc(full[slot], 1)
                        slot, use = bank["proj", t]
                        pe.wait_ge(free[slot], START + b * USES + use - 1)
                        pe.wait_ge(qkT_ready, START + b * TT + t + 1)
                        for k in range(6):
                            last = nc.tensor.matmul(ps[slot][:, 4 * FE * k:4 * FE * (k + 1)], qkT[:, k], rmat[:], start=True, stop=True)
                        last.then_inc(full[slot], 1)
                        pe.wait_ge(full[slot], START + b * USES + use)
                        pe.sem_inc(proj_done, 1)
                    if not final:
                        pe.wait_ge(xh_ready, START + b + 2)
                        pe.wait_ge(xl_ready, START + b + 2)
                        projections(b + 1, range(AHEAD))
                    for t in range(TT):
                        slot, use = bank["wo", t]
                        pe.wait_ge(free[slot], START + b * USES + use - 1)
                        pe.wait_ge(ol_ready, START + b * TT + TT)
                        product(slot, [(x[:, k, P * t:P * (t + 1)], w[:, k]) for k in range(DC)
                                       for x, w in ((oth, woh), (otl, woh), (oth, wol))]).then_inc(full[slot], 1)

                over_batches(pe, batch)


CTX, CDM, DCA = 1024, 256, 16
KT_N = CTX // P
CC = CDM // P
MAIN = CTX - DCA
LAST = P - DCA
GROUP = 4
GROUPS = HEADS // GROUP
BOUND = 60.0
ROWS = 3 * HD


def cross_attention(nc, io, x1_dram, x2_dram, wq_dram, wd_dram, wkv_dram):
    HT = HEADS * HD
    TILES = TT + KT_N
    PAIRS = KT_N // 2
    Q_TURN = TT + 3

    def packed(g, kind, bounded):
        queries_first = bounded and g == 0
        return 2 * g + 1 + (kind == ("kT" if queries_first else "qT"))

    def pe_groups(bounded):
        order = []
        for t in range(TT + 1):
            order += [("x1T", t)] * (t < TT) + [("head", t - 1)] * (t > 0)
        if bounded:
            order += [("head", n) for n in range(TT, Q_TURN)] + [("qT", 0)]
            order += [("head", n) for n in range(Q_TURN, TILES)] + [("kT", 0)]
            for g in range(GROUPS):
                for kk in range(PAIRS):
                    order += [("score", g, kk, i) for i in (0, 1)]
                    order += [("qT", g + 1)] * (kk == 2 and g + 1 < GROUPS)
                    order += [("score", g, kk, i) for i in (2, 3)]
                    order += [("kT", g + 1)] * (kk == 0 and g + 1 < GROUPS)
        else:
            order += [("head", n) for n in range(TT, TILES)]
            for g in range(GROUPS):
                order += [("kT", g), ("qT", g)]
                order += [("max", g, i, t) for i in range(GROUP) for t in range(TT)]
                order += [("shift", g, j) for j in range(2)]
                order += [("score", g, kk, i) for kk in range(PAIRS) for i in range(GROUP)]
        return order + [("wo", t) for t in range(TT)]

    order_of = {bounded: pe_groups(bounded) for bounded in (False, True)}
    plan_of = {bounded: (bank_plan(order_of[bounded], 2), len(order_of[bounded]) // 2) for bounded in (False, True)}
    EXPS = GROUPS * PAIRS * GROUP

    with ExitStack() as ctx:
        def sem(name):
            return ctx.enter_context(nc.semaphore("c_" + name))

        counters = []

        def counter(name):
            counters.append(sem(name))
            return counters[-1]

        def sb_in(stack):
            return lambda name, shape, dt=F32: stack.enter_context(nc.sbuf_tensor("sc_" + name, shape, dt))

        sb = sb_in(ctx)
        wide = [ctx.enter_context(nc.psum_tensor(f"c_wide{i}", [P, 2, 512], F32)) for i in range(2)]
        acc = {n: ctx.enter_context(nc.psum_tensor("c_" + n, [P, 512], F32)) for n in ("ctx_main", "sum_main", "ctx_dca", "sum_dca")}
        full = [counter(f"wide{i}_full") for i in range(2)]

        qk = sb("qk", [P, TILES, HT])
        packh, packl = sb("packh", [P, CTX + SEQ], F32R), sb("packl", [P, CTX + SEQ], F32R)
        v = sb("v", [P, KT_N, HT])
        vd = sb("vd", [P, HT])
        with ExitStack() as region:
            wqh_early, wql_early = sb_in(region)("wqh_early", [P, DC, HT], F32R), sb_in(region)("wql_early", [P, DC, HT], F32R)
        kT = sb("kT", [P, GROUP, CTX], F32R)
        with ExitStack() as region:
            yt_early = sb_in(region)("yt_early", [P, CC, CTX])
        qT = sb("qT", [P, GROUP, SEQ], F32R)
        x1_early = qk[:, TT + 4:TT + 8]
        qT2 = sb("qT2", [ROWS, GROUP, SEQ], F32R)
        with ExitStack() as region:
            wkvh, wkvl = sb_in(region)("wkvh", [P, CC, 2 * HT], F32R), sb_in(region)("wkvl", [P, CC, 2 * HT], F32R)
        kT2 = sb("kT2", [P, GROUP, CTX], F32R)
        kTs, qTs = (kT2, kT), (qT2, qT)
        outs = sb("outs", [P, 2, SEQ])
        bound_parts, bound, unbounded = sb("bound_parts", [P, 2, 3, HD]), sb("bound", [P, 2, 4]), sb("unbounded", [P, 1], U32)
        woh, wol = sb("woh", [P, DC, DM], F32R), sb("wol", [P, DC, DM], F32R)
        x1 = sb("x1", [P, TT, DM])
        ct = sb("ct", [P, 2, SEQ])
        rec = sb("rec", [P, 2, SEQ])
        bq, bkv, bkv7, bo = sb("bq", [P, HT]), sb("bkv", [P, 2 * HT]), sb("bkv7", [P, 2 * HT]), sb("bo", [P, DM])
        nw, nb = sb("nw", [P, 3, HD]), sb("nb", [P, 3, HD])
        ident = sb("ident", [P, P])
        dca_row = sb("dca_row", [P, 1])
        ones, ones_dca = sb("ones", [P, HD]), sb("ones_dca", [P, HD])
        yd = sb("yd", [P, CC, P])
        eps6, halves = sb("eps6", [P, 1]), sb("halves", [P, 2])
        ss, sd = sb("ss", [P, 2, HEADS]), sb("sd", [P, 2, HEADS])
        mx = sb("mx", [P, ROWS + HEADS * TT * 2])
        st6, mv, ve, rstd = sb("st6", [P, 2, 6]), sb("mv", [P, 2, 2]), sb("ve", [P, 2]), sb("rstd", [P, 2])
        with ExitStack() as region:
            r = sb_in(region)
            x1h, x1l = r("x1h", [P, DC, SEQ], F32R), r("x1l", [P, DC, SEQ], F32R)
            wqh, wql = r("wqh", [P, DC, HT], F32R), r("wql", [P, DC, HT], F32R)
        with ExitStack() as region:
            r = sb_in(region)
            yh, yl = r("yh", [P, CC, CTX], F32R), r("yl", [P, CC, CTX], F32R)
            yt, wd = r("yt", [P, CC, CTX]), r("wd", [P, CC, 2 * HT])
        with ExitStack() as region:
            r = sb_in(region)
            wd_late = r("wd_late", [P, CC, 2 * HT])
            r("gap", [P, CC, 2 * HT])
            yh_late, yl_late = r("yh_late", [P, CC, CTX], F32R), r("yl_late", [P, CC, CTX], F32R)
        x1_from = {False: x1, True: x1_early}
        wq_of = {False: (wqh, wql), True: (wqh_early, wql_early)}
        y_of = {False: (yt, yh, yl, wd), True: (yt_early, yh_late, yl_late, wd_late)}
        p = sb("p", [P, 2, GROUP, 2, SEQ])
        with ExitStack() as region:
            r = sb_in(region)
            raw, sq, kn = r("raw", [P, 4, HT]), r("sq", [P, 2, HT]), r("kn", [P, 2, HT])
        cth, ctl = sb("cth", [P, GROUPS, SEQ], F32R), sb("ctl", [P, GROUPS, SEQ], F32R)
        x2 = rec

        wkv_in, outs_taken, sums_taken, xres_in = counter("wkv_in"), counter("outs_taken"), counter("sums_taken"), counter("xres_in")
        norms_ready, roots_ready = sem("norms_ready"), sem("roots_ready")
        const_in, w_ready = sem("const_in"), sem("w_ready")
        x1_in, wq_in, y_in, wd_in = counter("x1_in"), counter("wq_in"), counter("y_in"), counter("wd_in")
        x1h_ready, x1l_ready, yh_ready, yl_ready, yd_ready = counter("x1h_ready"), counter("x1l_ready"), counter("yh_ready"), counter("yl_ready"), counter("yd_ready")
        raw_ready, sq_ready, ss_ready, sd_ready, unit_ready, kn_ready = (counter(n) for n in ("raw_ready", "sq_ready", "ss_ready", "sd_ready", "unit_ready", "kn_ready"))
        vd_ready = counter("vd_ready")
        packh_ready, packl_ready = counter("packh_ready"), counter("packl_ready")
        heads_in = [counter(f"head{i}_in") for i in range(GROUP)]
        v_ready, wo_taken = counter("v_ready"), counter("wo_taken")
        mx_ready, shift_ready, exp_ready, pv_done = counter("mx_ready"), counter("shift_ready"), counter("exp_ready"), counter("pv_done")
        ct_ready, ch_ready, cl_ready = counter("ct_ready"), counter("ch_ready"), counter("cl_ready")
        x1_biased, ve_ready, rstd_ready, x2_ready = counter("x1_biased"), counter("ve_ready"), counter("rstd_ready"), counter("x2_ready")
        x2_out = [counter(f"x2_out{i}") for i in range(2)]
        HEAD_DMAS = 16 * 6
        dchain, pchain = sem("dchain"), sem("pchain")
        spill, split = sem("spill"), sem("split")
        stage = qk[:].rearrange("p a n -> p (a n)")
        W = {"wkv": (CC, 2 * HT), "wo": (DC, DM), "wq": (DC, HT), "wd": (CC, 2 * HT)}
        staged = {n: stage[:, 2048 * i:2048 * (i + 1)].rearrange("p (c n) -> p c n", c=W[n][0]) for i, n in enumerate(("wkv", "wo", "wq"))}
        staged["wd"] = v[:, 0:4].rearrange("p a n -> p (a n)").rearrange("p (c n) -> p c n", c=CC)

        with nc.Block() as block:
            @block.sync
            def _(sp):
                for s in counters:
                    sp.sem_inc(s, START)
                for n in W:
                    sp.dma_start(staged[n], io["c_" + n].rearrange("(c p) n -> p c n", p=P)).then_inc(const_in, 16)
                sp.dma_start(bq[:], io["c_bq"].partition_broadcast(P)).then_inc(const_in, 16)
                sp.dma_start(bkv[:], io["c_bkv"].partition_broadcast(P)).then_inc(const_in, 16)
                sp.dma_start(bkv7[0:LAST], io["c_bkv"].partition_broadcast(LAST)).then_inc(const_in, 16)
                sp.dma_start(bkv7[LAST:P], io["c_bd"].partition_broadcast(DCA)).then_inc(const_in, 16)
                sp.dma_start(bo[:], io["c_bo"].partition_broadcast(P)).then_inc(const_in, 16)
                for t_, src in ((nw, "nw"), (nb, "nb")):
                    for k in range(2):
                        sp.dma_start(t_[:, k], io[src][k].partition_broadcast(P)).then_inc(const_in, 16)
                    sp.dma_start(t_[0:LAST, 2], io[src][1].partition_broadcast(LAST)).then_inc(const_in, 16)
                    sp.dma_start(t_[LAST:P, 2], io[src][2].partition_broadcast(DCA)).then_inc(const_in, 16)
                sp.dma_start(ident[:], io["ident"]).then_inc(const_in, 16)
                sp.dma_start(dca_row[:], io["dca_row"]).then_inc(const_in, 16)
                sp.dma_start(rec[ROWS:ROWS + 2].rearrange("p a n -> p (a n)"), io["key_rows"]).then_inc(const_in, 16)
                sp.wait_ge(w_ready, 1)
                sp.dma_start(wd_dram, staged["wd"]).then_inc(spill, 16)
                sp.wait_ge(split, 2)
                sp.dma_start(wq_dram[0], wqh[:].bitcast(F32)).then_inc(spill, 16)
                sp.dma_start(wq_dram[1], wql[:].bitcast(F32)).then_inc(spill, 16)
                sp.dma_start(wkv_dram[0], wkvh[:].bitcast(F32)).then_inc(spill, 16)
                sp.dma_start(wkv_dram[1], wkvl[:].bitcast(F32)).then_inc(spill, 16)
                sp.wait_ge(spill, 80)

            @block.scalar
            def _(act):
                act.wait_ge(const_in, 16 * 20)
                for i in range(GROUP):
                    nc.scalar.copy(kT[ROWS:ROWS + 2, i], rec[ROWS:ROWS + 2].rearrange("p a n -> p (a n)"))
                act.wait_ge(w_ready, 1)
                nc.scalar.copy(wqh[:], staged["wq"])
                nc.scalar.copy(wkvh[:], staged["wkv"])
                nc.scalar.copy(woh[:], staged["wo"]).then_inc(split, 1)
                act.wait_ge(norms_ready, 1)
                nc.scalar.activation(bound[:, :, 1:3], bound[:, :, 1:3], ACT.Sqrt, scale=float(HD)).then_inc(roots_ready, 1)

            @block.gpsimd
            def _(pool):
                pool.memset(ones[:], 1.0)
                pool.memset(eps6[:], 1e-6)
                pool.memset(halves[:], -0.5)
                pool.memset(mx[:], 0.0)
                pool.memset(yd[:], 0.0)

            @block.vector
            def _(dve):
                dve.wait_ge(const_in, 16 * 20)
                c = Chain(dve, dchain)
                for k in range(2):
                    for a_, (x, y) in enumerate(((nw, nw), (nw, nb), (nb, nw))):
                        c(nc.vector.tensor_tensor(bound_parts[:, k, a_], x[:, 0], y[:, 1 + k], ALU.mult))
                c.wait()
                c(nc.vector.tensor_reduce(bound[:, :, 0:1], bound_parts[:, :, 0:1], AX.X, ALU.max, apply_absolute_value=True))
                for k in range(2):
                    c(nc.vector.tensor_tensor(bound_parts[:, k, 1:3], bound_parts[:, k, 1:3], bound_parts[:, k, 1:3], ALU.mult))
                c.wait()
                c(nc.vector.tensor_reduce(bound[:, :, 1:3], bound_parts[:, :, 1:3], AX.X, ALU.add))
                for k in range(2):
                    c(nc.vector.tensor_tensor(bound_parts[:, k, 0], nb[:, 0], nb[:, 1 + k], ALU.mult))
                c.wait()
                dve.sem_inc(norms_ready, 1)
                c(nc.vector.tensor_reduce(bound[:, :, 3:4], bound_parts[:, :, 0:1], AX.X, ALU.add, apply_absolute_value=True))
                c(nc.vector.tensor_scalar(bound[:, :, 0], bound[:, :, 0], float(HD), None, ALU.mult))
                c.wait()
                c(nc.vector.tensor_scalar(ones_dca[:], ident[:, 0:HD], 0.0, dca_row[:, 0:1], ALU.mult, ALU.add))
                for part, mean in ((staged["wq"], ss[:].rearrange("p a h -> p (a h)")), (staged["wkv"][:, :, 0:HT], ss[:].rearrange("p a h -> p (a h)")),
                                   (staged["wd"][:, :, 0:HT], ss[:].rearrange("p a h -> p (a h)")), (bq[:].unsqueeze(1), ss[:, 0]),
                                   (bkv[:, 0:HT].unsqueeze(1), ss[:, 0]), (bkv7[:, 0:HT].unsqueeze(1), ss[:, 0])):
                    n = part.shape[1]
                    step = min(n, 2)
                    for k in range(0, n, step):
                        w = part[:, k:k + step].rearrange("p c (h d) -> p c h d", d=HD)
                        m = mean.rearrange("p (c h) -> p c h", h=HEADS)
                        c.wait()
                        c(nc.vector.tensor_reduce(m, w, AX.X, ALU.add))
                        c.wait()
                        c(nc.vector.tensor_scalar(m, m, -1.0 / HD, None, ALU.mult))
                        c.wait()
                        c(nc.vector.tensor_tensor(w, w, m.unsqueeze(3).broadcast_to([P, step, HEADS, HD]), ALU.add))
                c.wait()
                dve.sem_inc(w_ready, 1)
                dve.wait_ge(split, 1)
                nc.vector.tensor_tensor(wql[:], staged["wq"], wqh[:].bitcast(F32), ALU.subtract)
                nc.vector.tensor_tensor(wkvl[:], staged["wkv"], wkvh[:].bitcast(F32), ALU.subtract)
                nc.vector.tensor_tensor(wol[:], staged["wo"], woh[:].bitcast(F32), ALU.subtract).then_inc(split, 1)
                dve.wait_ge(split, 2)
                dve.wait_ge(roots_ready, 1)
                sums = bound_parts[:, :, 0, 0:1]
                c(nc.vector.tensor_reduce(sums, bound[:], AX.X, ALU.add))
                c.wait()
                c(nc.vector.tensor_reduce(bound_parts[:, 0, 1, 0:1], sums.rearrange("p k o -> p (k o)"), AX.X, ALU.max))
                c.wait()
                c(nc.vector.tensor_scalar(unbounded[:], bound_parts[:, 0, 1, 0:1], BOUND * HD ** 0.5, None, ALU.is_gt))
                c.wait()
                dve.sem_clear(dchain)

        def either_way(eng, batch, first=None):
            with eng.If(eng.value_load(unbounded[P - 1:P, 0:1]) > 0):
                with eng.Fori(0, BATCH) as b:
                    batch(b, False)
            with eng.Else():
                if first:
                    first()
                with eng.Fori(0, BATCH - 1) as b:
                    batch(b, True)
                batch(BATCH - 1, True, True)

        with nc.Block() as block:
            @block.sync
            def _(sp):
                def batch(b, bounded, final=False):
                    bank, USES = plan_of[bounded]
                    (yt, yh, yl, wd), (wqh, wql) = y_of[bounded], wq_of[bounded]
                    first = b * TT if final else sp.snap(b * TT)
                    if bounded:
                        sp.wait_ge(x2_ready, START + b * TT)
                        sp.dma_start(x1[:], x1_dram[bass.ds(first, TT)].rearrange("t p n -> p t n")).then_inc(xres_in, 16)
                        sp.wait_ge(raw_ready, START + b * TILES + TT)
                        sp.dma_start(wd[:], wd_dram).then_inc(wd_in, 16)
                    else:
                        sp.wait_ge(x2_ready, START + b * TT)
                        sp.dma_start(x1[:], x1_dram[bass.ds(first, TT)].rearrange("t p n -> p t n")).then_inc(x1_in, 16)
                        sp.wait_ge(pv_done, START + b * GROUPS * PAIRS)
                        sp.dma_start(wqh[:].bitcast(F32), wq_dram[0]).then_inc(wq_in, 16)
                        sp.dma_start(wql[:].bitcast(F32), wq_dram[1]).then_inc(wq_in, 16)
                        sp.wait_ge(raw_ready, START + b * TILES + TT)
                        sp.dma_start(wd[:], wd_dram).then_inc(wd_in, 16)
                        sp.dma_start(yt[:], io["yT"][bass.ds(b, 1)].rearrange("o (c p) n -> p (o c) n", p=P)).then_inc(y_in, 16)
                    for g in range(GROUPS):
                        k_to, q_to = (kTs[g % 2], qTs[g % 2]) if bounded else (kT, qT)
                        parts = [("kT", k_to, 0, CTX, (packh, packl, packh)), ("qT", q_to, CTX, SEQ, (packh, packh, packl))]
                        for kind, to, lo, n, packs in sorted(parts, key=lambda part: packed(g, part[0], bounded)):
                            sp.wait_ge(packl_ready, START + b * 2 * GROUPS + packed(g, kind, bounded))
                            for i in range(GROUP):
                                of = slice(HD * i, HD * (i + 1))
                                for r, pack in enumerate(packs):
                                    sp.dma_start(to[HD * r:HD * (r + 1), i].bitcast(F32), pack[of, lo:lo + n].bitcast(F32)).then_inc(heads_in[i], 16)
                    if bounded and not final:
                        load_x1(sp.snap(b * TT + TT))
                        following = sp.snap(b + 1)
                        sp.wait_ge(exp_ready, START + b * EXPS + 3 * PAIRS * GROUP)
                        sp.dma_start(wkvh[:].bitcast(F32), wkv_dram[0]).then_inc(wkv_in, 16)
                        sp.dma_start(wkvl[:].bitcast(F32), wkv_dram[1]).then_inc(wkv_in, 16)
                        sp.wait_ge(exp_ready, START + b * EXPS + 4 * PAIRS * GROUP)
                        load_early(following)
                    for t in range(TT):
                        sp.wait_ge(x2_ready, START + b * TT + t + 1)
                        sp.dma_start(x2_dram[bass.ds(b * TT + t, 1)].rearrange("o p n -> p (o n)"), x2[:, t % 2]).then_inc(x2_out[t % 2], 16)

                def load_x1(first):
                    sp.dma_start(x1_early, x1_dram[bass.ds(first, TT)].rearrange("t p n -> p t n")).then_inc(x1_in, 16)

                def load_early(b):
                    sp.dma_start(wqh_early[:].bitcast(F32), wq_dram[0]).then_inc(wq_in, 16)
                    sp.dma_start(wql_early[:].bitcast(F32), wq_dram[1]).then_inc(wq_in, 16)
                    sp.dma_start(yt_early[:], io["yT"][bass.ds(b, 1)].rearrange("o (c p) n -> p (o c) n", p=P)).then_inc(y_in, 16)

                def first():
                    load_x1(0)
                    load_early(0)

                either_way(sp, batch, first)
                for i in range(2):
                    sp.wait_ge(x2_out[i], START + 16 * BATCH * TT // 2)

            @block.scalar
            def _(act):
                def batch(b, bounded, final=False):
                    bank, USES = plan_of[bounded]
                    (yt, yh, yl, wd), (wqh, wql) = y_of[bounded], wq_of[bounded]
                    def square(n):
                        act.wait_ge(raw_ready, START + b * TILES + n + 1)
                        act.wait_ge(ss_ready, START + b * TILES + max(n - 1, 0))
                        nc.scalar.activation(sq[:, n % 2], raw[:, n % 4], ACT.Square).then_inc(sq_ready, 1)

                    def deviation(n):
                        act.wait_ge(ss_ready, START + b * TILES + n + 1)
                        act.wait_ge(unit_ready, START + b * TILES + max(n - 1, 0))
                        nc.scalar.activation(sd[:, n % 2], ss[:, n % 2], ACT.Sqrt, bias=eps6[:, 0:1], scale=1.0 / HD).then_inc(sd_ready, 1)

                    def heads(n):
                        if n < TILES:
                            square(n)
                        if 0 <= n - 1 < TILES:
                            deviation(n - 1)

                    act.wait_ge(x1_in, START + b * 16 + 16)
                    for t in range(TT + 1):
                        if t < TT:
                            slot, use = bank["x1T", t]
                            act.wait_ge(full[slot], START + b * USES + use)
                            nc.scalar.copy(x1h[:, :, P * t:P * (t + 1)], wide[slot][:, 0].rearrange("p (c n) -> p c n", n=P)).then_inc(x1h_ready, 1)
                        if t > 0:
                            heads(t - 1)
                    def pack(g, kind, lo, n):
                        for i in range(GROUP):
                            act.wait_ge(heads_in[i], START + (b * GROUPS + g) * HEAD_DMAS)
                        slot, use = bank[kind, g]
                        act.wait_ge(full[slot], START + b * USES + use)
                        nc.scalar.copy(packh[:, lo:lo + n], wide[slot][:].rearrange("p a n -> p (a n)")[:, 0:n]).then_inc(packh_ready, 1)

                    act.wait_ge(y_in, START + b * 16 + 16)
                    nc.scalar.copy(yh[:], yt[:]).then_inc(yh_ready, 1)
                    nc.scalar.copy(yd[:, :, LAST:P], yt[:, :, MAIN:CTX]).then_inc(yd_ready, 1)
                    for n in range(TT, TILES + 1):
                        if bounded and n == Q_TURN:
                            pack(0, "qT", CTX, SEQ)
                        heads(n)

                    def exponentials(g, kk, heads=range(GROUP)):
                        if heads[0] == 0:
                            act.wait_ge(pv_done, START + (b * GROUPS * PAIRS + g * PAIRS + kk - 1 if g * PAIRS + kk else b * GROUPS * PAIRS))
                        for i in heads:
                            slot, use = bank["score", g, kk, i]
                            act.wait_ge(full[slot], START + b * USES + use)
                            nc.scalar.activation(p[:, kk % 2, i], wide[slot][:], ACT.Exp, scale=float(HD) ** -0.5).then_inc(exp_ready, 1)

                    def round_output(g):
                        if g == 0:
                            act.wait_ge(x2_ready, START + b * TT)
                        act.wait_ge(ct_ready, START + b * GROUPS + g + 1)
                        nc.scalar.copy(cth[:, g], ct[:, g % 2]).then_inc(ch_ready, 1)

                    def take_sums(g):
                        act.wait_ge(pv_done, START + b * GROUPS * PAIRS + PAIRS * (g + 1))
                        act.wait_ge(ct_ready, START + b * GROUPS + g)
                        if g == 0:
                            for x in x2_out:
                                act.wait_ge(x, START + b * 16 * TT // 2)
                        nc.scalar.copy(rec[:, 0], acc["sum_main"][:]).then_inc(sums_taken, 1)
                        nc.scalar.copy(rec[:, 1], acc["sum_dca"][:]).then_inc(sums_taken, 1)

                    k_part, q_part = ("kT", 0, CTX), ("qT", CTX, SEQ)
                    if bounded:
                        pack(0, *k_part)
                    for g in range(GROUPS):
                        more = bounded and g + 1 < GROUPS
                        if not bounded:
                            pack(g, *k_part)
                            pack(g, *q_part)
                            for j in range(2):
                                slot, use = bank["shift", g, j]
                                act.wait_ge(full[slot], START + b * USES + use)
                                nc.scalar.copy(qT[ROWS:ROWS + 2, 2 * j:2 * j + 2], wide[slot][ROWS:ROWS + 2]).then_inc(shift_ready, 1)
                        exponentials(g, 0)
                        if bounded and g:
                            take_sums(g - 1)
                        if more:
                            pack(g + 1, *k_part)
                        exponentials(g, 1)
                        if more:
                            exponentials(g, 2, (0, 1))
                            pack(g + 1, *q_part)
                            exponentials(g, 2, (2, 3))
                        else:
                            exponentials(g, 2)
                        if bounded and g:
                            round_output(g - 1)
                        exponentials(g, 3)
                        if not bounded:
                            take_sums(g)
                            round_output(g)
                    if bounded:
                        take_sums(GROUPS - 1)
                        round_output(GROUPS - 1)

                either_way(act, batch)

            @block.gpsimd
            def _(pool):
                def batch(b, bounded, final=False):
                    bank, USES = plan_of[bounded]
                    (yt, yh, yl, wd), (wqh, wql) = y_of[bounded], wq_of[bounded]
                    pool.sem_clear(pchain)
                    c = Chain(pool, pchain)

                    def weigh(n):
                        k = 0 if n < TT else 2 if n == TILES - 1 else 1
                        rw, kw, to = (x.rearrange("p (h d) -> p h d", d=HD) for x in (raw[:, n % 4], kn[:, n % 2], qk[:, n]))
                        pool.wait_ge(unit_ready, START + b * TILES + n + 1)
                        c(nc.gpsimd.tensor_tensor(kw, rw, nw[:, k].unsqueeze(1).broadcast_to([P, HEADS, HD]), ALU.mult))
                        c.wait()
                        nc.gpsimd.tensor_tensor(to, kw, nb[:, k].unsqueeze(1).broadcast_to([P, HEADS, HD]), ALU.add).then_inc(kn_ready, 1)

                    pool.wait_ge(packl_ready, START + b * 2 * GROUPS)
                    for n in range(TILES):
                        weigh(n)
                    pool.wait_ge(x1l_ready, START + b * TT + TT)
                    if bounded:
                        pool.wait_ge(xres_in, START + b * 16 + 16)
                    nc.gpsimd.tensor_tensor(x1[:], x1[:], bo[:].unsqueeze(1).broadcast_to([P, TT, DM]), ALU.add).then_inc(x1_biased, 1)
                    for g in range(GROUPS):
                        pool.wait_ge(ch_ready, START + b * GROUPS + g + 1)
                        nc.gpsimd.tensor_tensor(ctl[:, g], ct[:, g % 2], cth[:, g].bitcast(F32), ALU.subtract).then_inc(cl_ready, 1)
                    for t in range(0, TT, 2):
                        pool.wait_ge(ve_ready, START + b * (TT // 2) + t // 2 + 1)
                        nc.gpsimd.tensor_tensor(rstd[:], ve[:], halves[:], ALU.pow).then_inc(rstd_ready, 1)
                    c.wait()

                either_way(pool, batch)

            @block.vector
            def _(dve):
                def batch(b, bounded, final=False):
                    bank, USES = plan_of[bounded]
                    (yt, yh, yl, wd), (wqh, wql) = y_of[bounded], wq_of[bounded]
                    dve.sem_clear(dchain)
                    c = Chain(dve, dchain)

                    def take(n):
                        slot, use = bank["head", n]
                        dve.wait_ge(full[slot], START + b * USES + use)
                        if n < TT:
                            dve.wait_ge(kn_ready, START + b * TILES + max(n - 3, 0))
                            nc.vector.tensor_tensor(raw[:, n % 4], wide[slot][:, 0], bq[:], ALU.add).then_inc(raw_ready, 1)
                            return
                        k = n - TT
                        bias = bkv7 if k == KT_N - 1 else bkv
                        dve.wait_ge(kn_ready, START + b * TILES + n - 3)
                        nc.vector.tensor_tensor(raw[:, n % 4], wide[slot][:, 0], bias[:, 0:HT], ALU.add).then_inc(raw_ready, 1)
                        nc.vector.tensor_tensor(v[:, k], wide[slot][:, 1], bias[:, HT:2 * HT], ALU.add).then_inc(v_ready, 1)
                        if k == KT_N - 1:
                            dve.wait_ge(v_ready, START + b * KT_N + KT_N)
                            nc.vector.tensor_scalar(vd[:], v[:, k], dca_row[:, 0:1], None, ALU.mult).then_inc(vd_ready, 1)

                    def square_sum(n):
                        dve.wait_ge(sq_ready, START + b * TILES + n + 1)
                        dve.wait_ge(sd_ready, START + b * TILES + max(n - 1, 0))
                        nc.vector.tensor_reduce(ss[:, n % 2], sq[:, n % 2].rearrange("p (h d) -> p h d", d=HD), AX.X, ALU.add).then_inc(ss_ready, 1)

                    def unit(n):
                        dve.wait_ge(sd_ready, START + b * TILES + n + 1)
                        c(nc.vector.reciprocal(sd[:, n % 2], sd[:, n % 2]))
                        c.wait()
                        rw = raw[:, n % 4].rearrange("p (h d) -> p h d", d=HD)
                        nc.vector.tensor_tensor(rw, rw, sd[:, n % 2].unsqueeze(2).broadcast_to([P, HEADS, HD]), ALU.mult).then_inc(unit_ready, 1)

                    def heads(n):
                        if n < TILES:
                            take(n)
                        if 0 <= n - 1 < TILES:
                            square_sum(n - 1)
                        if 0 <= n - 2 < TILES:
                            unit(n - 2)

                    for t in range(TT + 1):
                        if t < TT:
                            slot, use = bank["x1T", t]
                            dve.wait_ge(x1h_ready, START + b * TT + t + 1)
                            nc.vector.tensor_tensor(x1l[:, :, P * t:P * (t + 1)], wide[slot][:, 0].rearrange("p (c n) -> p c n", n=P),
                                                    x1h[:, :, P * t:P * (t + 1)].bitcast(F32), ALU.subtract).then_inc(x1l_ready, 1)
                        if t > 0:
                            heads(t - 1)
                    dve.wait_ge(yh_ready, START + b + 1)
                    nc.vector.tensor_tensor(yl[:], yt[:], yh[:].bitcast(F32), ALU.subtract).then_inc(yl_ready, 1)

                    def pack(g, a):
                        kind, lo, n = (("kT", 0, CTX), ("qT", CTX, SEQ))[a]
                        slot, use = bank[kind, g]
                        dve.wait_ge(packh_ready, START + b * 2 * GROUPS + packed(g, kind, bounded))
                        nc.vector.tensor_tensor(packl[:, lo:lo + n], wide[slot][:].rearrange("p a n -> p (a n)")[:, 0:n],
                                                packh[:, lo:lo + n].bitcast(F32), ALU.subtract).then_inc(packl_ready, 1)

                    for n in range(TT, TILES + 2):
                        heads(n)
                        if bounded and n == Q_TURN - 1:
                            pack(0, 1)

                    def maxima(g):
                        for i in range(GROUP):
                            for t in range(TT):
                                slot, use = bank["max", g, i, t]
                                at = ROWS + 2 * ((GROUP * g + i) * TT + t)
                                dve.wait_ge(full[slot], START + b * USES + use)
                                flat = wide[slot][:].rearrange("p a n -> p (a n)")
                                c(nc.vector.tensor_reduce(mx[:, at + 1:at + 2], flat[:, MAIN:CTX], AX.X, ALU.max, negate=True))
                                nc.vector.tensor_reduce(mx[:, at:at + 1], flat[:, 0:MAIN], AX.X, ALU.max, negate=True).then_inc(mx_ready, 1)

                    def divide(g, ahead):
                        dve.wait_ge(pv_done, START + b * GROUPS * PAIRS + PAIRS * (g + 1))
                        c(nc.vector.tensor_copy(outs[:, 0], acc["ctx_main"][:]))
                        c(nc.vector.tensor_copy(outs[:, 1], acc["ctx_dca"][:]))
                        c.wait()
                        dve.sem_inc(outs_taken, 1)
                        if ahead:
                            pack(g + 2, 0)
                        dve.wait_ge(sums_taken, START + b * 2 * GROUPS + 2 * g + 2)
                        c(nc.vector.reciprocal(rec[:], rec[:]))
                        if ahead:
                            pack(g + 2, 1)
                        c.wait()
                        dve.wait_ge(cl_ready, START + b * GROUPS + max(g - 1, 0))
                        c(nc.vector.tensor_tensor(outs[:], outs[:], rec[:], ALU.mult))
                        c.wait()
                        nc.vector.tensor_tensor(ct[:, g % 2], outs[:, 0], outs[:, 1], ALU.add).then_inc(ct_ready, 1)

                    if bounded:
                        pack(0, 0)
                        pack(1, 0)
                        pack(1, 1)
                        for g in range(GROUPS):
                            divide(g, g + 2 < GROUPS)
                    else:
                        for g in range(GROUPS):
                            pack(g, 0)
                            pack(g, 1)
                            maxima(g)
                            divide(g, False)
                    dve.wait_ge(ct_ready, START + b * GROUPS + GROUPS)
                    dve.wait_ge(x1_biased, START + b + 1)
                    for t in range(0, TT, 2):
                        for j in range(2):
                            slot, use = bank["wo", t + j]
                            dve.wait_ge(full[slot], START + b * USES + use)
                            nc.vector.tensor_tensor(ct[:, j], wide[slot][:, 0], x1[:, t + j], ALU.add).then_inc(wo_taken, 1)
                        for j in range(2):
                            dve.wait_ge(wo_taken, START + b * TT + t + j + 1)
                            c(nc.vector.bn_stats(st6[:, j], ct[:, j]))
                        c.wait()
                        for j in range(2):
                            c(nc.vector.bn_aggr(mv[:, j], st6[:, j]))
                        c.wait()
                        nc.vector.tensor_scalar(ve[:], mv[:, :, 1], 1e-5, None, ALU.add).then_inc(ve_ready, 1)
                        dve.wait_ge(rstd_ready, START + b * (TT // 2) + t // 2 + 1)
                        for j in range(2):
                            dve.wait_ge(x2_out[j], START + (b * (TT // 2) + t // 2) * 16)
                            nc.vector.tensor_scalar(x2[:, j], ct[:, j], mv[:, j, 0:1], rstd[:, j:j + 1],
                                                    ALU.subtract, ALU.mult).then_inc(x2_ready, 1)
                        dve.wait_ge(x2_ready, START + b * TT + t + 2)
                    c.wait()

                either_way(dve, batch)

            @block.tensor
            def _(pe):
                def product(out, pairs, first=True):
                    for i, (l, r) in enumerate(pairs):
                        last = nc.tensor.matmul(out, l, r, start=(first and i == 0), stop=(i == len(pairs) - 1))
                    return last

                def taken(bounded, kind, *at):
                    if kind == "x1T":
                        return x1l_ready, at[0] + 1, TT
                    if kind == "head":
                        return (raw_ready, at[0] + 1, TILES) if at[0] < TT else (v_ready, at[0] - TT + 1, KT_N)
                    if kind in ("kT", "qT"):
                        return packl_ready, packed(at[0], kind, bounded), 2 * GROUPS
                    if kind == "max":
                        return mx_ready, (GROUP * at[0] + at[1]) * TT + at[2] + 1, HEADS * TT
                    if kind == "shift":
                        return shift_ready, 2 * at[0] + at[1] + 1, 2 * GROUPS
                    if kind == "score":
                        return exp_ready, (at[0] * PAIRS + at[1]) * GROUP + at[2] + 1, EXPS
                    return wo_taken, at[0] + 1, TT

                def batch(b, bounded, final=False):
                    bank, USES = plan_of[bounded]
                    (yt, yh, yl, wd), (wqh, wql) = y_of[bounded], wq_of[bounded]
                    def claim(*group):
                        order = order_of[bounded]
                        at = order.index(group)
                        what, value, per_batch = taken(bounded, *order[at - 2])
                        pe.wait_ge(what, START + (b * per_batch + (value if at >= 2 else 0)))
                        return bank[group][0]

                    def x1_turned(t):
                        slot = claim("x1T", t)
                        for k in range(DC):
                            last = nc.tensor.transpose(wide[slot][:, 0, P * k:P * (k + 1)], x1_from[bounded][:, t, P * k:P * (k + 1)], ident[:])
                        last.then_inc(full[slot], 1)

                    def queries(t):
                        slot = claim("head", t)
                        pe.wait_ge(x1l_ready, START + b * TT + t + 1)
                        tok = slice(P * t, P * (t + 1))
                        product(wide[slot][:, 0], [(x[:, k, tok], w[:, k]) for k in range(DC)
                                                   for x, w in ((x1h, wqh), (x1l, wqh), (x1h, wql))]).then_inc(full[slot], 1)

                    pe.wait_ge(x1_in, START + b * 16 + 16)
                    for t in range(TT + 1):
                        if t < TT:
                            x1_turned(t)
                        if t == 1:
                            pe.wait_ge(wq_in, START + b * 32 + 32)
                        if t > 0:
                            queries(t - 1)
                    pe.wait_ge(yh_ready, START + b + 1)
                    pe.wait_ge(yl_ready, START + b + 1)
                    if bounded:
                        pe.wait_ge(wkv_in, START + b * 32)

                    def heads_turned(g, kind, first, n):
                        slot = claim(kind, g)
                        for k in range(n):
                            last = nc.tensor.transpose(wide[slot][:, k // 4, P * (k % 4):P * (k % 4 + 1)],
                                                       qk[:, first + k, P * g:P * (g + 1)], ident[:])
                        last.then_inc(full[slot], 1)

                    k_part, q_part = ("kT", TT, KT_N), ("qT", 0, TT)
                    for k in range(KT_N):
                        if bounded and TT + k == Q_TURN:
                            pe.wait_ge(kn_ready, START + b * TILES + TT)
                            heads_turned(0, *q_part)
                        slot = claim("head", TT + k)
                        keys = LAST if k == KT_N - 1 else P
                        tok = slice(P * k, P * k + keys)
                        if k == KT_N - 1:
                            pe.wait_ge(yd_ready, START + b + 1)
                            pe.wait_ge(wd_in, START + b * 16 + 16)
                        for half_ in range(2):
                            cols = slice(HT * half_, HT * (half_ + 1))
                            if k == KT_N - 1:
                                for cc in range(CC):
                                    nc.tensor.matmul(wide[slot][:, half_], yd[:, cc], wd[:, cc, cols], start=(cc == 0), stop=False)
                            last = product(wide[slot][0:keys, half_], [(x[:, cc, tok], w[:, cc, cols]) for cc in range(CC)
                                                                       for x, w in ((yh, wkvh), (yl, wkvh), (yh, wkvl))], k < KT_N - 1)
                        last.then_inc(full[slot], 1)


                    def maxima(g):
                        for i in range(GROUP):
                            pe.wait_ge(heads_in[i], START + (b * GROUPS + g + 1) * HEAD_DMAS)
                            for t in range(TT):
                                slot = claim("max", g, i, t)
                                for a in range(2):
                                    last = nc.tensor.matmul(wide[slot][:, a], qT[0:ROWS, i, P * t:P * (t + 1)], kT[0:ROWS, i, 512 * a:512 * (a + 1)],
                                                            start=True, stop=True)
                                last.then_inc(full[slot], 1)
                        for j in range(2):
                            slot = claim("shift", g, j)
                            pe.wait_ge(mx_ready, START + b * HEADS * TT + (GROUP * g + 2 * j + 2) * TT)
                            for i in range(2):
                                for t in range(TT):
                                    at = 2 * ((GROUP * g + 2 * j + i) * TT + t)
                                    last = nc.tensor.transpose(wide[slot][0:ROWS + 2, i, P * t:P * (t + 1)], mx[:, at:at + ROWS + 2], ident[:])
                            last.then_inc(full[slot], 1)

                    def scores(g, kk, heads):
                        for i in heads:
                            keys_t, queries_t, rows = (kTs[g % 2], qTs[g % 2], ROWS) if bounded else (kT, qT, ROWS + 2)
                            slot = claim("score", g, kk, i)
                            if kk == 0 and bounded:
                                pe.wait_ge(heads_in[i], START + (b * GROUPS + g + 1) * HEAD_DMAS)
                            elif kk == 0:
                                pe.wait_ge(shift_ready, START + b * 2 * GROUPS + 2 * g + i // 2 + 1)
                            for a in range(2):
                                k = 2 * kk + a
                                last = nc.tensor.matmul(wide[slot][:, a], keys_t[0:rows, i, P * k:P * (k + 1)], queries_t[0:rows, i], start=True, stop=True)
                            last.then_inc(full[slot], 1)

                    def values(g, kk, a):
                        k = 2 * kk + a
                        if a == 0:
                            pe.wait_ge(exp_ready, START + b * EXPS + (g * PAIRS + kk + 1) * GROUP)
                        if k == 0:
                            pe.wait_ge(outs_taken, START + b * GROUPS + g)
                            pe.wait_ge(sums_taken, START + b * 2 * GROUPS + 2 * g)
                        rows = LAST if k == KT_N - 1 else P
                        work = [("ctx_main", rows, lambda i: v[0:rows, k, HD * (GROUP * g + i):HD * (GROUP * g + i + 1)], k == 0, k == KT_N - 1),
                                ("sum_main", rows, lambda i: ones[0:rows], k == 0, k == KT_N - 1)]
                        if k == KT_N - 1:
                            work += [("ctx_dca", P, lambda i: vd[:, HD * (GROUP * g + i):HD * (GROUP * g + i + 1)], True, True),
                                     ("sum_dca", P, lambda i: ones_dca[:], True, True)]
                        for name, m, left, start, stop in work:
                            for i in range(GROUP):
                                last = nc.tensor.matmul(acc[name][HD * i:HD * (i + 1)], left(i), p[0:m, kk % 2, i, a], start=start, stop=stop,
                                                        tile_position=(0, HD * i))
                        if a:
                            last.then_inc(pv_done, 1)

                    pe.wait_ge(kn_ready, START + b * TILES + TILES)
                    pe.wait_ge(vd_ready, START + b + 1)
                    if bounded:
                        heads_turned(0, *k_part)
                        before = None
                        for g in range(GROUPS):
                            for kk in range(PAIRS):
                                scores(g, kk, (0, 1))
                                if before:
                                    values(*before, 0)
                                if kk == 2 and g + 1 < GROUPS:
                                    heads_turned(g + 1, *q_part)
                                scores(g, kk, (2, 3))
                                if before:
                                    values(*before, 1)
                                if kk == 0 and g + 1 < GROUPS:
                                    heads_turned(g + 1, *k_part)
                                before = (g, kk)
                        values(*before, 0)
                        values(*before, 1)
                    else:
                        for g in range(GROUPS):
                            heads_turned(g, *k_part)
                            heads_turned(g, *q_part)
                            maxima(g)
                            for kk in range(PAIRS + 1):
                                if kk < PAIRS:
                                    scores(g, kk, range(GROUP))
                                if kk:
                                    values(g, kk - 1, 0)
                                    values(g, kk - 1, 1)
                    for t in range(TT):
                        slot = claim("wo", t)
                        pe.wait_ge(cl_ready, START + b * GROUPS + GROUPS)
                        product(wide[slot][:, 0], [(x[:, k, P * t:P * (t + 1)], w[:, k]) for k in range(GROUPS)
                                                   for x, w in ((cth, woh), (ctl, woh), (cth, wol))]).then_inc(full[slot], 1)

                either_way(pe, batch)


FF = 2048
KEEP = 204
FC = FF // P
KEY_BITS = 31
AIM = 200
START_SIGMAS = 1.2831
DENSITY = 358.7
STEP_GAINS = (0.96, 0.78, 0.7, 0.52, 0.35)
COUNTS = len(STEP_GAINS) + 1


def sparse_ffn(nc, io, x2_dram, out):
    HALF = FF // 2
    with ExitStack() as ctx:
        def sb(name, shape, dt=F32):
            return ctx.enter_context(nc.sbuf_tensor("sf_" + name, shape, dt))

        def sem(name):
            return ctx.enter_context(nc.semaphore("f_" + name))

        counters = []

        def counter(name):
            counters.append(sem(name))
            return counters[-1]

        wide = [ctx.enter_context(nc.psum_tensor(f"f_wide{i}", [P, 2, 512], F32)) for i in range(4)]

        w_in_t = sb("w_in_t", [P, DC, FF], F32R)
        w_out_t = sb("w_out_t", [P, FC, DM], F32R)
        b_syn, b_out, gamma, beta = sb("b_syn", [P, FF]), sb("b_out", [P, DM]), sb("gamma", [P, DM]), sb("beta", [P, DM])
        ident, ones = sb("ident", [P, P]), sb("ones", [P, P])
        bits = sb("bits", [P, KEY_BITS], U32)
        places = sb("places", [P, 9])
        parts, total = sb("parts", [P, 2, 64]), sb("total", [P, 2])
        scale, limit, low_limit = sb("scale", [P, 2]), sb("limit", [P, 2]), sb("low_limit", [P, 2])
        square_sums = sb("square_sums", [P, 5])
        spread, bias_spread = sb("spread", [P, 1]), sb("bias_spread", [P, 1])
        first_guess = sb("first_guess", [P, 1])
        gains = sb("gains", [P, COUNTS - 1])
        half, aim = sb("half", [P, 2]), sb("aim", [P, 1])
        xin, xres, x2b = sb("xin", [P, TT, DM]), sb("xres", [P, TT, DM]), sb("x2b", [P, 2, DM])
        z = sb("z", [P, TT, FF])
        guess = sb("guess", [P, 2, 1])
        above = sb("above", [P, 2, 1])
        miss, far, step = sb("miss", [P, 1]), sb("far", [P, 1]), sb("step", [P, 1])
        top = sb("top", [P, 2, 9])
        place, chosen = sb("place", [P, 2, 1]), sb("chosen", [P, 2, 9])
        cut = sb("cut", [P, 2, 1])
        kept, wrong = sb("kept", [P, 2]), sb("wrong", [P, 2])
        any_wrong = sb("any_wrong", [P, 1], U32)
        key, trial = sb("key", [P, 1], U32), sb("trial", [P, 1], U32)
        count = sb("count", [P, 1])
        enough = sb("enough", [P, 1], U32)
        st6, mv, ve, rstd = sb("st6", [P, 2, 6]), sb("mv", [P, 2, 2]), sb("ve", [P, 2]), sb("rstd", [P, 2])
        with ExitStack() as region:
            w_raw = region.enter_context(nc.sbuf_tensor("sf_w_raw", [P, 4 * FF], F32))
            sign = region.enter_context(nc.sbuf_tensor("sf_sign", [P, 2, FF], F32))
        x2h, x2l = sb("x2h", [P, 2, DC, P], F32R), sb("x2l", [P, 2, DC, P], F32R)
        hid = sb("hid", [P, 2, FF])
        hTh, hTl = sb("hTh", [P, FC, P], F32R), sb("hTl", [P, FC, P], F32R)
        s, u, y = sb("s", [P, 2, DM]), sb("u", [P, 2, DM]), sb("y", [P, 2, DM])
        unused = sb("unused", [P, 2, FF], mybir.dt.bfloat16)

        const_in, w_in = sem("const_in"), [sem(f"w{i}_in") for i in range(2)]
        ones_ready, part_ready, total_ready, signs_ready = sem("ones_ready"), sem("part_ready"), sem("total_ready"), sem("signs_ready")
        squares_ready, sums_ready, spread_ready, root_ready = sem("squares_ready"), sem("sums_ready"), sem("spread_ready"), sem("root_ready")
        xin_in = [counter(f"xin{h}_in") for h in range(2)]
        xres_in = [counter(f"xres{h}_in") for h in range(2)]
        y_out = [counter(f"y{h}_out") for h in range(2)]
        (xT_full, x2h_ready, x2l_ready, z_full, z_ready, counted, stepped, tried, kept_ready, wrong_ready, wrong_sum,
         hid_ready, hT_full, hh_ready, hl_ready, out_full, s_ready, x2_biased, ve_ready, rstd_ready, residual_used,
         y_ready) = (counter(n) for n in (
             "xT_full", "x2h_ready", "x2l_ready", "z_full", "z_ready", "counted", "stepped", "tried", "kept_ready", "wrong_ready",
             "wrong_sum", "hid_ready", "hT_full", "hh_ready", "hl_ready", "out_full", "s_ready", "x2_biased", "ve_ready",
             "rstd_ready", "residual_used", "y_ready"))
        dchain, pchain = sem("dchain"), sem("pchain")

        with nc.Block() as block:
            @block.sync
            def _(sp):
                for c in counters:
                    sp.sem_inc(c, START)
                sp.dma_start(w_raw[:].rearrange("p (c n) -> p c n", c=DC), io["w_synT"].rearrange("(c p) n -> p c n", p=P)).then_inc(w_in[0], 16)
                for t_, n in ((b_syn, "b_syn"), (b_out, "b_out"), (gamma, "gamma"), (beta, "beta"), (places, "places"), (bits, "bits")):
                    sp.dma_start(t_[:], io[n].partition_broadcast(P)).then_inc(const_in, 16)
                sp.dma_start(ident[:], io["ident"]).then_inc(const_in, 16)
                sp.wait_ge(signs_ready, 4)
                sp.dma_start(w_raw[:].rearrange("p (c n) -> p c n", c=FC), io["w_outT"].rearrange("(c p) n -> p c n", p=P)).then_inc(w_in[1], 16)
                sp.wait_ge(const_in, 16 * 7)

            @block.gpsimd
            def _(pool):
                pool.memset(half[:], -0.5)
                pool.memset(aim[:], float(FF - 2 * AIM))
                pool.memset(ones[:], 1.0).then_inc(ones_ready, 1)

            @block.scalar
            def _(act):
                for a in range(4):
                    act.wait_ge(signs_ready, a + 1)
                    nc.scalar.activation(z[:, a], w_in_t[:, a].bitcast(F32), ACT.Square, accum_out=square_sums[:, a:a + 1]).then_inc(squares_ready, 1)
                act.wait_ge(const_in, 16 * 7)
                act.wait_ge(squares_ready, 4)
                nc.scalar.activation(z[:, 0], b_syn[:], ACT.Square, accum_out=square_sums[:, 4:5]).then_inc(squares_ready, 1)
                act.wait_ge(spread_ready, 1)
                nc.scalar.activation(spread[:], spread[:], ACT.Sqrt).then_inc(root_ready, 1)

            @block.tensor
            def _(pe):
                pe.wait_ge(ones_ready, 1)
                for k in range(2):
                    pe.wait_ge(part_ready, k + 1)
                    nc.tensor.matmul(wide[k][:, 0, 0:1], ones[:], total[:, k:k + 1], start=True, stop=True).then_inc(total_ready, 1)
                pe.wait_ge(squares_ready, 4)
                nc.tensor.matmul(wide[2][:, 0, 0:4], ones[:], square_sums[:, 0:4], start=True, stop=True).then_inc(sums_ready, 1)

            @block.vector
            def _(dve):
                c = Chain(dve, dchain)
                for k, dst in enumerate((w_in_t[:].rearrange("p c n -> p (c n)"), w_out_t[:].rearrange("p c n -> p (c n)"))):
                    dve.wait_ge(w_in[k], 16)
                    c(nc.vector.tensor_reduce(parts[:, k], w_raw[:].rearrange("p (a n) -> p a n", a=64), AX.X, ALU.add, apply_absolute_value=True))
                    c.wait()
                    nc.vector.tensor_reduce(total[:, k:k + 1], parts[:, k], AX.X, ALU.add).then_inc(part_ready, 1)
                    dve.wait_ge(total_ready, k + 1)
                    c(nc.vector.tensor_scalar(scale[:, k:k + 1], wide[k][:, 0, 0:1], 1.0 / (FF * DM), None, ALU.mult))
                    c.wait()
                    c(nc.vector.tensor_scalar(limit[:, k:k + 1], scale[:, k:k + 1], 1e-8, 0.5, ALU.add, ALU.mult))
                    c.wait()
                    c(nc.vector.tensor_scalar(low_limit[:, k:k + 1], limit[:, k:k + 1], -1.0, None, ALU.mult))
                    c(nc.vector.tensor_scalar(scale[:, k:k + 1], scale[:, k:k + 1], -1.0, None, ALU.mult))
                    for a in range(4):
                        part = slice(FF * a, FF * (a + 1))
                        c.wait()
                        if a >= 2:
                            dve.wait_ge(signs_ready, 4 * k + a - 1)
                        c(nc.vector.tensor_scalar(sign[:, a % 2], w_raw[:, part], limit[:, k:k + 1], None, ALU.is_gt))
                        c.wait()
                        nc.vector.scalar_tensor_tensor(dst[:, part], w_raw[:, part], low_limit[:, k:k + 1], sign[:, a % 2], ALU.is_lt, ALU.subtract).then_inc(signs_ready, 1)
                dve.wait_ge(sums_ready, 1)
                c(nc.vector.tensor_reduce(spread[:], wide[2][:, 0, 0:4], AX.X, ALU.add))
                c.wait()
                dve.wait_ge(squares_ready, 5)
                for factor in (scale[:, 0:1], scale[:, 0:1]):
                    c(nc.vector.tensor_scalar(spread[:], spread[:], factor, None, ALU.mult))
                    c.wait()
                c(nc.vector.tensor_tensor(spread[:], spread[:], square_sums[:, 4:5], ALU.add))
                c.wait()
                nc.vector.tensor_scalar(spread[:], spread[:], 1.0 / FF, None, ALU.mult).then_inc(spread_ready, 1)
                dve.wait_ge(root_ready, 1)
                c(nc.vector.tensor_scalar(first_guess[:], spread[:], -START_SIGMAS, None, ALU.mult))
                for i, gain in enumerate(STEP_GAINS):
                    c(nc.vector.tensor_scalar(gains[:, i:i + 1], spread[:], -gain / (2 * DENSITY), None, ALU.mult))
                c.wait()
                dve.wait_ge(signs_ready, 8)
                dve.sem_clear(dchain)

        def after(b, t, per_tile):
            return START + b * (TT * per_tile) + t * per_tile

        def over_pairs(eng, first, pair):
            first()
            with eng.Fori(0, BATCH - 1) as b:
                pair(b, 0, 2)
                pair(b, 2, 2)
            pair(BATCH - 1, 0, 1)
            pair(BATCH - 1, 2, 0)

        with nc.Block() as block:
            @block.sync
            def _(sp):
                def load(to, first, t, done):
                    sp.dma_start(to[:, t:t + 2], x2_dram[bass.ds(first, 2)].rearrange("t p n -> p t n")).then_inc(done[t // 2], 16)

                def pair(b, t, left):
                    first = b * TT + t if isinstance(b, int) else sp.snap(b * TT + t)
                    ahead = b * TT + t + TT if isinstance(b, int) else sp.snap(b * TT + t + TT)
                    if left == 2:
                        sp.wait_ge(xT_full, START + b * 2 + t // 2 + 1)
                        load(xin, ahead, t, xin_in)
                    sp.wait_ge(residual_used, START + b * 2 + t // 2)
                    load(xres, first, t, xres_in)
                    sp.wait_ge(y_ready, START + b * 2 + t // 2 + 1)
                    sp.dma_start(out[bass.ds(b, 1), t * P:(t + 2) * P].rearrange("o (t p) n -> p (o t) n", p=P), y[:]).then_inc(y_out[t // 2], 16)

                def first():
                    load(xin, 0, 0, xin_in)
                    load(xin, 2, 2, xin_in)

                over_pairs(sp, first, pair)
                for i in range(2):
                    sp.wait_ge(y_out[i], START + 16 * BATCH)

            @block.scalar
            def _(act):
                def split(b, t):
                    act.wait_ge(xT_full, START + b * 2 + t // 2 + 1)
                    act.wait_ge(z_full, after(b, t, 2))
                    nc.scalar.copy(x2h[:], wide[0][:].rearrange("p t (c n) -> p t c n", n=P)).then_inc(x2h_ready, 1)

                def rounds(b, t, some):
                    for r in some:
                        for i in range(2):
                            if r == 0:
                                act.wait_ge(z_ready, after(b, t + i + 1, 2))
                                act.wait_ge(kept_ready, after(b, t, 1))
                                bias = first_guess[:]
                            else:
                                act.wait_ge(stepped, START + b * 20 + t * 5 + 2 * (r - 1) + i + 1)
                                bias = guess[:, i]
                            nc.scalar.activation(unused[:, i], z[:, t % 4 + i], ACT.Sign, bias=bias, accum_out=above[:, i]).then_inc(counted, 1)

                def turned(b, n):
                    act.wait_ge(out_full, after(b, n, 1))
                    for a in range(2):
                        act.wait_ge(hT_full, START + b * 8 + 2 * n + a + 1)
                        nc.scalar.copy(hTh[:, 8 * a:8 * a + 8], wide[3 - 3 * a][:].rearrange("p a (c n) -> p (a c) n", n=P)).then_inc(hh_ready, 1)

                def first():
                    split(0, 0)
                    rounds(0, 0, [0])
                    split(0, 2)
                    rounds(0, 0, range(1, COUNTS))

                def pair(b, t, left):
                    for i in range(2):
                        act.wait_ge(tried, after(b, t + i + 1, 1))
                        nc.scalar.activation(unused[:, i], hid[:, i], ACT.Sign, accum_out=kept[:, i:i + 1]).then_inc(kept_ready, 1)
                    if left:
                        rounds(b, t + 2, [0])
                    turned(b, t)
                    if left:
                        rounds(b, t + 2, [1, 2])
                    turned(b, t + 1)
                    if left:
                        rounds(b, t + 2, [3])
                    if left == 2:
                        split(b, t + 4)
                    if left:
                        rounds(b, t + 2, range(4, COUNTS))

                over_pairs(act, first, pair)

            @block.gpsimd
            def _(pool):
                def steps(c, b, t, some):
                    for r in some:
                        for i in range(2):
                            pool.wait_ge(counted, START + b * 24 + t * 6 + 2 * r + i + 1)
                            c(nc.gpsimd.tensor_tensor(miss[:], above[:, i], aim[:], ALU.add))
                            c.wait()
                            c(nc.gpsimd.tensor_tensor(far[:], miss[:], miss[:], ALU.mult))
                            c.wait()
                            c(nc.gpsimd.tensor_scalar(far[:], far[:], 64.5, None, ALU.is_gt))
                            c.wait()
                            c(nc.gpsimd.tensor_tensor(step[:], far[:], miss[:], ALU.mult))
                            c.wait()
                            c(nc.gpsimd.tensor_tensor(step[:], step[:], gains[:, r:r + 1], ALU.mult))
                            c.wait()
                            c(nc.gpsimd.tensor_tensor(guess[:, i], step[:], first_guess[:] if r == 0 else guess[:, i], ALU.add))
                            c.wait()
                            pool.sem_inc(stepped, 1)

                def pair(b, t, left):
                    c = Chain(pool, pchain)
                    if left:
                        steps(c, b, t + 2, range(3))
                    pool.wait_ge(s_ready, after(b, t, 1))
                    pool.wait_ge(xres_in[t // 2], START + b * 16 + 16)
                    nc.gpsimd.tensor_tensor(x2b[:], xres[:, t:t + 2], b_out[:].unsqueeze(1).broadcast_to([P, 2, DM]), ALU.add).then_inc(x2_biased, 1)
                    if left:
                        steps(c, b, t + 2, range(3, COUNTS - 1))
                    for n in range(2):
                        pool.wait_ge(ve_ready, START + b * 4 + t + n + 1)
                        nc.gpsimd.tensor_tensor(rstd[:], ve[:], half[:], ALU.pow).then_inc(rstd_ready, 1)
                    pool.sem_clear(pchain)

                def first():
                    steps(Chain(pool, pchain), 0, 0, range(COUNTS - 1))
                    pool.sem_clear(pchain)

                over_pairs(pool, first, pair)

            @block.vector
            def _(dve):
                def split(b, t):
                    dve.wait_ge(x2h_ready, START + b * 2 + t // 2 + 1)
                    nc.vector.tensor_tensor(x2l[:], wide[0][:].rearrange("p t (c n) -> p t c n", n=P), x2h[:].bitcast(F32), ALU.subtract).then_inc(x2l_ready, 1)

                def into_hidden(b, t, i):
                    for a in range(2):
                        cols = slice(HALF * a, HALF * (a + 1))
                        dve.wait_ge(z_full, START + b * 8 + 2 * (t + i) + a + 1)
                        nc.vector.scalar_tensor_tensor(z[:, t % 4 + i, cols], wide[1 + a][:].rearrange("p a n -> p (a n)"), scale[:, 0:1],
                                                       b_syn[:, cols], ALU.mult, ALU.add).then_inc(z_ready, 1)

                def search_bits(t):
                    for i in range(2):
                        nc.vector.memset(key[:], 0).then_inc(dchain, 1)
                        dve.wait_ge(dchain, 1)
                        dve.sem_clear(dchain)
                        with dve.Fori(0, KEY_BITS) as k:
                            nc.vector.tensor_tensor(trial[:], key[:], bits[:, bass.ds(k, 1)], ALU.bitwise_or).then_inc(dchain, 1)
                            dve.wait_ge(dchain, 1)
                            nc.vector.tensor_scalar(hid[:, i], z[:, t % 4 + i], trial[:].bitcast(F32), None, ALU.is_ge, ALU.add, accum_out=count[:]).then_inc(dchain, 1)
                            dve.wait_ge(dchain, 2)
                            nc.vector.tensor_scalar(enough[:], count[:], KEEP - 0.5, None, ALU.is_ge).then_inc(dchain, 1)
                            dve.wait_ge(dchain, 3)
                            nc.vector.copy_predicated(key[:], enough[:], trial[:]).then_inc(dchain, 1)
                            dve.wait_ge(dchain, 4)
                            dve.sem_clear(dchain)
                        zt = z[:, t % 4 + i]
                        nc.vector.scalar_tensor_tensor(hid[:, i], zt, key[:].bitcast(F32), zt, ALU.is_ge, ALU.mult).then_inc(dchain, 1)
                        dve.wait_ge(dchain, 1)
                        dve.sem_clear(dchain)

                def keep_largest(c, b, t, i):
                    zt = z[:, t % 4 + i]
                    dve.wait_ge(counted, START + b * 24 + t * 6 + 10 + i + 1)
                    c(nc.vector.tensor_scalar(top[:, i, 8:9], guess[:, i], -1.0, None, ALU.mult))
                    c(nc.vector.tensor_scalar(place[:, i], above[:, i], -0.5, KEEP - 1 - FF / 2, ALU.mult, ALU.add))
                    c.wait()
                    c(nc.vector.scalar_tensor_tensor(hid[:, i], zt, top[:, i, 8:9], zt, ALU.is_lt, ALU.mult))
                    c.wait()
                    c(nc.vector.max(top[:, i, 0:8], hid[:, i]))
                    c.wait()
                    c(nc.vector.scalar_tensor_tensor(chosen[:, i], places[:], place[:, i], top[:, i], ALU.is_equal, ALU.mult))
                    c.wait()
                    c(nc.vector.tensor_reduce(cut[:, i], chosen[:, i], AX.X, ALU.add))
                    c.wait()
                    c(nc.vector.scalar_tensor_tensor(hid[:, i], zt, cut[:, i], zt, ALU.is_ge, ALU.mult))
                    c.wait()
                    dve.sem_inc(tried, 1)

                def check_kept(c, b, t):
                    dve.wait_ge(kept_ready, after(b, t + 2, 1))
                    c(nc.vector.tensor_scalar(wrong[:], kept[:], float(KEEP), None, ALU.not_equal))
                    c.wait()
                    dve.sem_inc(wrong_ready, 1)
                    dve.wait_ge(wrong_sum, START + b * 2 + t // 2 + 1)
                    c(nc.vector.tensor_copy(any_wrong[:], wide[1][:, 1, 0:1]))
                    c.wait()
                    dve.sem_clear(dchain)
                    c.n = 0
                    rows = dve.value_load(any_wrong[0:1, 0:1])
                    with dve.If(rows > 0):
                        search_bits(t)
                    dve.sem_inc(hid_ready, 1)

                def layernorm(c, nth, src, to):
                    for i in range(2):
                        c(nc.vector.bn_stats(st6[:, i], src[:, i]))
                    c.wait()
                    for i in range(2):
                        c(nc.vector.bn_aggr(mv[:, i], st6[:, i]))
                    c.wait()
                    nc.vector.tensor_scalar(ve[:], mv[:, :, 1], 1e-5, None, ALU.add).then_inc(ve_ready, 1)
                    dve.wait_ge(rstd_ready, nth)
                    for i in range(2):
                        c(nc.vector.tensor_scalar(to[:, i], src[:, i], mv[:, i, 0:1], rstd[:, i:i + 1], ALU.subtract, ALU.mult))
                    c.wait()

                def first():
                    split(0, 0)
                    for i in range(2):
                        into_hidden(0, 0, i)
                    split(0, 2)

                def finish(c, b, t, left):
                    for i in range(2):
                        for a in range(2):
                            dve.wait_ge(hh_ready, START + b * 8 + 2 * (t + i) + a + 1)
                            nc.vector.tensor_tensor(hTl[:, 8 * a:8 * a + 8], wide[3 - 3 * a][:].rearrange("p a (c n) -> p (a c) n", n=P),
                                                    hTh[:, 8 * a:8 * a + 8].bitcast(F32), ALU.subtract).then_inc(hl_ready, 1)
                    dve.wait_ge(x2_biased, START + b * 2 + t // 2 + 1)
                    for i in range(2):
                        dve.wait_ge(out_full, after(b, t + i + 1, 1))
                        nc.vector.scalar_tensor_tensor(s[:, i], wide[1 + i][:, 0], scale[:, 1:2], x2b[:, i], ALU.mult, ALU.add).then_inc(s_ready, 1)
                    if left == 2:
                        split(b, t + 4)
                    dve.wait_ge(s_ready, after(b, t + 2, 1))
                    layernorm(c, START + b * 4 + t + 1, s, u)
                    c(nc.vector.tensor_tensor(u[:], u[:], gamma[:].unsqueeze(1).broadcast_to([P, 2, DM]), ALU.mult))
                    c.wait()
                    c(nc.vector.tensor_tensor(u[:], u[:], beta[:].unsqueeze(1).broadcast_to([P, 2, DM]), ALU.add))
                    c.wait()
                    nc.vector.tensor_tensor(u[:], u[:], xres[:, t:t + 2], ALU.add).then_inc(residual_used, 1)
                    dve.wait_ge(residual_used, START + b * 2 + t // 2 + 1)
                    dve.wait_ge(y_out[1 - t // 2], START + b * 16 + (16 if t else 0))
                    layernorm(c, START + b * 4 + t + 2, u, y)
                    dve.sem_inc(y_ready, 1)

                def pair(b, t, left):
                    c = Chain(dve, dchain)
                    for i in range(2):
                        if left:
                            into_hidden(b, t + 2, i)
                        keep_largest(c, b, t, i)
                    check_kept(c, b, t)
                    finish(c, b, t, left)
                    dve.sem_clear(dchain)

                over_pairs(dve, first, pair)

            @block.tensor
            def _(pe):
                def turn(b, t):
                    pe.wait_ge(xin_in[t // 2 % 2], START + b * 16 + (32 if t >= 4 else 16))
                    for i in range(2):
                        for k in range(DC):
                            last = nc.tensor.transpose(wide[0][:, i, P * k:P * (k + 1)], xin[:, t % 4 + i, P * k:P * (k + 1)], ident[:])
                    last.then_inc(xT_full, 1)

                def into_hidden(b, t, first=False):
                    pe.wait_ge(x2l_ready, START + b * 2 + t // 2 + 1)
                    for i in range(2):
                        for a in range(2):
                            if i:
                                pe.wait_ge(z_ready, START + b * 8 + 2 * t + a + 1)
                            elif not first:
                                pe.wait_ge(z_ready, after(b, t, 2))
                                pe.wait_ge(s_ready, after(b, t - 2, 1))
                            for h in range(2):
                                cols = slice(HALF * a + 512 * h, HALF * a + 512 * (h + 1))
                                for k in range(DC):
                                    for x in (x2h, x2l):
                                        last = nc.tensor.matmul(wide[1 + a][:, h], x[:, i, k], w_in_t[:, k, cols],
                                                                start=(k == 0 and x is x2h), stop=(k == DC - 1 and x is x2l))
                            last.then_inc(z_full, 1)

                def pair(b, t, left):
                    if left:
                        into_hidden(b, t + 2)
                    pe.wait_ge(z_ready, after(b, t + (4 if left else 2), 2))
                    pe.wait_ge(wrong_ready, START + b * 2 + t // 2 + 1)
                    nc.tensor.matmul(wide[1][:, 1, 0:1], ones[:], wrong[:, 0:1], start=True, stop=False)
                    nc.tensor.matmul(wide[1][:, 1, 0:1], ones[:], wrong[:, 1:2], start=False, stop=True).then_inc(wrong_sum, 1)
                    for i in range(2):
                        for a in range(2):
                            pe.wait_ge(hid_ready, START + b * 2 + t // 2 + 1)
                            pe.wait_ge(hl_ready, after(b, t + i, 2))
                            for k in range(8):
                                last = nc.tensor.transpose(wide[3 - 3 * a][:, k // 4, P * (k % 4):P * (k % 4 + 1)], hid[:, i, P * (8 * a + k):P * (8 * a + k + 1)], ident[:])
                            last.then_inc(hT_full, 1)
                        pe.wait_ge(hl_ready, after(b, t + i + 1, 2))
                        if i == 1 and left == 2:
                            turn(b, t + 4)
                        for k in range(FC):
                            for x in (hTh, hTl):
                                last = nc.tensor.matmul(wide[1 + i][:, 0], x[:, k], w_out_t[:, k], start=(k == 0 and x is hTh), stop=(k == FC - 1 and x is hTl))
                        last.then_inc(out_full, 1)

                def first():
                    turn(0, 0)
                    into_hidden(0, 0, first=True)
                    turn(0, 2)

                over_pairs(pe, first, pair)


def decoder_layer(nc, io, out):
    def scratch(name, shape):
        return nc.dram_tensor(name, shape, F32, kind="Internal").ap()

    tiles = BATCH * TT
    x1_dram, x2_dram = scratch("x1_scratch", [tiles, P, DM]), scratch("x2_scratch", [tiles, P, DM])
    wq_dram, wd_dram = scratch("wq_scratch", [2, P, DC, HEADS * HD]), scratch("wd_scratch", [P, CC, 2 * HEADS * HD])
    wkv_dram = scratch("wkv_scratch", [2, P, CC, 2 * HEADS * HD])
    self_attention(nc, io, x1_dram)
    cross_attention(nc, io, x1_dram, x2_dram, wq_dram, wd_dram, wkv_dram)
    sparse_ffn(nc, io, x2_dram, out)


def rotary_tables(np):
    f32 = np.float32
    inv_freq = (f32(1.0) / f32(10000.0) ** (np.arange(0, HD, 2, dtype=f32) / f32(HD))).astype(f32)
    angle = np.arange(SEQ, dtype=f32)[:, None] * inv_freq[None, :]
    angle = np.concatenate([angle, angle], axis=-1).astype(np.float64)
    sign = np.where(np.arange(HD) < HD // 2, -1.0, 1.0)
    return [by_sixteenths(np, t.astype(f32), 0) for t in (np.cos(angle), np.sin(angle) * sign)]


def by_sixteenths(np, a, axis):
    shape = a.shape
    a = a.reshape(shape[:axis] + (SEQ // 16, 4, 4) + shape[axis + 1:])
    a = np.moveaxis(a, axis, axis + 2)
    return np.ascontiguousarray(a.reshape(shape))


def kernel(**inputs):
    import numpy as np
    import concourse.bacc as bacc
    from concourse.bass_utils import run_bass_kernel_spmd

    given = {k: np.asarray(v) for k, v in inputs.items()}
    attn, cross, ffn = ({k[len(p):]: v for k, v in given.items() if k.startswith(p)} for p in ("L0_attn_", "L0_xattn_", "L0_ffn_"))
    x, ctx = given["x"], given["ctx_1024"]
    HT = HEADS * HD
    cos, sin = rotary_tables(np)
    wkv = np.concatenate([cross["Wk"], cross["Wv"]], axis=1).reshape(CDM, HEADS, 2, HD)
    bkv = np.concatenate([cross["bk"], cross["bv"]]).reshape(HEADS, 2, HD)
    is_dca = np.arange(CTX) >= MAIN
    arrays = {
        "x": x,
        "xT": by_sixteenths(np, x.transpose(0, 2, 1), 2),
        "w1T": np.concatenate([attn["Wq"], attn["Wk"], attn["Wv"]], axis=0).T,
        "b1": np.concatenate([attn["bq"], attn["bk"], attn["bv"]]),
        "woT": attn["Wo"].T,
        "a_bo": attn["bo"],
        "randT": attn["rand_matrix"].T,
        "cos": cos,
        "sin": sin,
        "ident": np.eye(P, dtype=np.float32),
        "yT": ctx.transpose(0, 2, 1),
        "c_wkv": np.concatenate([wkv[:, :, 0].reshape(CDM, HT), wkv[:, :, 1].reshape(CDM, HT)], axis=1),
        "c_bkv": np.concatenate([bkv[:, 0].reshape(HT), bkv[:, 1].reshape(HT)]),
        "c_wq": cross["Wq"],
        "c_bq": cross["bq"],
        "c_wd": cross["Wkv_dca"],
        "c_bd": cross["bkv_dca"],
        "c_wo": cross["Wo"],
        "c_bo": cross["bo"],
        "nw": np.stack([cross["qn_w"], cross["kn_w"], cross["kn_dca_w"]]),
        "nb": np.stack([cross["qn_b"], cross["kn_b"], cross["kn_dca_b"]]),
        "key_rows": np.stack([~is_dca, is_dca]).astype(np.float32),
        "dca_row": is_dca[-P:].astype(np.float32)[:, None],
        "w_synT": ffn["W_syn"].T,
        "w_outT": ffn["W_out"].T,
        "b_syn": ffn["b_syn"],
        "b_out": ffn["b_out"],
        "gamma": ffn["gamma"],
        "beta": ffn["beta"],
        "places": np.append(np.arange(8), -1).astype(np.float32),
        "bits": np.uint32(1) << np.arange(KEY_BITS - 1, -1, -1, dtype=np.uint32),
    }
    nc = bacc.Bacc("TRN2", target_bir_lowering=False, num_devices=1)
    arrays = {"in_" + k: np.ascontiguousarray(a) for k, a in arrays.items()}
    io = {k[3:]: nc.dram_tensor(k, a.shape, mybir.dt.from_np(a.dtype), kind="ExternalInput").ap() for k, a in arrays.items()}
    out = nc.dram_tensor("out", [BATCH, SEQ, DM], F32, kind="ExternalOutput").ap()
    decoder_layer(nc, io, out)
    result = run_bass_kernel_spmd(nc, [arrays], core_ids=[0])
    return result.results[0]["out"]
```

```python
import concourse.bass as bass
from concourse import mybir
from contextlib import ExitStack

F32 = mybir.dt.float32
F32R = mybir.dt.float32r
U32 = mybir.dt.uint32
ALU = mybir.AluOpType
ACT = mybir.ActivationFunctionType
AX = mybir.AxisListType

P = 128
BATCH, SEQ, DM = 4, 512, 512
TT = SEQ // P
DC = DM // P
HEADS, KV_HEADS, HD = 16, 8, 32
TURN = 6.283185
START = 1
ROUND_MAGIC = 12582912.0


class Chain:

    def __init__(self, eng, sem):
        self.eng, self.sem, self.n = eng, sem, 0

    def __call__(self, ins):
        self.n += 1
        return ins.then_inc(self.sem, 1)

    def wait(self):
        self.eng.wait_ge(self.sem, self.n)


def bank_plan(groups, slots):
    assert len(groups) % slots == 0
    return {g: (i % slots, i // slots + 1) for i, g in enumerate(groups)}


def start_counters(nc, counters):
    with nc.Block() as block:
        @block.sync
        def _(sp):
            for s in counters:
                sp.sem_inc(s, START)


def self_attention(nc, io, x1_dram):
    QKV = DM + 2 * KV_HEADS * HD
    QK_HEADS = HEADS + KV_HEADS
    FE = HD // 2
    SLOTS, USES, AHEAD = 8, 3, 2
    bank = {g: (i, 1) for i, g in enumerate((n, t) for t in range(AHEAD) for n in ("q", "kv"))}
    groups = [(n, t) for t in range(AHEAD, TT) for n in ("q", "kv")]
    groups += [(n, t) for t in range(TT) for n in ("rot0", "rot1", "proj")]
    groups += [("next", i) for i in range(2 * AHEAD)] + [("wo", t) for t in range(TT)]
    assert len(groups) == SLOTS * USES
    bank.update({g: (i % SLOTS, i // SLOTS + (2 if i % SLOTS < 2 * AHEAD else 1)) for i, g in enumerate(groups)})
    POOL_H = 7

    with ExitStack() as ctx:
        def sb(name, shape, dt=F32):
            return ctx.enter_context(nc.sbuf_tensor("sa_" + name, shape, dt))

        def sem(name):
            return ctx.enter_context(nc.semaphore("a_" + name))

        counters = []

        def counter(name):
            counters.append(sem(name))
            return counters[-1]

        ps = [ctx.enter_context(nc.psum_tensor(f"a_ps{i}", [P, 512], F32)) for i in range(SLOTS)]
        full = [counter(f"bank{i}_full") for i in range(SLOTS)]
        free = [counter(f"bank{i}_free") for i in range(SLOTS)]

        w1h, w1l = sb("w1h", [P, DC, QKV], F32R), sb("w1l", [P, DC, QKV], F32R)
        woh, wol = sb("woh", [P, DC, DM], F32R), sb("wol", [P, DC, DM], F32R)
        b1 = sb("b1", [P, QKV])
        bo = sb("bo", [P, DM])
        cosb, sinb = sb("cosb", [P, TT, HD]), sb("sinb", [P, TT, HD])
        ident = sb("ident", [P, P])
        rmat = sb("rmat", [P, 4 * FE])
        xt = sb("xt", [P, DC, SEQ])
        xth, xtl = sb("xth", [P, DC, SEQ], F32R), sb("xtl", [P, DC, SEQ], F32R)
        xres = sb("xres", [P, TT, DM])
        qkv = sb("qkv", [P, 2, QKV])
        vs = sb("vs", [P, TT, KV_HEADS * HD])
        turn = sb("turn", [P, 2, QK_HEADS * HD])
        qkr = sb("qkr", [P, TT, QK_HEADS * HD])
        sq = sb("sq", [P, QK_HEADS * HD])
        ssum = sb("ssum", [P, TT * QK_HEADS])
        rn = sb("rn", [P, TT * QK_HEADS])
        qkT = sb("qkT", [P, 6, P])
        feat = sb("feat", [P, 2, QK_HEADS * HD])
        whole = sb("whole", [P, QK_HEADS * HD])
        sc = sb("sc", [P, 2, QK_HEADS * HD])
        prod = sb("prod", [P, HEADS, KV_HEADS, HD])
        prod_v = sb("prod_v", [P, HEADS, HD, KV_HEADS])
        w1 = prod[:].rearrange("p h g d -> p (h g d)").rearrange("p (c n) -> p c n", c=DC)
        wo = xt[:]
        amat = sb("amat", [P, HEADS, KV_HEADS])
        o = sb("o", [P, DM])
        oT = sb("oT", [P, TT, DM])
        oth, otl = sb("oth", [P, TT, DM], F32R), sb("otl", [P, TT, DM], F32R)
        s = sb("s", [P, 2, DM])
        st6 = sb("st6", [P, 2, 6])
        mv = sb("mv", [P, 2, 2])
        ve = sb("ve", [P, 2])
        rstd = sb("rstd", [P, 2])
        halves = sb("halves", [P, 2])
        x1 = sb("x1", [P, 2, DM])

        w_in, const_in, xt_in, xres_in = sem("w_in"), sem("const_in"), counter("xt_in"), counter("xres_in")
        rzero = sem("rzero")
        wh_ready, w_ready = sem("wh_ready"), sem("w_ready")
        xh_ready, xl_ready = counter("xh_ready"), counter("xl_ready")
        qkv_ready, v_ready, turn_ready = counter("qkv_ready"), counter("v_ready"), counter("turn_ready")
        qkr_ready, sq_ready, sqsum_ready, norm_ready = counter("qkr_ready"), counter("sq_ready"), counter("sqsum_ready"), counter("norm_ready")
        qkT_ready, proj_done = counter("qkT_ready"), counter("proj_done")
        arg_ready, sc_ready = counter("arg_ready"), counter("sc_ready")
        prod_ready, prod_v_ready, a_ready, o_ready = counter("prod_ready"), counter("prod_v_ready"), counter("a_ready"), counter("o_ready")
        oT_ready, oh_ready, ol_ready = counter("oT_ready"), counter("oh_ready"), counter("ol_ready")
        x_biased, ve_ready, rstd_ready = counter("x_biased"), counter("ve_ready"), counter("rstd_ready")
        x1_ready, x1_out = counter("x1_ready"), [counter(f"x1_out{i}") for i in range(2)]
        dchain = sem("dchain")

        def over_batches(eng, batch):
            with eng.Fori(0, BATCH - 1) as b:
                batch(b, False)
            batch(BATCH - 1, True)

        start_counters(nc, counters)
        with nc.Block() as block:

            @block.sync
            def _(sp):
                sp.dma_start(w1, io["w1T"].rearrange("(c p) n -> p c n", p=P)).then_inc(w_in, 16)
                sp.dma_start(wo, io["woT"].rearrange("(c p) n -> p c n", p=P)).then_inc(w_in, 16)
                sp.dma_start(b1[:], io["b1"].partition_broadcast(P)).then_inc(const_in, 16)
                sp.dma_start(bo[:], io["a_bo"].partition_broadcast(P)).then_inc(const_in, 16)
                sp.dma_start(cosb[:], io["cos"].rearrange("(t p) d -> p t d", p=P)).then_inc(const_in, 16)
                sp.dma_start(sinb[:], io["sin"].rearrange("(t p) d -> p t d", p=P)).then_inc(const_in, 16)
                sp.dma_start(ident[:], io["ident"]).then_inc(const_in, 16)
                sp.wait_ge(rzero, 1)
                for j in range(4):
                    sp.dma_start(rmat[HD * j:HD * (j + 1), FE * j:FE * (j + 1)], io["randT"]).then_inc(const_in, 16)
                sp.wait_ge(w_ready, 1)
                sp.dma_start(xt[:], io["xT"][0:1].rearrange("o (c p) n -> p (o c) n", p=P)).then_inc(xt_in, 16)

                def batch(b, final):
                    if not final:
                        following = sp.snap(b + 1)
                        sp.wait_ge(xh_ready, START + b + 1)
                        sp.wait_ge(xl_ready, START + b + 1)
                        sp.dma_start(xt[:], io["xT"][bass.ds(following, 1)].rearrange("o (c p) n -> p (o c) n", p=P)).then_inc(xt_in, 16)
                    sp.wait_ge(x1_ready, START + b * TT)
                    sp.dma_start(xres[:], io["x"][bass.ds(b, 1)].rearrange("o (t p) n -> p (o t) n", p=P)).then_inc(xres_in, 16)
                    for t in range(TT):
                        sp.wait_ge(x1_ready, START + b * TT + t + 1)
                        sp.dma_start(x1_dram[bass.ds(b * TT + t, 1)].rearrange("o p n -> p (o n)"), x1[:, t % 2]).then_inc(x1_out[t % 2], 16)
                over_batches(sp, batch)
                for i in range(2):
                    sp.wait_ge(x1_out[i], START + 16 * BATCH * TT // 2)

            @block.scalar
            def _(act):
                act.wait_ge(w_in, 32)
                nc.scalar.copy(w1h[:], w1)
                nc.scalar.copy(woh[:], wo).then_inc(wh_ready, 1)
                act.wait_ge(xt_in, START + 16)
                nc.scalar.copy(xth[:], xt[:]).then_inc(xh_ready, 1)

                def batch(b, final):
                    def turned(t):
                        for i in range(2):
                            slot, use = bank[f"rot{i}", t]
                            act.wait_ge(full[slot], START + b * USES + use)
                            if i == 0:
                                act.wait_ge(proj_done, START + b * TT + t)
                            nc.scalar.copy(qkT[:, 3 * i:3 * i + 3], ps[slot][:, 0:3 * P].rearrange("p (c n) -> p c n", n=P)).then_inc(free[slot], 1)
                        act.wait_ge(free[slot], START + b * USES + use)
                        act.sem_inc(qkT_ready, 1)

                    for t in range(TT):
                        act.wait_ge(qkr_ready, START + b * TT + t + 1)
                        if t:
                            act.wait_ge(sqsum_ready, START + b * TT + t)
                        else:
                            act.wait_ge(sqsum_ready, START + b * TT)
                        nc.scalar.activation(sq[:], qkr[:, t], ACT.Square).then_inc(sq_ready, 1)
                        if t == 2:
                            turned(0)
                    act.wait_ge(sqsum_ready, START + b * TT + TT)
                    nc.scalar.activation(rn[:], ssum[:], ACT.Sqrt).then_inc(norm_ready, 1)

                    def features(t):
                        act.wait_ge(a_ready, START + b * TT + max(t - 1, 0))
                        act.wait_ge(arg_ready, START + b * TT + t + 1)
                        nc.scalar.activation(sc[:, t % 2], feat[:, t % 2], ACT.Sin, scale=TURN).then_inc(sc_ready, 1)

                    turned(1)
                    features(0)
                    turned(2)
                    features(1)
                    turned(3)
                    if not final:
                        act.wait_ge(xt_in, START + b * 16 + 32)
                        act.wait_ge(v_ready, START + b * TT + TT)
                        nc.scalar.copy(xth[:], xt[:]).then_inc(xh_ready, 1)
                    for t in range(TT):
                        if t + 2 < TT:
                            features(t + 2)
                        if t == 0:
                            act.wait_ge(x1_ready, START + b * TT)
                        act.wait_ge(oT_ready, START + b * TT + t + 1)
                        nc.scalar.copy(oth[:, t], oT[:, t]).then_inc(oh_ready, 1)

                over_batches(act, batch)

            @block.gpsimd
            def _(pool):
                pool.memset(rmat[:], 0.0).then_inc(rzero, 1)
                pool.memset(halves[:], -0.5)
                pool.wait_ge(const_in, 16 * 9)
                pool.wait_ge(w_ready, 1)
                def batch(b, final):
                    def lower_part(t):
                        pool.wait_ge(oh_ready, START + b * TT + t + 1)
                        nc.gpsimd.tensor_tensor(otl[:, t], oT[:, t], oth[:, t].bitcast(F32), ALU.subtract).then_inc(ol_ready, 1)

                    for t in range(TT):
                        pool.wait_ge(qkv_ready, START + b * TT + t + 1)
                        pool.wait_ge(qkr_ready, START + b * TT + max(t - 1, 0))
                        x3 = qkv[:, t % 2, 0:QK_HEADS * HD].rearrange("p (h d) -> p h d", d=HD)
                        o3 = turn[:, t % 2].rearrange("p (h d) -> p h d", d=HD)
                        sn = sinb[:, t].unsqueeze(1).broadcast_to([P, QK_HEADS, HD])
                        nc.gpsimd.tensor_tensor(o3[:, :, 0:FE], x3[:, :, FE:HD], sn[:, :, 0:FE], ALU.mult)
                        nc.gpsimd.tensor_tensor(o3[:, :, FE:HD], x3[:, :, 0:FE], sn[:, :, FE:HD], ALU.mult).then_inc(turn_ready, 1)

                    def feature_products(t):
                        f = sc[:, t % 2].rearrange("p (h d) -> p h d", d=HD)
                        pool.wait_ge(sc_ready, START + b * TT + t + 1)
                        pool.wait_ge(a_ready, START + b * TT + t)
                        nc.gpsimd.tensor_tensor(
                            prod[:, 0:POOL_H],
                            f[:, 0:POOL_H].unsqueeze(2).broadcast_to([P, POOL_H, KV_HEADS, HD]),
                            f[:, HEADS:].unsqueeze(1).broadcast_to([P, POOL_H, KV_HEADS, HD]), ALU.mult).then_inc(prod_ready, 1)

                    def value_products(t):
                        pool.wait_ge(a_ready, START + b * TT + t + 1)
                        pool.wait_ge(o_ready, START + b * TT + t)
                        nc.gpsimd.tensor_tensor(
                            prod_v[:, 0:POOL_H],
                            amat[:, 0:POOL_H].unsqueeze(2).broadcast_to([P, POOL_H, HD, KV_HEADS]),
                            vs[:, t].rearrange("p (g d) -> p d g", d=HD).unsqueeze(1).broadcast_to([P, POOL_H, HD, KV_HEADS]),
                            ALU.mult).then_inc(prod_v_ready, 1)

                    pool.wait_ge(xres_in, START + b * 16 + 16)
                    nc.gpsimd.tensor_tensor(xres[:], xres[:], bo[:].unsqueeze(1).broadcast_to([P, TT, DM]), ALU.add).then_inc(x_biased, 1)
                    feature_products(0)
                    for t in range(TT):
                        value_products(t)
                        if t + 1 < TT:
                            feature_products(t + 1)
                        lower_part(t)
                    for t in range(0, TT, 2):
                        pool.wait_ge(ve_ready, START + b * (TT // 2) + t // 2 + 1)
                        nc.gpsimd.tensor_tensor(rstd[:], ve[:], halves[:], ALU.pow).then_inc(rstd_ready, 1)

                over_batches(pool, batch)

            NH = HEADS - POOL_H

            def feature_products(dve, c, b, t):
                f = sc[:, t % 2].rearrange("p (h d) -> p h d", d=HD)
                dve.wait_ge(sc_ready, START + b * TT + t + 1)
                c.wait()
                c(nc.vector.tensor_tensor(
                    prod[:, POOL_H:],
                    f[:, POOL_H:HEADS].unsqueeze(2).broadcast_to([P, NH, KV_HEADS, HD]),
                    f[:, HEADS:].unsqueeze(1).broadcast_to([P, NH, KV_HEADS, HD]), ALU.mult))

            def feature_sums(dve, c, b, t):
                c.wait()
                dve.wait_ge(prod_ready, START + b * TT + t + 1)
                c(nc.vector.tensor_reduce(amat[:], prod[:], AX.X, ALU.add))
                c.wait()
                dve.sem_inc(a_ready, 1)

            def value_products(dve, c, b, t):
                c(nc.vector.tensor_tensor(
                    prod_v[:, POOL_H:],
                    amat[:, POOL_H:].unsqueeze(2).broadcast_to([P, NH, HD, KV_HEADS]),
                    vs[:, t].rearrange("p (g d) -> p d g", d=HD).unsqueeze(1).broadcast_to([P, NH, HD, KV_HEADS]), ALU.mult))

            def value_sums(dve, c, b, t):
                c.wait()
                dve.wait_ge(prod_v_ready, START + b * TT + t + 1)
                nc.vector.tensor_reduce(o[:].rearrange("p (h d) -> p h d", d=HD), prod_v[:], AX.X, ALU.add).then_inc(o_ready, 1)
                dve.wait_ge(o_ready, START + b * TT + t + 1)
                nc.vector.transpose(oT[:, t], o[:]).then_inc(oT_ready, 1)

            @block.vector
            def _(dve):
                dve.wait_ge(w_in, 32)
                dve.wait_ge(wh_ready, 1)
                nc.vector.tensor_tensor(w1l[:], w1, w1h[:].bitcast(F32), ALU.subtract)
                nc.vector.tensor_tensor(wol[:], wo, woh[:].bitcast(F32), ALU.subtract).then_inc(w_ready, 1)
                dve.wait_ge(const_in, 16 * 9)
                dve.wait_ge(xh_ready, START + 1)
                nc.vector.tensor_tensor(xtl[:], xt[:], xth[:].bitcast(F32), ALU.subtract).then_inc(xl_ready, 1)

                def batch(b, final):
                    dve.sem_clear(dchain)
                    c = Chain(dve, dchain)
                    def take(t):
                        for n, lo in (("q", 0), ("kv", 512)):
                            slot, use = bank[n, t]
                            dve.wait_ge(full[slot], START + b * USES + use)
                            c(nc.vector.tensor_tensor(qkv[:, t % 2, lo:lo + 512], ps[slot][:], b1[:, lo:lo + 512], ALU.add))
                            c.wait()
                            dve.sem_inc(free[slot], 1)
                        dve.sem_inc(qkv_ready, 1)
                        c(nc.vector.tensor_scalar(vs[:, t], qkv[:, t % 2, QK_HEADS * HD:], 1.0 / 16, None, ALU.mult))
                        c(nc.vector.tensor_tensor(qkr[:, t].rearrange("p (h d) -> p h d", d=HD),
                                                  qkv[:, t % 2, 0:QK_HEADS * HD].rearrange("p (h d) -> p h d", d=HD),
                                                  cosb[:, t].unsqueeze(1).broadcast_to([P, QK_HEADS, HD]), ALU.mult))
                        c.wait()
                        dve.sem_inc(v_ready, 1)

                    def rotate(t):
                        dve.wait_ge(turn_ready, START + b * TT + t + 1)
                        nc.vector.tensor_tensor(qkr[:, t], qkr[:, t], turn[:, t % 2], ALU.add).then_inc(qkr_ready, 1)

                    def square_sums(t):
                        dve.wait_ge(sq_ready, START + b * TT + t + 1)
                        nc.vector.tensor_reduce(ssum[:, t * QK_HEADS:(t + 1) * QK_HEADS], sq[:].rearrange("p (h d) -> p h d", d=HD),
                                                AX.X, ALU.add).then_inc(sqsum_ready, 1)

                    for t in range(TT + 2):
                        if t < TT:
                            take(t)
                        if 1 <= t <= TT:
                            rotate(t - 1)
                        if t >= 2:
                            square_sums(t - 2)
                    dve.wait_ge(norm_ready, START + b + 1)
                    c(nc.vector.tensor_scalar(rn[:], rn[:], 1e-6, None, ALU.max))
                    c.wait()
                    c(nc.vector.reciprocal(rn[:], rn[:]))
                    c.wait()
                    c(nc.vector.tensor_scalar(rn[:], rn[:], 0.15915494309189535, None, ALU.mult))

                    def feature_arguments(t):
                        slot, use = bank["proj", t]
                        f = feat[:, t % 2].rearrange("p (h d) -> p h d", d=HD)
                        dve.wait_ge(full[slot], START + b * USES + use)
                        if t >= 2:
                            dve.wait_ge(sc_ready, START + b * TT + t - 1)
                        c.wait()
                        c(nc.vector.tensor_tensor(f[:, :, 0:FE], ps[slot][:, 0:QK_HEADS * FE].rearrange("p (h d) -> p h d", d=FE),
                                                  rn[:, t * QK_HEADS:(t + 1) * QK_HEADS].unsqueeze(2).broadcast_to([P, QK_HEADS, FE]), ALU.mult))
                        c.wait()
                        dve.sem_inc(free[slot], 1)
                        c(nc.vector.tensor_scalar(f[:, :, FE:HD], f[:, :, 0:FE], 0.25, None, ALU.add))
                        c.wait()
                        c(nc.vector.tensor_scalar(whole[:], feat[:, t % 2], ROUND_MAGIC, ROUND_MAGIC, ALU.add, ALU.subtract))
                        c.wait()
                        nc.vector.tensor_tensor(feat[:, t % 2], feat[:, t % 2], whole[:], ALU.subtract).then_inc(arg_ready, 1)

                    feature_arguments(0)
                    feature_products(dve, c, b, 0)
                    feature_arguments(1)
                    for t in range(TT):
                        feature_sums(dve, c, b, t)
                        value_products(dve, c, b, t)
                        if t + 1 < TT:
                            feature_products(dve, c, b, t + 1)
                        if t == 0 and not final:
                            dve.wait_ge(xh_ready, START + b + 2)
                            nc.vector.tensor_tensor(xtl[:], xt[:], xth[:].bitcast(F32), ALU.subtract).then_inc(xl_ready, 1)
                        value_sums(dve, c, b, t)
                        if t + 2 < TT:
                            feature_arguments(t + 2)
                    dve.wait_ge(x_biased, START + b + 1)
                    for t in range(0, TT, 2):
                        for j in range(2):
                            slot, use = bank["wo", t + j]
                            dve.wait_ge(full[slot], START + b * USES + use)
                            c(nc.vector.tensor_tensor(s[:, j], ps[slot][:], xres[:, t + j], ALU.add))
                            c.wait()
                            dve.sem_inc(free[slot], 1)
                            c(nc.vector.bn_stats(st6[:, j], s[:, j]))
                        c.wait()
                        for j in range(2):
                            c(nc.vector.bn_aggr(mv[:, j], st6[:, j]))
                        c.wait()
                        nc.vector.tensor_scalar(ve[:], mv[:, :, 1], 1e-5, None, ALU.add).then_inc(ve_ready, 1)
                        dve.wait_ge(rstd_ready, START + b * (TT // 2) + t // 2 + 1)
                        for j in range(2):
                            dve.wait_ge(x1_out[j], START + (b * (TT // 2) + t // 2) * 16)
                            nc.vector.tensor_scalar(x1[:, j], s[:, j], mv[:, j, 0:1], rstd[:, j:j + 1], ALU.subtract, ALU.mult).then_inc(x1_ready, 1)
                        dve.wait_ge(x1_ready, START + b * TT + t + 2)
                    c.wait()

                over_batches(dve, batch)

            @block.tensor
            def _(pe):
                def product(slot, pairs):
                    for i, (l, r) in enumerate(pairs):
                        last = nc.tensor.matmul(ps[slot][:], l, r, start=(i == 0), stop=(i == len(pairs) - 1))
                    return last

                pe.wait_ge(const_in, 16 * 9)
                pe.wait_ge(w_ready, 1)
                def projections(b, tiles):
                    for t in tiles:
                        tok = slice(P * t, P * (t + 1))
                        for n, lo in (("q", 0), ("kv", 512)):
                            slot, use = bank[n, t]
                            pe.wait_ge(free[slot], START + b * USES + use - 1)
                            product(slot, [(x[:, k, tok], w[:, k, lo:lo + 512]) for k in range(DC)
                                           for x, w in ((xth, w1h), (xtl, w1h), (xth, w1l))]).then_inc(full[slot], 1)

                pe.wait_ge(xh_ready, START + 1)
                pe.wait_ge(xl_ready, START + 1)
                projections(0, range(AHEAD))

                def batch(b, final):
                    projections(b, range(AHEAD, TT))
                    for t in range(TT):
                        pe.wait_ge(qkr_ready, START + b * TT + t + 1)
                        for i in range(2):
                            slot, use = bank[f"rot{i}", t]
                            pe.wait_ge(free[slot], START + b * USES + use - 1)
                            for k in range(3):
                                last = nc.tensor.transpose(ps[slot][:, P * k:P * (k + 1)], qkr[:, t, P * (3 * i + k):P * (3 * i + k + 1)], ident[:])
                            last.then_inc(full[slot], 1)
                        slot, use = bank["proj", t]
                        pe.wait_ge(free[slot], START + b * USES + use - 1)
                        pe.wait_ge(qkT_ready, START + b * TT + t + 1)
                        for k in range(6):
                            last = nc.tensor.matmul(ps[slot][:, 4 * FE * k:4 * FE * (k + 1)], qkT[:, k], rmat[:], start=True, stop=True)
                        last.then_inc(full[slot], 1)
                        pe.wait_ge(full[slot], START + b * USES + use)
                        pe.sem_inc(proj_done, 1)
                    if not final:
                        pe.wait_ge(xh_ready, START + b + 2)
                        pe.wait_ge(xl_ready, START + b + 2)
                        projections(b + 1, range(AHEAD))
                    for chunks, tiles_done in ((range(DC - 1), TT - 1), ((DC - 1,), TT)):
                        for t in range(TT):
                            slot, use = bank["wo", t]
                            if tiles_done < TT:
                                pe.wait_ge(free[slot], START + b * USES + use - 1)
                            pe.wait_ge(ol_ready, START + b * TT + tiles_done)
                            for k in chunks:
                                for x, w in ((oth, woh), (otl, woh), (oth, wol)):
                                    product_end = nc.tensor.matmul(ps[slot][:], x[:, k, P * t:P * (t + 1)], w[:, k],
                                                                   start=(k == 0 and x is oth and w is woh), stop=(k == DC - 1 and w is wol))
                            if tiles_done == TT:
                                product_end.then_inc(full[slot], 1)

                over_batches(pe, batch)


CTX, CDM, DCA = 1024, 256, 16
KT_N = CTX // P
CC = CDM // P
MAIN = CTX - DCA
LAST = P - DCA
GROUP = 4
GROUPS = HEADS // GROUP
BOUND = 60.0
ROWS = 3 * HD


def cross_attention(nc, io, x1_dram, x2_dram, wq_dram, wd_dram, wkv_dram):
    HT = HEADS * HD
    TILES = TT + KT_N
    PAIRS = KT_N // 2
    Q_TURN = TT + 3

    def packed(g, kind, bounded):
        queries_first = bounded and g == 0
        return 2 * g + 1 + (kind == ("kT" if queries_first else "qT"))

    def pe_groups(bounded):
        order = []
        for t in range(TT + 1):
            order += [("x1T", t)] * (t < TT) + [("head", t - 1)] * (t > 0)
        if bounded:
            order += [("head", n) for n in range(TT, Q_TURN)] + [("qT", 0)]
            order += [("head", n) for n in range(Q_TURN, TILES)] + [("kT", 0)]
            for g in range(GROUPS):
                for kk in range(PAIRS):
                    order += [("score", g, kk, i) for i in (0, 1)]
                    order += [("qT", g + 1)] * (kk == 2 and g + 1 < GROUPS)
                    order += [("score", g, kk, i) for i in (2, 3)]
                    order += [("kT", g + 1)] * (kk == 0 and g + 1 < GROUPS)
        else:
            order += [("head", n) for n in range(TT, TILES)]
            for g in range(GROUPS):
                order += [("kT", g), ("qT", g)]
                order += [("max", g, i, t) for i in range(GROUP) for t in range(TT)]
                order += [("shift", g, j) for j in range(2)]
                order += [("score", g, kk, i) for kk in range(PAIRS) for i in range(GROUP)]
        return order + [("wo", h) for h in range(TT // 2)]

    order_of = {bounded: pe_groups(bounded) for bounded in (False, True)}
    plan_of = {bounded: (bank_plan(order_of[bounded], 2), len(order_of[bounded]) // 2) for bounded in (False, True)}
    EXPS = GROUPS * PAIRS * GROUP

    with ExitStack() as ctx:
        def sem(name):
            return ctx.enter_context(nc.semaphore("c_" + name))

        counters = []

        def counter(name):
            counters.append(sem(name))
            return counters[-1]

        def sb_in(stack):
            return lambda name, shape, dt=F32: stack.enter_context(nc.sbuf_tensor("sc_" + name, shape, dt))

        sb = sb_in(ctx)
        wide = [ctx.enter_context(nc.psum_tensor(f"c_wide{i}", [P, 2, 512], F32)) for i in range(2)]
        acc = {n: ctx.enter_context(nc.psum_tensor("c_" + n, [P, 512], F32)) for n in ("ctx_main", "sum_main", "ctx_dca", "sum_dca")}
        full = [counter(f"wide{i}_full") for i in range(2)]

        qk = sb("qk", [P, TILES, HT])
        packh, packl = sb("packh", [P, CTX + SEQ], F32R), sb("packl", [P, CTX + SEQ], F32R)
        v = sb("v", [P, KT_N, HT])
        vd = sb("vd", [P, HT])
        with ExitStack() as region:
            wqh_early, wql_early = sb_in(region)("wqh_early", [P, DC, HT], F32R), sb_in(region)("wql_early", [P, DC, HT], F32R)
        kT = sb("kT", [P, GROUP, CTX], F32R)
        with ExitStack() as region:
            yt_early = sb_in(region)("yt_early", [P, CC, CTX])
        qT = sb("qT", [P, GROUP, SEQ], F32R)
        x1_early = qk[:, TT + 4:TT + 8]
        qT2 = sb("qT2", [ROWS, GROUP, SEQ], F32R)
        with ExitStack() as region:
            wkvh, wkvl = sb_in(region)("wkvh", [P, CC, 2 * HT], F32R), sb_in(region)("wkvl", [P, CC, 2 * HT], F32R)
        kT2 = sb("kT2", [P, GROUP, CTX], F32R)
        kTs, qTs = (kT2, kT), (qT2, qT)
        outs = sb("outs", [P, 2, SEQ])
        bound_parts, bound, unbounded = sb("bound_parts", [P, 2, 3, HD]), sb("bound", [P, 2, 4]), sb("unbounded", [P, 1], U32)
        woh, wol = sb("woh", [P, DC, DM], F32R), sb("wol", [P, DC, DM], F32R)
        x1 = sb("x1", [P, TT, DM])
        ct = sb("ct", [P, 2, SEQ])
        rec = sb("rec", [P, 2, SEQ])
        bq, bkv, bkv7, bo = sb("bq", [P, HT]), sb("bkv", [P, 2 * HT]), sb("bkv7", [P, 2 * HT]), sb("bo", [P, DM])
        nw, nb = sb("nw", [P, 3, HD]), sb("nb", [P, 3, HD])
        ident = sb("ident", [P, P])
        dca_row = sb("dca_row", [P, 1])
        ones, ones_dca = sb("ones", [P, HD]), sb("ones_dca", [P, HD])
        yd = sb("yd", [P, CC, P])
        eps6, halves = sb("eps6", [P, 1]), sb("halves", [P, 2])
        ss, sd = sb("ss", [P, 2, HEADS]), sb("sd", [P, 2, HEADS])
        mx = sb("mx", [P, ROWS + HEADS * TT * 2])
        st6, mv, ve, rstd = sb("st6", [P, 2, 6]), sb("mv", [P, 2, 2]), sb("ve", [P, 2]), sb("rstd", [P, 2])
        with ExitStack() as region:
            r = sb_in(region)
            x1h, x1l = r("x1h", [P, DC, SEQ], F32R), r("x1l", [P, DC, SEQ], F32R)
            wqh, wql = r("wqh", [P, DC, HT], F32R), r("wql", [P, DC, HT], F32R)
        with ExitStack() as region:
            r = sb_in(region)
            yh, yl = r("yh", [P, CC, CTX], F32R), r("yl", [P, CC, CTX], F32R)
            yt, wd = r("yt", [P, CC, CTX]), r("wd", [P, CC, 2 * HT])
        with ExitStack() as region:
            r = sb_in(region)
            wd_late = r("wd_late", [P, CC, 2 * HT])
            r("gap", [P, CC, 2 * HT])
            yh_late, yl_late = r("yh_late", [P, CC, CTX], F32R), r("yl_late", [P, CC, CTX], F32R)
        x1_from = {False: x1, True: x1_early}
        wq_of = {False: (wqh, wql), True: (wqh_early, wql_early)}
        y_of = {False: (yt, yh, yl, wd), True: (yt_early, yh_late, yl_late, wd_late)}
        p = sb("p", [P, 2, GROUP, 2, SEQ])
        with ExitStack() as region:
            r = sb_in(region)
            raw, sq, kn = r("raw", [P, 4, HT]), r("sq", [P, 2, HT]), r("kn", [P, 2, HT])
        cth, ctl = sb("cth", [P, GROUPS, SEQ], F32R), sb("ctl", [P, GROUPS, SEQ], F32R)
        x2 = rec

        wkv_in, outs_taken, sums_taken, xres_in = counter("wkv_in"), counter("outs_taken"), counter("sums_taken"), counter("xres_in")
        norms_ready, roots_ready = sem("norms_ready"), sem("roots_ready")
        const_in, w_ready = sem("const_in"), sem("w_ready")
        x1_in, wq_in, y_in, wd_in = counter("x1_in"), counter("wq_in"), counter("y_in"), counter("wd_in")
        x1h_ready, x1l_ready, yh_ready, yl_ready, yd_ready = counter("x1h_ready"), counter("x1l_ready"), counter("yh_ready"), counter("yl_ready"), counter("yd_ready")
        raw_ready, sq_ready, ss_ready, sd_ready, unit_ready, kn_ready = (counter(n) for n in ("raw_ready", "sq_ready", "ss_ready", "sd_ready", "unit_ready", "kn_ready"))
        vd_ready = counter("vd_ready")
        packh_ready, packl_ready = counter("packh_ready"), counter("packl_ready")
        heads_in = [counter(f"head{i}_in") for i in range(GROUP)]
        v_ready, wo_taken = counter("v_ready"), counter("wo_taken")
        mx_ready, shift_ready, exp_ready, pv_done = counter("mx_ready"), counter("shift_ready"), counter("exp_ready"), counter("pv_done")
        ct_ready, ch_ready, cl_ready = counter("ct_ready"), counter("ch_ready"), counter("cl_ready")
        x1_biased, ve_ready, rstd_ready, x2_ready = counter("x1_biased"), counter("ve_ready"), counter("rstd_ready"), counter("x2_ready")
        x2_out = [counter(f"x2_out{i}") for i in range(2)]
        HEAD_DMAS = 16 * 6
        dchain, pchain = sem("dchain"), sem("pchain")
        spill, wkv_spill, split, low_ready = sem("spill"), sem("wkv_spill"), sem("split"), sem("low_ready")
        stage = qk[:].rearrange("p a n -> p (a n)")
        W = {"wkv": (CC, 2 * HT), "wo": (DC, DM), "wq": (DC, HT), "wd": (CC, 2 * HT)}
        staged = {n: stage[:, 2048 * i:2048 * (i + 1)].rearrange("p (c n) -> p c n", c=W[n][0]) for i, n in enumerate(("wkv", "wo", "wq"))}
        staged["wd"] = v[:, 0:4].rearrange("p a n -> p (a n)").rearrange("p (c n) -> p c n", c=CC)

        with nc.Block() as block:
            @block.sync
            def _(sp):
                for s in counters:
                    sp.sem_inc(s, START)
                for n in W:
                    sp.dma_start(staged[n], io["c_" + n].rearrange("(c p) n -> p c n", p=P)).then_inc(const_in, 16)
                sp.dma_start(bq[:], io["c_bq"].partition_broadcast(P)).then_inc(const_in, 16)
                sp.dma_start(bkv[:], io["c_bkv"].partition_broadcast(P)).then_inc(const_in, 16)
                sp.dma_start(bkv7[0:LAST], io["c_bkv"].partition_broadcast(LAST)).then_inc(const_in, 16)
                sp.dma_start(bkv7[LAST:P], io["c_bd"].partition_broadcast(DCA)).then_inc(const_in, 16)
                sp.dma_start(bo[:], io["c_bo"].partition_broadcast(P)).then_inc(const_in, 16)
                for t_, src in ((nw, "nw"), (nb, "nb")):
                    for k in range(2):
                        sp.dma_start(t_[:, k], io[src][k].partition_broadcast(P)).then_inc(const_in, 16)
                    sp.dma_start(t_[0:LAST, 2], io[src][1].partition_broadcast(LAST)).then_inc(const_in, 16)
                    sp.dma_start(t_[LAST:P, 2], io[src][2].partition_broadcast(DCA)).then_inc(const_in, 16)
                sp.dma_start(ident[:], io["ident"]).then_inc(const_in, 16)
                sp.dma_start(dca_row[:], io["dca_row"]).then_inc(const_in, 16)
                sp.dma_start(rec[ROWS:ROWS + 2].rearrange("p a n -> p (a n)"), io["key_rows"]).then_inc(const_in, 16)
                sp.wait_ge(split, 1)
                sp.dma_start(wq_dram[0], wqh[:].bitcast(F32)).then_inc(spill, 16)
                sp.wait_ge(w_ready, 3)
                sp.dma_start(wd_dram, staged["wd"]).then_inc(spill, 16)
                sp.wait_ge(low_ready, 1)
                sp.dma_start(wq_dram[1], wql[:].bitcast(F32)).then_inc(spill, 16)
                sp.wait_ge(split, 2)
                sp.dma_start(wkv_dram[0], wkvh[:].bitcast(F32)).then_inc(wkv_spill, 16)
                sp.wait_ge(low_ready, 2)
                sp.dma_start(wkv_dram[1], wkvl[:].bitcast(F32)).then_inc(wkv_spill, 16)
                sp.wait_ge(spill, 48)

            @block.scalar
            def _(act):
                act.wait_ge(const_in, 16 * 20)
                for i in range(GROUP):
                    nc.scalar.copy(kT[ROWS:ROWS + 2, i], rec[ROWS:ROWS + 2].rearrange("p a n -> p (a n)"))
                nc.scalar.copy(woh[:], staged["wo"])
                act.wait_ge(w_ready, 1)
                nc.scalar.copy(wqh[:], staged["wq"]).then_inc(split, 1)
                act.wait_ge(w_ready, 2)
                nc.scalar.copy(wkvh[:], staged["wkv"]).then_inc(split, 1)
                act.wait_ge(norms_ready, 1)
                nc.scalar.activation(bound[:, :, 1:3], bound[:, :, 1:3], ACT.Sqrt, scale=float(HD)).then_inc(roots_ready, 1)

            @block.gpsimd
            def _(pool):
                pool.memset(ones[:], 1.0)
                pool.memset(eps6[:], 1e-6)
                pool.memset(halves[:], -0.5)
                pool.memset(mx[:], 0.0)
                pool.memset(yd[:], 0.0)

            @block.vector
            def _(dve):
                dve.wait_ge(const_in, 16 * 20)
                c = Chain(dve, dchain)
                for k in range(2):
                    for term, (x, y) in enumerate(((nw, nw), (nw, nb), (nb, nw))):
                        c(nc.vector.tensor_tensor(bound_parts[:, k, term], x[:, 0], y[:, 1 + k], ALU.mult))
                c.wait()
                c(nc.vector.tensor_reduce(bound[:, :, 0:1], bound_parts[:, :, 0:1], AX.X, ALU.max, apply_absolute_value=True))
                for k in range(2):
                    c(nc.vector.tensor_tensor(bound_parts[:, k, 1:3], bound_parts[:, k, 1:3], bound_parts[:, k, 1:3], ALU.mult))
                c.wait()
                c(nc.vector.tensor_reduce(bound[:, :, 1:3], bound_parts[:, :, 1:3], AX.X, ALU.add))
                for k in range(2):
                    c(nc.vector.tensor_tensor(bound_parts[:, k, 0], nb[:, 0], nb[:, 1 + k], ALU.mult))
                c.wait()
                dve.sem_inc(norms_ready, 1)
                c(nc.vector.tensor_reduce(bound[:, :, 3:4], bound_parts[:, :, 0:1], AX.X, ALU.add, apply_absolute_value=True))
                c(nc.vector.tensor_scalar(bound[:, :, 0], bound[:, :, 0], float(HD), None, ALU.mult))
                c.wait()
                c(nc.vector.tensor_scalar(ones_dca[:], ident[:, 0:HD], 0.0, dca_row[:, 0:1], ALU.mult, ALU.add))
                for part, mean in ((staged["wq"], ss[:].rearrange("p a h -> p (a h)")), (staged["wkv"][:, :, 0:HT], ss[:].rearrange("p a h -> p (a h)")),
                                   (staged["wd"][:, :, 0:HT], ss[:].rearrange("p a h -> p (a h)")), (bq[:].unsqueeze(1), ss[:, 0]),
                                   (bkv[:, 0:HT].unsqueeze(1), ss[:, 0]), (bkv7[:, 0:HT].unsqueeze(1), ss[:, 0])):
                    n = part.shape[1]
                    step = min(n, 2)
                    for k in range(0, n, step):
                        w = part[:, k:k + step].rearrange("p c (h d) -> p c h d", d=HD)
                        m = mean.rearrange("p (c h) -> p c h", h=HEADS)
                        c.wait()
                        c(nc.vector.tensor_reduce(m, w, AX.X, ALU.add))
                        c.wait()
                        c(nc.vector.tensor_scalar(m, m, -1.0 / HD, None, ALU.mult))
                        c.wait()
                        c(nc.vector.tensor_tensor(w, w, m.unsqueeze(3).broadcast_to([P, step, HEADS, HD]), ALU.add))
                    if n > 1:
                        c.wait()
                        dve.sem_inc(w_ready, 1)
                dve.wait_ge(split, 2)
                nc.vector.tensor_tensor(wql[:], staged["wq"], wqh[:].bitcast(F32), ALU.subtract).then_inc(low_ready, 1)
                nc.vector.tensor_tensor(wkvl[:], staged["wkv"], wkvh[:].bitcast(F32), ALU.subtract).then_inc(low_ready, 1)
                nc.vector.tensor_tensor(wol[:], staged["wo"], woh[:].bitcast(F32), ALU.subtract).then_inc(low_ready, 1)
                dve.wait_ge(low_ready, 3)
                dve.wait_ge(roots_ready, 1)
                sums = bound_parts[:, :, 0, 0:1]
                c(nc.vector.tensor_reduce(sums, bound[:], AX.X, ALU.add))
                c.wait()
                c(nc.vector.tensor_reduce(bound_parts[:, 0, 1, 0:1], sums.rearrange("p k o -> p (k o)"), AX.X, ALU.max))
                c.wait()
                c(nc.vector.tensor_scalar(unbounded[:], bound_parts[:, 0, 1, 0:1], BOUND * HD ** 0.5, None, ALU.is_gt))
                c.wait()
                dve.sem_clear(dchain)

        def either_way(eng, batch, first=None):
            with eng.If(eng.value_load(unbounded[P - 1:P, 0:1]) > 0):
                with eng.Fori(0, BATCH) as b:
                    batch(b, False)
            with eng.Else():
                if first:
                    first()
                with eng.Fori(0, BATCH - 1) as b:
                    batch(b, True)
                batch(BATCH - 1, True, True)

        with nc.Block() as block:
            @block.sync
            def _(sp):
                def batch(b, bounded, final=False):
                    bank, USES = plan_of[bounded]
                    (yt, yh, yl, wd), (wqh, wql) = y_of[bounded], wq_of[bounded]
                    first = b * TT if final else sp.snap(b * TT)
                    if bounded:
                        sp.wait_ge(x2_ready, START + b * TT)
                        sp.dma_start(x1[:], x1_dram[bass.ds(first, TT)].rearrange("t p n -> p t n")).then_inc(xres_in, 16)
                        sp.wait_ge(raw_ready, START + b * TILES + TT)
                        sp.dma_start(wd[:], wd_dram).then_inc(wd_in, 16)
                    else:
                        sp.wait_ge(x2_ready, START + b * TT)
                        sp.dma_start(x1[:], x1_dram[bass.ds(first, TT)].rearrange("t p n -> p t n")).then_inc(x1_in, 16)
                        sp.wait_ge(pv_done, START + b * GROUPS * PAIRS)
                        sp.dma_start(wqh[:].bitcast(F32), wq_dram[0]).then_inc(wq_in, 16)
                        sp.dma_start(wql[:].bitcast(F32), wq_dram[1]).then_inc(wq_in, 16)
                        sp.wait_ge(raw_ready, START + b * TILES + TT)
                        sp.dma_start(wd[:], wd_dram).then_inc(wd_in, 16)
                        sp.dma_start(yt[:], io["yT"][bass.ds(b, 1)].rearrange("o (c p) n -> p (o c) n", p=P)).then_inc(y_in, 16)
                    sp.wait_ge(wkv_spill, 32)
                    for g in range(GROUPS):
                        k_to, q_to = (kTs[g % 2], qTs[g % 2]) if bounded else (kT, qT)
                        parts = [("kT", k_to, 0, CTX, (packh, packl, packh)), ("qT", q_to, CTX, SEQ, (packh, packh, packl))]
                        for kind, to, lo, n, packs in sorted(parts, key=lambda part: packed(g, part[0], bounded)):
                            sp.wait_ge(packl_ready, START + b * 2 * GROUPS + packed(g, kind, bounded))
                            for i in range(GROUP):
                                of = slice(HD * i, HD * (i + 1))
                                for r, pack in enumerate(packs):
                                    sp.dma_start(to[HD * r:HD * (r + 1), i].bitcast(F32), pack[of, lo:lo + n].bitcast(F32)).then_inc(heads_in[i], 16)
                    if bounded and not final:
                        load_x1(sp.snap(b * TT + TT))
                        following = sp.snap(b + 1)
                        sp.wait_ge(exp_ready, START + b * EXPS + 3 * PAIRS * GROUP)
                        sp.dma_start(wkvh[:].bitcast(F32), wkv_dram[0]).then_inc(wkv_in, 16)
                        sp.dma_start(wkvl[:].bitcast(F32), wkv_dram[1]).then_inc(wkv_in, 16)
                        sp.wait_ge(exp_ready, START + b * EXPS + 4 * PAIRS * GROUP)
                        load_early(following)
                    for t in range(TT):
                        sp.wait_ge(x2_ready, START + b * TT + t + 1)
                        sp.dma_start(x2_dram[bass.ds(b * TT + t, 1)].rearrange("o p n -> p (o n)"), x2[:, t % 2]).then_inc(x2_out[t % 2], 16)

                def load_x1(first):
                    sp.dma_start(x1_early, x1_dram[bass.ds(first, TT)].rearrange("t p n -> p t n")).then_inc(x1_in, 16)

                def load_early(b):
                    sp.dma_start(wqh_early[:].bitcast(F32), wq_dram[0]).then_inc(wq_in, 16)
                    sp.dma_start(wql_early[:].bitcast(F32), wq_dram[1]).then_inc(wq_in, 16)
                    sp.dma_start(yt_early[:], io["yT"][bass.ds(b, 1)].rearrange("o (c p) n -> p (o c) n", p=P)).then_inc(y_in, 16)

                def first():
                    load_x1(0)
                    load_early(0)

                either_way(sp, batch, first)
                for i in range(2):
                    sp.wait_ge(x2_out[i], START + 16 * BATCH * TT // 2)

            @block.scalar
            def _(act):
                def batch(b, bounded, final=False):
                    bank, USES = plan_of[bounded]
                    (yt, yh, yl, wd), (wqh, wql) = y_of[bounded], wq_of[bounded]
                    def context_in():
                        act.wait_ge(y_in, START + b * 16 + 16)
                        nc.scalar.copy(yh[:], yt[:]).then_inc(yh_ready, 1)
                        nc.scalar.copy(yd[:, :, LAST:P], yt[:, :, MAIN:CTX]).then_inc(yd_ready, 1)

                    def square(n):
                        act.wait_ge(raw_ready, START + b * TILES + n + 1)
                        act.wait_ge(ss_ready, START + b * TILES + max(n - 1, 0))
                        nc.scalar.activation(sq[:, n % 2], raw[:, n % 4], ACT.Square).then_inc(sq_ready, 1)

                    def deviation(n):
                        act.wait_ge(ss_ready, START + b * TILES + n + 1)
                        act.wait_ge(unit_ready, START + b * TILES + max(n - 1, 0))
                        nc.scalar.activation(sd[:, n % 2], ss[:, n % 2], ACT.Sqrt, bias=eps6[:, 0:1], scale=1.0 / HD).then_inc(sd_ready, 1)

                    def heads(n):
                        if n < TILES:
                            square(n)
                        if 0 <= n - 1 < TILES:
                            deviation(n - 1)

                    act.wait_ge(x1_in, START + b * 16 + 16)
                    if bounded:
                        context_in()
                    for t in range(TT + 1):
                        if t < TT:
                            slot, use = bank["x1T", t]
                            act.wait_ge(full[slot], START + b * USES + use)
                            nc.scalar.copy(x1h[:, :, P * t:P * (t + 1)], wide[slot][:, 0].rearrange("p (c n) -> p c n", n=P)).then_inc(x1h_ready, 1)
                        if t > 0:
                            heads(t - 1)
                    def pack(g, kind, lo, n):
                        for i in range(GROUP):
                            act.wait_ge(heads_in[i], START + (b * GROUPS + g) * HEAD_DMAS)
                        slot, use = bank[kind, g]
                        act.wait_ge(full[slot], START + b * USES + use)
                        nc.scalar.copy(packh[:, lo:lo + n], wide[slot][:].rearrange("p a n -> p (a n)")[:, 0:n]).then_inc(packh_ready, 1)

                    if not bounded:
                        context_in()
                    for n in range(TT, TILES + 1):
                        if bounded and n == Q_TURN:
                            pack(0, "qT", CTX, SEQ)
                        heads(n)

                    def exponentials(g, kk, heads=range(GROUP)):
                        if heads[0] == 0:
                            act.wait_ge(pv_done, START + (b * GROUPS * PAIRS + g * PAIRS + kk - 1 if g * PAIRS + kk else b * GROUPS * PAIRS))
                        for i in heads:
                            slot, use = bank["score", g, kk, i]
                            act.wait_ge(full[slot], START + b * USES + use)
                            nc.scalar.activation(p[:, kk % 2, i], wide[slot][:], ACT.Exp, scale=float(HD) ** -0.5).then_inc(exp_ready, 1)

                    def round_output(g):
                        if g == 0:
                            act.wait_ge(x2_ready, START + b * TT)
                        act.wait_ge(ct_ready, START + b * GROUPS + g + 1)
                        nc.scalar.copy(cth[:, g], ct[:, g % 2]).then_inc(ch_ready, 1)

                    def take_sums(g):
                        act.wait_ge(pv_done, START + b * GROUPS * PAIRS + PAIRS * (g + 1))
                        act.wait_ge(ct_ready, START + b * GROUPS + g)
                        if g == 0:
                            for x in x2_out:
                                act.wait_ge(x, START + b * 16 * TT // 2)
                        nc.scalar.copy(rec[:, 0], acc["sum_main"][:]).then_inc(sums_taken, 1)
                        nc.scalar.copy(rec[:, 1], acc["sum_dca"][:]).then_inc(sums_taken, 1)

                    k_part, q_part = ("kT", 0, CTX), ("qT", CTX, SEQ)
                    if bounded:
                        pack(0, *k_part)
                    for g in range(GROUPS):
                        more = bounded and g + 1 < GROUPS
                        if not bounded:
                            pack(g, *k_part)
                            pack(g, *q_part)
                            for j in range(2):
                                slot, use = bank["shift", g, j]
                                act.wait_ge(full[slot], START + b * USES + use)
                                nc.scalar.copy(qT[ROWS:ROWS + 2, 2 * j:2 * j + 2], wide[slot][ROWS:ROWS + 2]).then_inc(shift_ready, 1)
                        exponentials(g, 0)
                        if bounded and g:
                            take_sums(g - 1)
                        if more:
                            pack(g + 1, *k_part)
                        exponentials(g, 1)
                        if more:
                            exponentials(g, 2, (0, 1))
                            pack(g + 1, *q_part)
                            exponentials(g, 2, (2, 3))
                        else:
                            exponentials(g, 2)
                        if bounded and g:
                            round_output(g - 1)
                        exponentials(g, 3)
                        if not bounded:
                            take_sums(g)
                            round_output(g)
                    if bounded:
                        take_sums(GROUPS - 1)
                        round_output(GROUPS - 1)

                either_way(act, batch)

            @block.gpsimd
            def _(pool):
                def batch(b, bounded, final=False):
                    bank, USES = plan_of[bounded]
                    (yt, yh, yl, wd), (wqh, wql) = y_of[bounded], wq_of[bounded]
                    pool.sem_clear(pchain)
                    c = Chain(pool, pchain)

                    def weigh(n):
                        k = 0 if n < TT else 2 if n == TILES - 1 else 1
                        rw, kw, to = (x.rearrange("p (h d) -> p h d", d=HD) for x in (raw[:, n % 4], kn[:, n % 2], qk[:, n]))
                        pool.wait_ge(unit_ready, START + b * TILES + n + 1)
                        c(nc.gpsimd.tensor_tensor(kw, rw, nw[:, k].unsqueeze(1).broadcast_to([P, HEADS, HD]), ALU.mult))
                        c.wait()
                        nc.gpsimd.tensor_tensor(to, kw, nb[:, k].unsqueeze(1).broadcast_to([P, HEADS, HD]), ALU.add).then_inc(kn_ready, 1)

                    if bounded:
                        pool.wait_ge(yh_ready, START + b + 1)
                        nc.gpsimd.tensor_tensor(yl[:], yt[:], yh[:].bitcast(F32), ALU.subtract).then_inc(yl_ready, 1)
                    pool.wait_ge(packl_ready, START + b * 2 * GROUPS)
                    for n in range(TILES):
                        weigh(n)
                    pool.wait_ge(x1l_ready, START + b * TT + TT)
                    if bounded:
                        pool.wait_ge(xres_in, START + b * 16 + 16)
                    nc.gpsimd.tensor_tensor(x1[:], x1[:], bo[:].unsqueeze(1).broadcast_to([P, TT, DM]), ALU.add).then_inc(x1_biased, 1)
                    for g in range(GROUPS):
                        pool.wait_ge(ch_ready, START + b * GROUPS + g + 1)
                        nc.gpsimd.tensor_tensor(ctl[:, g], ct[:, g % 2], cth[:, g].bitcast(F32), ALU.subtract).then_inc(cl_ready, 1)
                    for t in range(0, TT, 2):
                        pool.wait_ge(ve_ready, START + b * (TT // 2) + t // 2 + 1)
                        nc.gpsimd.tensor_tensor(rstd[:], ve[:], halves[:], ALU.pow).then_inc(rstd_ready, 1)
                    c.wait()

                either_way(pool, batch)

            @block.vector
            def _(dve):
                def batch(b, bounded, final=False):
                    bank, USES = plan_of[bounded]
                    (yt, yh, yl, wd), (wqh, wql) = y_of[bounded], wq_of[bounded]
                    dve.sem_clear(dchain)
                    c = Chain(dve, dchain)

                    def take(n):
                        slot, use = bank["head", n]
                        dve.wait_ge(full[slot], START + b * USES + use)
                        if n < TT:
                            dve.wait_ge(kn_ready, START + b * TILES + max(n - 3, 0))
                            nc.vector.tensor_tensor(raw[:, n % 4], wide[slot][:, 0], bq[:], ALU.add).then_inc(raw_ready, 1)
                            return
                        k = n - TT
                        bias = bkv7 if k == KT_N - 1 else bkv
                        dve.wait_ge(kn_ready, START + b * TILES + n - 3)
                        nc.vector.tensor_tensor(raw[:, n % 4], wide[slot][:, 0], bias[:, 0:HT], ALU.add).then_inc(raw_ready, 1)
                        nc.vector.tensor_tensor(v[:, k], wide[slot][:, 1], bias[:, HT:2 * HT], ALU.add).then_inc(v_ready, 1)
                        if k == KT_N - 1:
                            dve.wait_ge(v_ready, START + b * KT_N + KT_N)
                            nc.vector.tensor_scalar(vd[:], v[:, k], dca_row[:, 0:1], None, ALU.mult).then_inc(vd_ready, 1)

                    def square_sum(n):
                        dve.wait_ge(sq_ready, START + b * TILES + n + 1)
                        dve.wait_ge(sd_ready, START + b * TILES + max(n - 1, 0))
                        nc.vector.tensor_reduce(ss[:, n % 2], sq[:, n % 2].rearrange("p (h d) -> p h d", d=HD), AX.X, ALU.add).then_inc(ss_ready, 1)

                    def unit(n):
                        dve.wait_ge(sd_ready, START + b * TILES + n + 1)
                        c(nc.vector.reciprocal(sd[:, n % 2], sd[:, n % 2]))
                        c.wait()
                        rw = raw[:, n % 4].rearrange("p (h d) -> p h d", d=HD)
                        nc.vector.tensor_tensor(rw, rw, sd[:, n % 2].unsqueeze(2).broadcast_to([P, HEADS, HD]), ALU.mult).then_inc(unit_ready, 1)

                    def heads(n):
                        if n < TILES:
                            take(n)
                        if 0 <= n - 1 < TILES:
                            square_sum(n - 1)
                        if 0 <= n - 2 < TILES:
                            unit(n - 2)

                    for t in range(TT + 1):
                        if t < TT:
                            slot, use = bank["x1T", t]
                            dve.wait_ge(x1h_ready, START + b * TT + t + 1)
                            nc.vector.tensor_tensor(x1l[:, :, P * t:P * (t + 1)], wide[slot][:, 0].rearrange("p (c n) -> p c n", n=P),
                                                    x1h[:, :, P * t:P * (t + 1)].bitcast(F32), ALU.subtract).then_inc(x1l_ready, 1)
                        if t > 0:
                            heads(t - 1)
                    if not bounded:
                        dve.wait_ge(yh_ready, START + b + 1)
                        nc.vector.tensor_tensor(yl[:], yt[:], yh[:].bitcast(F32), ALU.subtract).then_inc(yl_ready, 1)

                    def pack(g, a):
                        kind, lo, n = (("kT", 0, CTX), ("qT", CTX, SEQ))[a]
                        slot, use = bank[kind, g]
                        dve.wait_ge(packh_ready, START + b * 2 * GROUPS + packed(g, kind, bounded))
                        nc.vector.tensor_tensor(packl[:, lo:lo + n], wide[slot][:].rearrange("p a n -> p (a n)")[:, 0:n],
                                                packh[:, lo:lo + n].bitcast(F32), ALU.subtract).then_inc(packl_ready, 1)

                    for n in range(TT, TILES + 2):
                        heads(n)
                        if bounded and n == Q_TURN - 1:
                            pack(0, 1)

                    def maxima(g):
                        for i in range(GROUP):
                            for t in range(TT):
                                slot, use = bank["max", g, i, t]
                                at = ROWS + 2 * ((GROUP * g + i) * TT + t)
                                dve.wait_ge(full[slot], START + b * USES + use)
                                flat = wide[slot][:].rearrange("p a n -> p (a n)")
                                c(nc.vector.tensor_reduce(mx[:, at + 1:at + 2], flat[:, MAIN:CTX], AX.X, ALU.max, negate=True))
                                nc.vector.tensor_reduce(mx[:, at:at + 1], flat[:, 0:MAIN], AX.X, ALU.max, negate=True).then_inc(mx_ready, 1)

                    def divide(g, ahead):
                        dve.wait_ge(pv_done, START + b * GROUPS * PAIRS + PAIRS * (g + 1))
                        c(nc.vector.tensor_copy(outs[:, 0], acc["ctx_main"][:]))
                        c(nc.vector.tensor_copy(outs[:, 1], acc["ctx_dca"][:]))
                        c.wait()
                        dve.sem_inc(outs_taken, 1)
                        if ahead:
                            pack(g + 2, 0)
                        dve.wait_ge(sums_taken, START + b * 2 * GROUPS + 2 * g + 2)
                        c(nc.vector.reciprocal(rec[:], rec[:]))
                        if ahead:
                            pack(g + 2, 1)
                        c.wait()
                        dve.wait_ge(cl_ready, START + b * GROUPS + max(g - 1, 0))
                        c(nc.vector.tensor_tensor(outs[:], outs[:], rec[:], ALU.mult))
                        c.wait()
                        nc.vector.tensor_tensor(ct[:, g % 2], outs[:, 0], outs[:, 1], ALU.add).then_inc(ct_ready, 1)

                    if bounded:
                        pack(0, 0)
                        pack(1, 0)
                        pack(1, 1)
                        for g in range(GROUPS):
                            divide(g, g + 2 < GROUPS)
                    else:
                        for g in range(GROUPS):
                            pack(g, 0)
                            pack(g, 1)
                            maxima(g)
                            divide(g, False)
                    dve.wait_ge(ct_ready, START + b * GROUPS + GROUPS)
                    dve.wait_ge(x1_biased, START + b + 1)
                    for t in range(0, TT, 2):
                        slot, use = bank["wo", t // 2]
                        dve.wait_ge(full[slot], START + b * USES + use)
                        for j in range(2):
                            nc.vector.tensor_tensor(ct[:, j], wide[slot][:, j], x1[:, t + j], ALU.add).then_inc(wo_taken, 1)
                        for j in range(2):
                            dve.wait_ge(wo_taken, START + b * TT + t + j + 1)
                            c(nc.vector.bn_stats(st6[:, j], ct[:, j]))
                        c.wait()
                        for j in range(2):
                            c(nc.vector.bn_aggr(mv[:, j], st6[:, j]))
                        c.wait()
                        nc.vector.tensor_scalar(ve[:], mv[:, :, 1], 1e-5, None, ALU.add).then_inc(ve_ready, 1)
                        dve.wait_ge(rstd_ready, START + b * (TT // 2) + t // 2 + 1)
                        for j in range(2):
                            dve.wait_ge(x2_out[j], START + (b * (TT // 2) + t // 2) * 16)
                            nc.vector.tensor_scalar(x2[:, j], ct[:, j], mv[:, j, 0:1], rstd[:, j:j + 1],
                                                    ALU.subtract, ALU.mult).then_inc(x2_ready, 1)
                        dve.wait_ge(x2_ready, START + b * TT + t + 2)
                    c.wait()

                either_way(dve, batch)

            @block.tensor
            def _(pe):
                def product(out, pairs, first=True):
                    for i, (l, r) in enumerate(pairs):
                        last = nc.tensor.matmul(out, l, r, start=(first and i == 0), stop=(i == len(pairs) - 1))
                    return last

                def taken(bounded, kind, *at):
                    if kind == "x1T":
                        return x1l_ready, at[0] + 1, TT
                    if kind == "head":
                        return (raw_ready, at[0] + 1, TILES) if at[0] < TT else (v_ready, at[0] - TT + 1, KT_N)
                    if kind in ("kT", "qT"):
                        return packl_ready, packed(at[0], kind, bounded), 2 * GROUPS
                    if kind == "max":
                        return mx_ready, (GROUP * at[0] + at[1]) * TT + at[2] + 1, HEADS * TT
                    if kind == "shift":
                        return shift_ready, 2 * at[0] + at[1] + 1, 2 * GROUPS
                    if kind == "score":
                        return exp_ready, (at[0] * PAIRS + at[1]) * GROUP + at[2] + 1, EXPS
                    return wo_taken, 2 * (at[0] + 1), TT

                def batch(b, bounded, final=False):
                    bank, USES = plan_of[bounded]
                    (yt, yh, yl, wd), (wqh, wql) = y_of[bounded], wq_of[bounded]
                    def claim(*group):
                        order = order_of[bounded]
                        at = order.index(group)
                        what, value, per_batch = taken(bounded, *order[at - 2])
                        pe.wait_ge(what, START + (b * per_batch + (value if at >= 2 else 0)))
                        return bank[group][0]

                    def x1_turned(t):
                        slot = claim("x1T", t)
                        for k in range(DC):
                            last = nc.tensor.transpose(wide[slot][:, 0, P * k:P * (k + 1)], x1_from[bounded][:, t, P * k:P * (k + 1)], ident[:])
                        last.then_inc(full[slot], 1)

                    def queries(t):
                        slot = claim("head", t)
                        pe.wait_ge(x1l_ready, START + b * TT + t + 1)
                        tok = slice(P * t, P * (t + 1))
                        product(wide[slot][:, 0], [(x[:, k, tok], w[:, k]) for k in range(DC)
                                                   for x, w in ((x1h, wqh), (x1l, wqh), (x1h, wql))]).then_inc(full[slot], 1)

                    pe.wait_ge(x1_in, START + b * 16 + 16)
                    for t in range(TT + 1):
                        if t < TT:
                            x1_turned(t)
                        if t == 1:
                            pe.wait_ge(wq_in, START + b * 32 + 32)
                        if t > 0:
                            queries(t - 1)
                    pe.wait_ge(yh_ready, START + b + 1)
                    pe.wait_ge(yl_ready, START + b + 1)
                    if bounded:
                        pe.wait_ge(wkv_in, START + b * 32)

                    def heads_turned(g, kind, first, n):
                        slot = claim(kind, g)
                        for k in range(n):
                            last = nc.tensor.transpose(wide[slot][:, k // 4, P * (k % 4):P * (k % 4 + 1)],
                                                       qk[:, first + k, P * g:P * (g + 1)], ident[:])
                        last.then_inc(full[slot], 1)

                    k_part, q_part = ("kT", TT, KT_N), ("qT", 0, TT)
                    for k in range(KT_N):
                        if bounded and TT + k == Q_TURN:
                            pe.wait_ge(kn_ready, START + b * TILES + TT)
                            heads_turned(0, *q_part)
                        slot = claim("head", TT + k)
                        keys = LAST if k == KT_N - 1 else P
                        tok = slice(P * k, P * k + keys)
                        if k == KT_N - 1:
                            pe.wait_ge(yd_ready, START + b + 1)
                            pe.wait_ge(wd_in, START + b * 16 + 16)
                        for side in range(2):
                            cols = slice(HT * side, HT * (side + 1))
                            if k == KT_N - 1:
                                for cc in range(CC):
                                    nc.tensor.matmul(wide[slot][:, side], yd[:, cc], wd[:, cc, cols], start=(cc == 0), stop=False)
                            last = product(wide[slot][0:keys, side], [(x[:, cc, tok], w[:, cc, cols]) for cc in range(CC)
                                                                       for x, w in ((yh, wkvh), (yl, wkvh), (yh, wkvl))], k < KT_N - 1)
                        last.then_inc(full[slot], 1)


                    def maxima(g):
                        for i in range(GROUP):
                            pe.wait_ge(heads_in[i], START + (b * GROUPS + g + 1) * HEAD_DMAS)
                            for t in range(TT):
                                slot = claim("max", g, i, t)
                                for a in range(2):
                                    last = nc.tensor.matmul(wide[slot][:, a], qT[0:ROWS, i, P * t:P * (t + 1)], kT[0:ROWS, i, 512 * a:512 * (a + 1)],
                                                            start=True, stop=True)
                                last.then_inc(full[slot], 1)
                        for j in range(2):
                            slot = claim("shift", g, j)
                            pe.wait_ge(mx_ready, START + b * HEADS * TT + (GROUP * g + 2 * j + 2) * TT)
                            for i in range(2):
                                for t in range(TT):
                                    at = 2 * ((GROUP * g + 2 * j + i) * TT + t)
                                    last = nc.tensor.transpose(wide[slot][0:ROWS + 2, i, P * t:P * (t + 1)], mx[:, at:at + ROWS + 2], ident[:])
                            last.then_inc(full[slot], 1)

                    def scores(g, kk, heads):
                        for i in heads:
                            keys_t, queries_t, rows = (kTs[g % 2], qTs[g % 2], ROWS) if bounded else (kT, qT, ROWS + 2)
                            slot = claim("score", g, kk, i)
                            if kk == 0 and bounded:
                                pe.wait_ge(heads_in[i], START + (b * GROUPS + g + 1) * HEAD_DMAS)
                            elif kk == 0:
                                pe.wait_ge(shift_ready, START + b * 2 * GROUPS + 2 * g + i // 2 + 1)
                            for a in range(2):
                                k = 2 * kk + a
                                last = nc.tensor.matmul(wide[slot][:, a], keys_t[0:rows, i, P * k:P * (k + 1)], queries_t[0:rows, i], start=True, stop=True)
                            last.then_inc(full[slot], 1)

                    def values(g, kk, a):
                        k = 2 * kk + a
                        if a == 0:
                            pe.wait_ge(exp_ready, START + b * EXPS + (g * PAIRS + kk + 1) * GROUP)
                        if k == 0:
                            pe.wait_ge(outs_taken, START + b * GROUPS + g)
                            pe.wait_ge(sums_taken, START + b * 2 * GROUPS + 2 * g)
                        rows = LAST if k == KT_N - 1 else P
                        work = [("ctx_main", rows, lambda i: v[0:rows, k, HD * (GROUP * g + i):HD * (GROUP * g + i + 1)], k == 0, k == KT_N - 1),
                                ("sum_main", rows, lambda i: ones[0:rows], k == 0, k == KT_N - 1)]
                        if k == KT_N - 1:
                            work += [("ctx_dca", P, lambda i: vd[:, HD * (GROUP * g + i):HD * (GROUP * g + i + 1)], True, True),
                                     ("sum_dca", P, lambda i: ones_dca[:], True, True)]
                        for name, m, left, start, stop in work:
                            for i in range(GROUP):
                                last = nc.tensor.matmul(acc[name][HD * i:HD * (i + 1)], left(i), p[0:m, kk % 2, i, a], start=start, stop=stop,
                                                        tile_position=(0, HD * i))
                        if a:
                            last.then_inc(pv_done, 1)

                    pe.wait_ge(kn_ready, START + b * TILES + TILES)
                    pe.wait_ge(vd_ready, START + b + 1)
                    if bounded:
                        heads_turned(0, *k_part)
                        before = None
                        for g in range(GROUPS):
                            for kk in range(PAIRS):
                                scores(g, kk, (0, 1))
                                if before:
                                    values(*before, 0)
                                if kk == 2 and g + 1 < GROUPS:
                                    heads_turned(g + 1, *q_part)
                                scores(g, kk, (2, 3))
                                if before:
                                    values(*before, 1)
                                if kk == 0 and g + 1 < GROUPS:
                                    heads_turned(g + 1, *k_part)
                                before = (g, kk)
                        values(*before, 0)
                        values(*before, 1)
                    else:
                        for g in range(GROUPS):
                            heads_turned(g, *k_part)
                            heads_turned(g, *q_part)
                            maxima(g)
                            for kk in range(PAIRS + 1):
                                if kk < PAIRS:
                                    scores(g, kk, range(GROUP))
                                if kk:
                                    values(g, kk - 1, 0)
                                    values(g, kk - 1, 1)
                    for groups, wait_for in ((range(GROUPS - 1), GROUPS - 1), ((GROUPS - 1,), GROUPS)):
                        for h in range(TT // 2):
                            slot = claim("wo", h) if wait_for < GROUPS else bank["wo", h][0]
                            pe.wait_ge(cl_ready, START + b * GROUPS + wait_for)
                            for j in range(2):
                                tok = slice(P * (2 * h + j), P * (2 * h + j + 1))
                                for k in groups:
                                    for x, w in ((cth, woh), (ctl, woh), (cth, wol)):
                                        last = nc.tensor.matmul(wide[slot][:, j], x[:, k, tok], w[:, k], start=(k == 0 and x is cth and w is woh),
                                                                stop=(k == GROUPS - 1 and w is wol))
                            if wait_for == GROUPS:
                                last.then_inc(full[slot], 1)

                either_way(pe, batch)


FF = 2048
KEEP = 204
FC = FF // P
KEY_BITS = 31
AIM = 200
START_SIGMAS = 1.2831
DENSITY = 358.7
STEP_GAINS = (0.96, 0.78, 0.7, 0.52, 0.35)
COUNTS = len(STEP_GAINS) + 1
SEARCH = [(0, 0), (1, 0), (0, 1), (1, 1)] + [(r, i) for r in range(2, COUNTS) for i in range(2)]


def sparse_ffn(nc, io, x2_dram, out):
    HALF = FF // 2
    with ExitStack() as ctx:
        def sb(name, shape, dt=F32):
            return ctx.enter_context(nc.sbuf_tensor("sf_" + name, shape, dt))

        def sem(name):
            return ctx.enter_context(nc.semaphore("f_" + name))

        counters = []

        def counter(name):
            counters.append(sem(name))
            return counters[-1]

        wide = [ctx.enter_context(nc.psum_tensor(f"f_wide{i}", [P, 2, 512], F32)) for i in range(4)]

        w_in_t = sb("w_in_t", [P, DC, FF], F32R)
        w_out_t = sb("w_out_t", [P, FC, DM], F32R)
        b_syn, b_out, gamma, beta = sb("b_syn", [P, FF]), sb("b_out", [P, DM]), sb("gamma", [P, DM]), sb("beta", [P, DM])
        ident, ones = sb("ident", [P, P]), sb("ones", [P, P])
        bits = sb("bits", [P, KEY_BITS], U32)
        places = sb("places", [P, 9])
        parts, total = sb("parts", [P, 2, 64]), sb("total", [P, 2])
        scale, limit, low_limit = sb("scale", [P, 2]), sb("limit", [P, 2]), sb("low_limit", [P, 2])
        square_sums = sb("square_sums", [P, 10])
        spread, bias_spread = sb("spread", [P, 1]), sb("bias_spread", [P, 1])
        first_guess = sb("first_guess", [P, 1])
        gains = sb("gains", [P, COUNTS - 1])
        halves, aim = sb("halves", [P, 2]), sb("aim", [P, 1])
        xin, xres, x2b = sb("xin", [P, TT, DM]), sb("xres", [P, TT, DM]), sb("x2b", [P, 2, DM])
        z = sb("z", [P, TT, FF])
        guess = sb("guess", [P, 2, 1])
        above = sb("above", [P, 2, 1])
        miss, far, step = sb("miss", [P, 1]), sb("far", [P, 1]), sb("step", [P, 1])
        top = sb("top", [P, 2, 9])
        place, chosen = sb("place", [P, 2, 1]), sb("chosen", [P, 2, 9])
        cut = sb("cut", [P, 2, 1])
        kept, wrong = sb("kept", [P, 2]), sb("wrong", [P, 2])
        any_wrong = sb("any_wrong", [P, 1], U32)
        key, trial = sb("key", [P, 1], U32), sb("trial", [P, 1], U32)
        count = sb("count", [P, 1])
        enough = sb("enough", [P, 1], U32)
        st6, mv, ve, rstd = sb("st6", [P, 2, 6]), sb("mv", [P, 2, 2]), sb("ve", [P, 2]), sb("rstd", [P, 2])
        with ExitStack() as region:
            w_raw = region.enter_context(nc.sbuf_tensor("sf_w_raw", [P, 4 * FF], F32))
            sign = region.enter_context(nc.sbuf_tensor("sf_sign", [P, 2, FF], F32))
        x2h, x2l = sb("x2h", [P, 2, DC, P], F32R), sb("x2l", [P, 2, DC, P], F32R)
        hid = sb("hid", [P, 2, FF])
        hTh, hTl = sb("hTh", [P, 2, FC, P], F32R), sb("hTl", [P, 2, FC, P], F32R)
        s, y = sb("s", [P, 2, DM]), sb("y", [P, 2, DM])
        unused = sb("unused", [P, 2, FF], mybir.dt.bfloat16)

        const_in, w_in = sem("const_in"), [sem(f"w{i}_in") for i in range(2)]
        ones_ready, part_ready, total_ready, signs_ready = sem("ones_ready"), sem("part_ready"), sem("total_ready"), sem("signs_ready")
        abs_ready = sem("abs_ready")
        squares_ready, sums_ready, spread_ready, root_ready = sem("squares_ready"), sem("sums_ready"), sem("spread_ready"), sem("root_ready")
        xin_in = [counter(f"xin{h}_in") for h in range(2)]
        xres_in = [counter(f"xres{h}_in") for h in range(2)]
        y_out = [counter(f"y{h}_out") for h in range(2)]
        (xT_full, x2h_ready, x2l_ready, z_full, z_ready, counted, stepped, tried, kept_ready, wrong_ready, wrong_sum,
         hid_ready, hT_full, hh_ready, hl_ready, out_full, s_ready, x2_biased, ve_ready, rstd_ready, residual_used,
         y_ready) = (counter(n) for n in (
             "xT_full", "x2h_ready", "x2l_ready", "z_full", "z_ready", "counted", "stepped", "tried", "kept_ready", "wrong_ready",
             "wrong_sum", "hid_ready", "hT_full", "hh_ready", "hl_ready", "out_full", "s_ready", "x2_biased", "ve_ready",
             "rstd_ready", "residual_used", "y_ready"))
        dchain, pchain = sem("dchain"), sem("pchain")

        raw = (w_raw[:], z[:].rearrange("p t n -> p (t n)"))

        with nc.Block() as block:
            @block.sync
            def _(sp):
                for c in counters:
                    sp.sem_inc(c, START)
                sp.sem_inc(residual_used, 1)
                sp.dma_start(w_raw[:].rearrange("p (c n) -> p c n", c=DC), io["w_synT"].rearrange("(c p) n -> p c n", p=P)).then_inc(w_in[0], 16)
                for t_, n in ((b_syn, "b_syn"), (b_out, "b_out"), (gamma, "gamma"), (beta, "beta"), (places, "places"), (bits, "bits")):
                    sp.dma_start(t_[:], io[n].partition_broadcast(P)).then_inc(const_in, 16)
                sp.dma_start(ident[:], io["ident"]).then_inc(const_in, 16)
                sp.dma_start(raw[1].rearrange("p (c n) -> p c n", c=FC), io["w_outT"].rearrange("(c p) n -> p c n", p=P)).then_inc(w_in[1], 16)
                sp.wait_ge(const_in, 16 * 7)

            @block.gpsimd
            def _(pool):
                pool.memset(halves[:], -0.5)
                pool.memset(aim[:], float(FF - 2 * AIM))
                pool.memset(ones[:], 1.0).then_inc(ones_ready, 1)

            @block.scalar
            def _(act):
                unused = wide[3][:].rearrange("p a n -> p (a n)")
                act.wait_ge(w_in[1], 16)
                for a in range(8):
                    if a:
                        act.wait_ge(abs_ready, a)
                    nc.scalar.activation(unused, raw[1][:, HALF * a:HALF * (a + 1)], ACT.Abs, accum_out=parts[:, 1, a:a + 1]).then_inc(abs_ready, 1)
                act.wait_ge(abs_ready, 8)
                for a in range(8):
                    act.wait_ge(signs_ready, a // 2 + 1)
                    if a:
                        act.wait_ge(squares_ready, a)
                    nc.scalar.activation(unused, w_in_t[:, a // 2, HALF * (a % 2):HALF * (a % 2 + 1)].bitcast(F32), ACT.Square,
                                         accum_out=square_sums[:, a:a + 1]).then_inc(squares_ready, 1)
                act.wait_ge(const_in, 16 * 7)
                for a in range(2):
                    act.wait_ge(squares_ready, 8 + a)
                    nc.scalar.activation(unused, b_syn[:, HALF * a:HALF * (a + 1)], ACT.Square, accum_out=square_sums[:, 8 + a:9 + a]).then_inc(squares_ready, 1)
                act.wait_ge(spread_ready, 1)
                nc.scalar.activation(spread[:], spread[:], ACT.Sqrt).then_inc(root_ready, 1)

            @block.tensor
            def _(pe):
                pe.wait_ge(ones_ready, 1)
                for k in range(2):
                    pe.wait_ge(part_ready, k + 1)
                    nc.tensor.matmul(wide[k][:, 0, 0:1], ones[:], total[:, k:k + 1], start=True, stop=True).then_inc(total_ready, 1)
                pe.wait_ge(squares_ready, 8)
                nc.tensor.matmul(wide[2][:, 0, 0:8], ones[:], square_sums[:, 0:8], start=True, stop=True).then_inc(sums_ready, 1)

            @block.vector
            def _(dve):
                c = Chain(dve, dchain)
                for k, dst in enumerate((w_in_t[:].rearrange("p c n -> p (c n)"), w_out_t[:].rearrange("p c n -> p (c n)"))):
                    dve.wait_ge(w_in[k], 16)
                    if k == 0:
                        c(nc.vector.tensor_reduce(parts[:, 0], raw[0].rearrange("p (a n) -> p a n", a=64), AX.X, ALU.add, apply_absolute_value=True))
                        c.wait()
                    else:
                        dve.wait_ge(abs_ready, 8)
                    nc.vector.tensor_reduce(total[:, k:k + 1], parts[:, k, 0:(64, 8)[k]], AX.X, ALU.add).then_inc(part_ready, 1)
                    dve.wait_ge(total_ready, k + 1)
                    c(nc.vector.tensor_scalar(scale[:, k:k + 1], wide[k][:, 0, 0:1], 1.0 / (FF * DM), None, ALU.mult))
                    c.wait()
                    c(nc.vector.tensor_scalar(limit[:, k:k + 1], scale[:, k:k + 1], 1e-8, 0.5, ALU.add, ALU.mult))
                    c.wait()
                    c(nc.vector.tensor_scalar(low_limit[:, k:k + 1], limit[:, k:k + 1], -1.0, None, ALU.mult))
                    c(nc.vector.tensor_scalar(scale[:, k:k + 1], scale[:, k:k + 1], -1.0, None, ALU.mult))
                    for a in range(4):
                        part = slice(FF * a, FF * (a + 1))
                        c.wait()
                        if a >= 2:
                            dve.wait_ge(signs_ready, 4 * k + a - 1)
                        c(nc.vector.tensor_scalar(sign[:, a % 2], raw[k][:, part], limit[:, k:k + 1], None, ALU.is_gt))
                        c.wait()
                        nc.vector.scalar_tensor_tensor(dst[:, part], raw[k][:, part], low_limit[:, k:k + 1], sign[:, a % 2], ALU.is_lt, ALU.subtract).then_inc(signs_ready, 1)
                dve.wait_ge(sums_ready, 1)
                c(nc.vector.tensor_reduce(spread[:], wide[2][:, 0, 0:8], AX.X, ALU.add))
                c.wait()
                dve.wait_ge(squares_ready, 10)
                for factor in (scale[:, 0:1], scale[:, 0:1]):
                    c(nc.vector.tensor_scalar(spread[:], spread[:], factor, None, ALU.mult))
                    c.wait()
                for a in range(2):
                    c(nc.vector.tensor_tensor(spread[:], spread[:], square_sums[:, 8 + a:9 + a], ALU.add))
                    c.wait()
                nc.vector.tensor_scalar(spread[:], spread[:], 1.0 / FF, None, ALU.mult).then_inc(spread_ready, 1)
                dve.wait_ge(root_ready, 1)
                c(nc.vector.tensor_scalar(first_guess[:], spread[:], -START_SIGMAS, None, ALU.mult))
                for i, gain in enumerate(STEP_GAINS):
                    c(nc.vector.tensor_scalar(gains[:, i:i + 1], spread[:], -gain / (2 * DENSITY), None, ALU.mult))
                c.wait()
                dve.wait_ge(signs_ready, 8)
                dve.sem_clear(dchain)

        def after(b, t, per_tile):
            return START + b * (TT * per_tile) + t * per_tile

        def over_pairs(eng, first, pair, last=None):
            first()
            pair(0, 0, 2)
            with eng.Fori(0, BATCH - 2) as b:
                pair(b, 2, 2)
                pair(b, 4, 2)
            pair(BATCH - 2, 2, 2)
            pair(BATCH - 1, 0, 1)
            pair(BATCH - 1, 2, 0)
            if last:
                last()

        def pair_before(b, t):
            return (b, t - 2) if t else (b - 1, t + 2)

        with nc.Block() as block:
            @block.sync
            def _(sp):
                def load(to, first, slot, done):
                    sp.dma_start(to[:, slot:slot + 2], x2_dram[bass.ds(first, 2)].rearrange("t p n -> p t n")).then_inc(done[slot // 2], 16)

                def now(value):
                    return value if isinstance(value, int) else sp.snap(value)

                def store(b, t):
                    of = now(b + t // TT)
                    sp.wait_ge(y_ready, START + b * 2 + t // 2 + 1)
                    sp.dma_start(out[bass.ds(of, 1), t % TT * P:(t % TT + 2) * P].rearrange("o (t p) n -> p (o t) n", p=P), y[:]).then_inc(y_out[t // 2 % 2], 16)

                def pair(b, t, left):
                    tile = now(b * TT + t)
                    ahead = now(b * TT + t + TT)
                    if left == 2:
                        sp.wait_ge(xT_full, START + b * 2 + t // 2 + 1)
                        load(xin, ahead, t % TT, xin_in)
                    sp.wait_ge(residual_used, START + b * 2 + t // 2)
                    load(xres, tile, t % TT, xres_in)
                    if t or not isinstance(b, int) or b:
                        store(*pair_before(b, t))

                def first():
                    load(xin, 0, 0, xin_in)
                    load(xin, 2, 2, xin_in)

                over_pairs(sp, first, pair, lambda: store(BATCH - 1, 2))
                for i in range(2):
                    sp.wait_ge(y_out[i], START + 16 * BATCH)

            @block.scalar
            def _(act):
                def split(b, t):
                    act.wait_ge(xT_full, START + b * 2 + t // 2 + 1)
                    act.wait_ge(z_full, after(b, t, 2))
                    nc.scalar.copy(x2h[:], wide[0][:].rearrange("p t (c n) -> p t c n", n=P)).then_inc(x2h_ready, 1)

                def counts(b, t, some):
                    for r, i in some:
                        if r == 0:
                            act.wait_ge(z_ready, after(b, t + i + 1, 2))
                            if t or i or not isinstance(b, int):
                                act.wait_ge(kept_ready, after(b, t + i - 1, 1))
                            bias = first_guess[:]
                        else:
                            act.wait_ge(stepped, START + b * 20 + t * 5 + SEARCH.index((r - 1, i)) + 1)
                            bias = guess[:, i]
                        nc.scalar.activation(unused[:, i], z[:, t % TT + i], ACT.Sign, bias=bias, accum_out=above[:, i]).then_inc(counted, 1)

                def turned(b, t):
                    act.wait_ge(out_full, after(b, t, 1))
                    for i in range(2):
                        for a in range(2):
                            act.wait_ge(hT_full, START + b * 8 + 2 * (t + i) + a + 1)
                            nc.scalar.copy(hTh[:, i, 8 * a:8 * a + 8], wide[3 - 3 * a][:].rearrange("p a (c n) -> p (a c) n", n=P)).then_inc(hh_ready, 1)

                def first():
                    split(0, 0)
                    counts(0, 0, SEARCH[:4])
                    split(0, 2)
                    counts(0, 0, SEARCH[4:])

                def pair(b, t, left):
                    for i in range(2):
                        act.wait_ge(tried, after(b, t + i + 1, 1))
                        nc.scalar.activation(unused[:, i], hid[:, i], ACT.Sign, accum_out=kept[:, i:i + 1]).then_inc(kept_ready, 1)
                        if left:
                            counts(b, t + 2, (SEARCH[0:2], SEARCH[2:3])[i])
                    turned(b, t)
                    if left:
                        counts(b, t + 2, SEARCH[3:8])
                    if left == 2:
                        split(b, t + 4)
                    if left:
                        counts(b, t + 2, SEARCH[8:])

                over_pairs(act, first, pair)

            @block.gpsimd
            def _(pool):
                def steps(c, b, t, some):
                    for r, i in some:
                        pool.wait_ge(counted, START + b * 24 + t * 6 + SEARCH.index((r, i)) + 1)
                        c(nc.gpsimd.tensor_tensor(miss[:], above[:, i], aim[:], ALU.add))
                        c.wait()
                        c(nc.gpsimd.tensor_tensor(far[:], miss[:], miss[:], ALU.mult))
                        c.wait()
                        c(nc.gpsimd.tensor_scalar(far[:], far[:], 64.5, None, ALU.is_gt))
                        c.wait()
                        c(nc.gpsimd.tensor_tensor(step[:], far[:], miss[:], ALU.mult))
                        c.wait()
                        c(nc.gpsimd.tensor_tensor(step[:], step[:], gains[:, r:r + 1], ALU.mult))
                        c.wait()
                        c(nc.gpsimd.tensor_tensor(guess[:, i], step[:], first_guess[:] if r == 0 else guess[:, i], ALU.add))
                        c.wait()
                        pool.sem_inc(stepped, 1)

                def root(b, t, n):
                    pool.wait_ge(ve_ready, START + b * 4 + t + n + 1)
                    nc.gpsimd.tensor_tensor(rstd[:], ve[:], halves[:], ALU.pow).then_inc(rstd_ready, 1)

                def pair(b, t, left):
                    c = Chain(pool, pchain)
                    behind = pair_before(b, t) if t or not isinstance(b, int) or b else None
                    pool.wait_ge(s_ready, after(b, t, 1))
                    pool.wait_ge(xres_in[t // 2 % 2], START + b * 16 + t // TT * 16 + 16)
                    nc.gpsimd.tensor_tensor(x2b[:], xres[:, t % TT:t % TT + 2], b_out[:].unsqueeze(1).broadcast_to([P, 2, DM]), ALU.add).then_inc(x2_biased, 1)
                    if left:
                        steps(c, b, t + 2, SEARCH[:3])
                    if behind:
                        root(*behind, 0)
                    if left:
                        steps(c, b, t + 2, SEARCH[3:6])
                    if behind:
                        root(*behind, 1)
                    if left:
                        steps(c, b, t + 2, SEARCH[6:-2])
                    pool.sem_clear(pchain)

                def last():
                    root(BATCH - 1, 2, 0)
                    root(BATCH - 1, 2, 1)

                def first():
                    steps(Chain(pool, pchain), 0, 0, SEARCH[:-2])
                    pool.sem_clear(pchain)

                over_pairs(pool, first, pair, last)

            @block.vector
            def _(dve):
                def split(b, t):
                    dve.wait_ge(x2h_ready, START + b * 2 + t // 2 + 1)
                    nc.vector.tensor_tensor(x2l[:], wide[0][:].rearrange("p t (c n) -> p t c n", n=P), x2h[:].bitcast(F32), ALU.subtract).then_inc(x2l_ready, 1)

                def into_hidden(b, t, i):
                    for a in range(2):
                        cols = slice(HALF * a, HALF * (a + 1))
                        dve.wait_ge(z_full, START + b * 8 + 2 * (t + i) + a + 1)
                        nc.vector.scalar_tensor_tensor(z[:, t % TT + i, cols], wide[1 + a][:].rearrange("p a n -> p (a n)"), scale[:, 0:1],
                                                       b_syn[:, cols], ALU.mult, ALU.add).then_inc(z_ready, 1)

                def search_bits(t):
                    for i in range(2):
                        nc.vector.memset(key[:], 0).then_inc(dchain, 1)
                        dve.wait_ge(dchain, 1)
                        dve.sem_clear(dchain)
                        with dve.Fori(0, KEY_BITS) as k:
                            nc.vector.tensor_tensor(trial[:], key[:], bits[:, bass.ds(k, 1)], ALU.bitwise_or).then_inc(dchain, 1)
                            dve.wait_ge(dchain, 1)
                            nc.vector.tensor_scalar(hid[:, i], z[:, t % TT + i], trial[:].bitcast(F32), None, ALU.is_ge, ALU.add, accum_out=count[:]).then_inc(dchain, 1)
                            dve.wait_ge(dchain, 2)
                            nc.vector.tensor_scalar(enough[:], count[:], KEEP - 0.5, None, ALU.is_ge).then_inc(dchain, 1)
                            dve.wait_ge(dchain, 3)
                            nc.vector.copy_predicated(key[:], enough[:], trial[:]).then_inc(dchain, 1)
                            dve.wait_ge(dchain, 4)
                            dve.sem_clear(dchain)
                        zt = z[:, t % TT + i]
                        nc.vector.scalar_tensor_tensor(hid[:, i], zt, key[:].bitcast(F32), zt, ALU.is_ge, ALU.mult).then_inc(dchain, 1)
                        dve.wait_ge(dchain, 1)
                        dve.sem_clear(dchain)

                def keep_largest(c, b, t, i):
                    zt = z[:, t % TT + i]
                    dve.wait_ge(counted, START + b * 24 + t * 6 + 10 + i + 1)
                    c(nc.vector.tensor_scalar(top[:, i, 8:9], guess[:, i], -1.0, None, ALU.mult))
                    c(nc.vector.tensor_scalar(place[:, i], above[:, i], -0.5, KEEP - 1 - FF / 2, ALU.mult, ALU.add))
                    c.wait()
                    c(nc.vector.scalar_tensor_tensor(hid[:, i], zt, top[:, i, 8:9], zt, ALU.is_lt, ALU.mult))
                    c.wait()
                    c(nc.vector.max(top[:, i, 0:8], hid[:, i]))
                    c.wait()
                    c(nc.vector.scalar_tensor_tensor(chosen[:, i], places[:], place[:, i], top[:, i], ALU.is_equal, ALU.mult))
                    c.wait()
                    c(nc.vector.tensor_reduce(cut[:, i], chosen[:, i], AX.X, ALU.add))
                    c.wait()
                    c(nc.vector.scalar_tensor_tensor(hid[:, i], zt, cut[:, i], zt, ALU.is_ge, ALU.mult))
                    c.wait()
                    dve.sem_inc(tried, 1)

                def check_kept(c, b, t):
                    dve.wait_ge(kept_ready, after(b, t + 2, 1))
                    c(nc.vector.tensor_scalar(wrong[:], kept[:], float(KEEP), None, ALU.not_equal))
                    c.wait()
                    dve.sem_inc(wrong_ready, 1)
                    dve.wait_ge(wrong_sum, START + b * 2 + t // 2 + 1)
                    c(nc.vector.tensor_copy(any_wrong[:], wide[1][:, 1, 0:1]))
                    c.wait()
                    dve.sem_clear(dchain)
                    c.n = 0
                    rows = dve.value_load(any_wrong[0:1, 0:1])
                    with dve.If(rows > 0):
                        search_bits(t)
                    dve.sem_inc(hid_ready, 1)

                def layernorm(c, nth, src, to):
                    for i in range(2):
                        c(nc.vector.bn_stats(st6[:, i], src[:, i]))
                    c.wait()
                    for i in range(2):
                        c(nc.vector.bn_aggr(mv[:, i], st6[:, i]))
                    c.wait()
                    nc.vector.tensor_scalar(ve[:], mv[:, :, 1], 1e-5, None, ALU.add).then_inc(ve_ready, 1)
                    dve.wait_ge(rstd_ready, nth)
                    for i in range(2):
                        c(nc.vector.tensor_scalar(to[:, i], src[:, i], mv[:, i, 0:1], rstd[:, i:i + 1], ALU.subtract, ALU.mult))
                    c.wait()

                def first():
                    split(0, 0)
                    for i in range(2):
                        into_hidden(0, 0, i)
                    split(0, 2)

                def lower_parts(b, t):
                    for i in range(2):
                        for a in range(2):
                            dve.wait_ge(hh_ready, START + b * 8 + 2 * (t + i) + a + 1)
                            nc.vector.tensor_tensor(hTl[:, i, 8 * a:8 * a + 8], wide[3 - 3 * a][:].rearrange("p a (c n) -> p (a c) n", n=P),
                                                    hTh[:, i, 8 * a:8 * a + 8].bitcast(F32), ALU.subtract).then_inc(hl_ready, 1)

                def take_out(b, t):
                    dve.wait_ge(x2_biased, START + b * 2 + t // 2 + 1)
                    for i in range(2):
                        dve.wait_ge(out_full, after(b, t + i + 1, 1))
                        nc.vector.scalar_tensor_tensor(s[:, i], wide[1 + i][:, 0], scale[:, 1:2], x2b[:, i], ALU.mult, ALU.add).then_inc(s_ready, 1)

                def normalise(c, b, t):
                    dve.wait_ge(s_ready, after(b, t + 2, 1))
                    layernorm(c, START + b * 4 + t + 1, s, s)
                    c(nc.vector.tensor_tensor(s[:], s[:], gamma[:].unsqueeze(1).broadcast_to([P, 2, DM]), ALU.mult))
                    c.wait()
                    c(nc.vector.tensor_tensor(s[:], s[:], beta[:].unsqueeze(1).broadcast_to([P, 2, DM]), ALU.add))
                    c.wait()
                    nc.vector.tensor_tensor(s[:], s[:], xres[:, t % TT:t % TT + 2], ALU.add).then_inc(residual_used, 1)
                    dve.wait_ge(residual_used, START + b * 2 + t // 2 + 2)
                    dve.wait_ge(y_out[(t // 2 - 1) % 2], START + b * 16 + ((t // 2 - 1) // 2 + 1) * 16)
                    layernorm(c, START + b * 4 + t + 2, s, y)
                    dve.sem_inc(y_ready, 1)

                def pair(b, t, left):
                    c = Chain(dve, dchain)
                    for i in range(2):
                        keep_largest(c, b, t, i)
                        if left:
                            into_hidden(b, t + 2, i)
                    check_kept(c, b, t)
                    lower_parts(b, t)
                    if t or not isinstance(b, int) or b:
                        normalise(c, *pair_before(b, t))
                    take_out(b, t)
                    if left == 2:
                        split(b, t + 4)
                    c.wait()
                    dve.sem_clear(dchain)

                def last():
                    normalise(Chain(dve, dchain), BATCH - 1, 2)
                    dve.sem_clear(dchain)

                over_pairs(dve, first, pair, last)

            @block.tensor
            def _(pe):
                def turn(b, t):
                    pe.wait_ge(xin_in[t // 2 % 2], START + b * 16 + t // TT * 16 + 16)
                    for i in range(2):
                        for k in range(DC):
                            last = nc.tensor.transpose(wide[0][:, i, P * k:P * (k + 1)], xin[:, t % TT + i, P * k:P * (k + 1)], ident[:])
                    last.then_inc(xT_full, 1)

                def into_hidden(b, t, first=False):
                    pe.wait_ge(x2l_ready, START + b * 2 + t // 2 + 1)
                    for i in range(2):
                        for a in range(2):
                            if i:
                                pe.wait_ge(z_ready, START + b * 8 + 2 * t + a + 1)
                            elif not first:
                                pe.wait_ge(z_ready, after(b, t, 2))
                                pe.wait_ge(s_ready, after(b, t - 2, 1))
                            for h in range(2):
                                cols = slice(HALF * a + 512 * h, HALF * a + 512 * (h + 1))
                                for k in range(DC):
                                    for x in (x2h, x2l):
                                        last = nc.tensor.matmul(wide[1 + a][:, h], x[:, i, k], w_in_t[:, k, cols],
                                                                start=(k == 0 and x is x2h), stop=(k == DC - 1 and x is x2l))
                            last.then_inc(z_full, 1)

                def pair(b, t, left):
                    if left:
                        into_hidden(b, t + 2)
                    pe.wait_ge(z_ready, after(b, t + (4 if left else 2), 2))
                    pe.wait_ge(wrong_ready, START + b * 2 + t // 2 + 1)
                    nc.tensor.matmul(wide[1][:, 1, 0:1], ones[:], wrong[:, 0:1], start=True, stop=False)
                    nc.tensor.matmul(wide[1][:, 1, 0:1], ones[:], wrong[:, 1:2], start=False, stop=True).then_inc(wrong_sum, 1)
                    pe.wait_ge(hid_ready, START + b * 2 + t // 2 + 1)
                    for i in range(3):
                        if i < 2:
                            pe.wait_ge(hl_ready, after(b, t + i, 2))
                            for a in range(2):
                                for k in range(8):
                                    last = nc.tensor.transpose(wide[3 - 3 * a][:, k // 4, P * (k % 4):P * (k % 4 + 1)], hid[:, i, P * (8 * a + k):P * (8 * a + k + 1)], ident[:])
                                last.then_inc(hT_full, 1)
                        if i:
                            pe.wait_ge(hl_ready, after(b, t + i, 2))
                            if i == 2 and left == 2:
                                turn(b, t + 4)
                            for k in range(FC):
                                for x in (hTh, hTl):
                                    last = nc.tensor.matmul(wide[i][:, 0], x[:, i - 1, k], w_out_t[:, k], start=(k == 0 and x is hTh), stop=(k == FC - 1 and x is hTl))
                            last.then_inc(out_full, 1)

                def first():
                    turn(0, 0)
                    into_hidden(0, 0, first=True)
                    turn(0, 2)

                over_pairs(pe, first, pair)


def decoder_layer(nc, io, out):
    def scratch(name, shape):
        return nc.dram_tensor(name, shape, F32, kind="Internal").ap()

    tiles = BATCH * TT
    x1_dram, x2_dram = scratch("x1_scratch", [tiles, P, DM]), scratch("x2_scratch", [tiles, P, DM])
    wq_dram, wd_dram = scratch("wq_scratch", [2, P, DC, HEADS * HD]), scratch("wd_scratch", [P, CC, 2 * HEADS * HD])
    wkv_dram = scratch("wkv_scratch", [2, P, CC, 2 * HEADS * HD])
    self_attention(nc, io, x1_dram)
    cross_attention(nc, io, x1_dram, x2_dram, wq_dram, wd_dram, wkv_dram)
    sparse_ffn(nc, io, x2_dram, out)


def rotary_tables(np):
    f32 = np.float32
    inv_freq = (f32(1.0) / f32(10000.0) ** (np.arange(0, HD, 2, dtype=f32) / f32(HD))).astype(f32)
    angle = np.arange(SEQ, dtype=f32)[:, None] * inv_freq[None, :]
    angle = np.concatenate([angle, angle], axis=-1).astype(np.float64)
    sign = np.where(np.arange(HD) < HD // 2, -1.0, 1.0)
    return [by_sixteenths(np, t.astype(f32), 0) for t in (np.cos(angle), np.sin(angle) * sign)]


def by_sixteenths(np, a, axis):
    shape = a.shape
    a = a.reshape(shape[:axis] + (SEQ // 16, 4, 4) + shape[axis + 1:])
    a = np.moveaxis(a, axis, axis + 2)
    return np.ascontiguousarray(a.reshape(shape))


def kernel(**inputs):
    import numpy as np
    import concourse.bacc as bacc
    from concourse.bass_utils import run_bass_kernel_spmd

    given = {k: np.asarray(v) for k, v in inputs.items()}
    attn, cross, ffn = ({k[len(p):]: v for k, v in given.items() if k.startswith(p)} for p in ("L0_attn_", "L0_xattn_", "L0_ffn_"))
    x, ctx = given["x"], given["ctx_1024"]
    HT = HEADS * HD
    cos, sin = rotary_tables(np)
    wkv = np.concatenate([cross["Wk"], cross["Wv"]], axis=1).reshape(CDM, HEADS, 2, HD)
    bkv = np.concatenate([cross["bk"], cross["bv"]]).reshape(HEADS, 2, HD)
    is_dca = np.arange(CTX) >= MAIN
    arrays = {
        "x": x,
        "xT": by_sixteenths(np, x.transpose(0, 2, 1), 2),
        "w1T": np.concatenate([attn["Wq"], attn["Wk"], attn["Wv"]], axis=0).T,
        "b1": np.concatenate([attn["bq"], attn["bk"], attn["bv"]]),
        "woT": attn["Wo"].T,
        "a_bo": attn["bo"],
        "randT": attn["rand_matrix"].T,
        "cos": cos,
        "sin": sin,
        "ident": np.eye(P, dtype=np.float32),
        "yT": ctx.transpose(0, 2, 1),
        "c_wkv": np.concatenate([wkv[:, :, 0].reshape(CDM, HT), wkv[:, :, 1].reshape(CDM, HT)], axis=1),
        "c_bkv": np.concatenate([bkv[:, 0].reshape(HT), bkv[:, 1].reshape(HT)]),
        "c_wq": cross["Wq"],
        "c_bq": cross["bq"],
        "c_wd": cross["Wkv_dca"],
        "c_bd": cross["bkv_dca"],
        "c_wo": cross["Wo"],
        "c_bo": cross["bo"],
        "nw": np.stack([cross["qn_w"], cross["kn_w"], cross["kn_dca_w"]]),
        "nb": np.stack([cross["qn_b"], cross["kn_b"], cross["kn_dca_b"]]),
        "key_rows": np.stack([~is_dca, is_dca]).astype(np.float32),
        "dca_row": is_dca[-P:].astype(np.float32)[:, None],
        "w_synT": ffn["W_syn"].T,
        "w_outT": ffn["W_out"].T,
        "b_syn": ffn["b_syn"],
        "b_out": ffn["b_out"],
        "gamma": ffn["gamma"],
        "beta": ffn["beta"],
        "places": np.append(np.arange(8), -1).astype(np.float32),
        "bits": np.uint32(1) << np.arange(KEY_BITS - 1, -1, -1, dtype=np.uint32),
    }
    nc = bacc.Bacc("TRN2", target_bir_lowering=False, num_devices=1)
    arrays = {"in_" + k: np.ascontiguousarray(a) for k, a in arrays.items()}
    io = {k[3:]: nc.dram_tensor(k, a.shape, mybir.dt.from_np(a.dtype), kind="ExternalInput").ap() for k, a in arrays.items()}
    out = nc.dram_tensor("out", [BATCH, SEQ, DM], F32, kind="ExternalOutput").ap()
    decoder_layer(nc, io, out)
    result = run_bass_kernel_spmd(nc, [arrays], core_ids=[0])
    return result.results[0]["out"]
```
